# Optimizing a Trainium2 kernel written in Bass

```python
import numpy as np
import jax
import jax.numpy as jnp

def _softmax(x, axis=-1):
    return jax.nn.softmax(x, axis=axis)

def _gelu(x):
    return jax.nn.gelu(x, approximate=True)

def _silu(x):
    return jax.nn.silu(x)

def _sigmoid(x):
    return jax.nn.sigmoid(x)

def _layernorm(x, axis=-1, eps=1e-05):
    m = jnp.mean(x, axis=axis, keepdims=True)
    v = jnp.var(x, axis=axis, keepdims=True)
    return (x - m) / jnp.sqrt(v + eps)

def _scatter_add(tgt, idx, src, axis=0):
    return tgt.at[idx].add(src)

def _segment_sum(src, seg, n):
    return jax.ops.segment_sum(src, seg, n)
kernel_name = 'mk_pixart_resid_d2_seqx_r8_5f396b'

def setup_inputs(seed: int=0):
    np.random.seed(seed)
    _w = jnp.asarray

    def _rec_inputs():
        import jax
        import jax.numpy as jnp
        _rk = jax.random.key(seed)
        x = -0.0005146 + 1 * jax.random.normal(jax.random.fold_in(_rk, 1), (4, 512, 128), jnp.float32)
        _lenS = 512 - jax.random.randint(jax.random.fold_in(_rk, 7), (4,), 0, max(1, 512 // 4) + 1, jnp.int32)
        _lenS2 = 77 - jax.random.randint(jax.random.fold_in(_rk, 8), (4,), 0, max(1, 77 // 4) + 1, jnp.int32)
        _ctx_1024P = jax.random.normal(jax.random.fold_in(_rk, 11), (4, 16, 128), jnp.float32)
        _ctx_1024c = jax.random.dirichlet(jax.random.fold_in(_rk, 511), 0.3 * jnp.ones((16,), jnp.float32), (4, 77))
        _ctx_1024t = jnp.einsum('bsk,bkd->bsd', _ctx_1024c, _ctx_1024P)
        _ctx_1024t = _ctx_1024t * jax.lax.rsqrt(jnp.mean(jnp.square(_ctx_1024t)) + 1e-12) * 0.953939
        ctx_1024 = -0.000125008 + 0.999885 * (_ctx_1024t + 0.3 * jax.random.normal(jax.random.fold_in(_rk, 611), (4, 77, 128), jnp.float32))
        cond_1024 = -0.00920427 + 1.00102 * jax.random.normal(jax.random.fold_in(_rk, 12), (4, 128), jnp.float32)
        _validS = jnp.arange(512)[None, :] < _lenS[:, None]
        _validS2 = jnp.arange(77)[None, :] < _lenS2[:, None]
        _causal = jnp.tril(jnp.ones((512, 512), dtype=bool))
        mask_BxS_bf0 = jnp.logical_not(jnp.ones((4, 512), dtype=bool))
        mask_BxS2_bf0 = jnp.logical_not(jnp.ones((4, 77), dtype=bool))
        return (x, ctx_1024, cond_1024, mask_BxS_bf0, mask_BxS2_bf0)
    x, ctx_1024, cond_1024, mask_BxS_bf0, mask_BxS2_bf0 = _rec_inputs()

    def _L0_xcond_setup():
        import jax, jax.numpy as jnp
        import numpy as np
        DIM = 128
        DIM_HEAD = 64
        HEADS = 16
        INNER = DIM_HEAD * HEADS
        B, N1, N2 = (8, 512, 32)
        EPS = 1e-05

        def layer_norm(x, w, b):
            mu = jnp.mean(x, axis=-1, keepdims=True)
            var = jnp.var(x, axis=-1, keepdims=True)
            return (x - mu) * jax.lax.rsqrt(var + EPS) * w + b
        key = jax.random.key(seed)
        ks = jax.random.split(key, 10)
        return {'x': jax.random.normal(ks[0], (B, N1, DIM), jnp.float32), 'latents': jax.random.normal(ks[1], (B, N2, DIM), jnp.float32), 'shift': jax.random.normal(ks[2], (B, DIM), jnp.float32), 'scale': jax.random.normal(ks[3], (B, DIM), jnp.float32), 'ln1_w': jnp.ones((DIM,), jnp.float32), 'ln1_b': jnp.zeros((DIM,), jnp.float32), 'ln2_w': jnp.ones((DIM,), jnp.float32), 'ln2_b': jnp.zeros((DIM,), jnp.float32), 'Wq': jax.random.normal(ks[4], (INNER, DIM), jnp.float32) * 0.02, 'Wkv': jax.random.normal(ks[5], (2 * INNER, DIM), jnp.float32) * 0.02, 'Wo': jax.random.normal(ks[6], (DIM, INNER), jnp.float32) * 0.02}
    _L0_xcond_all = _L0_xcond_setup()
    _L0_xcond_in = {k: v for k, v in _L0_xcond_all.items() if k in ('ln1_w', 'ln1_b', 'ln2_w', 'ln2_b', 'Wq', 'Wkv', 'Wo')}
    del _L0_xcond_all

    def _L0_ffn_setup():
        import jax, jax.numpy as jnp
        import numpy as np
        EPS_NORM = 1e-08
        EPS_Q = 1e-05

        def rmsnorm(x, w):
            v = jnp.mean(jnp.square(x.astype(jnp.float32)), axis=-1, keepdims=True)
            x_hat = x * jax.lax.rsqrt(v + EPS_NORM)
            return (x_hat * w).astype(x.dtype)

        def activation_quant(x):
            scale = 127.0 / jnp.clip(jnp.max(jnp.abs(x), axis=-1, keepdims=True), EPS_Q, None)
            return jnp.clip(jnp.round(x * scale), -128, 127) / scale

        def weight_quant(w):
            scale = 1.0 / jnp.clip(jnp.mean(jnp.abs(w)), EPS_Q, None)
            return jnp.clip(jnp.round(w * scale), -1, 1) / scale

        def bitlinear(x, norm_w, w):
            x_norm = rmsnorm(x, norm_w)
            x_q = x_norm + jax.lax.stop_gradient(activation_quant(x_norm) - x_norm)
            w_q = w + jax.lax.stop_gradient(weight_quant(w) - w)
            return jnp.einsum('bsd,hd->bsh', x_q, w_q)
        key = jax.random.key(seed)
        k1, k2, k3 = jax.random.split(key, 3)
        dim, hidden = (128, 512)
        return {'x': jax.random.normal(k1, (4, 256, dim), dtype=jnp.float32), 'norm1_w': jnp.ones((dim,), jnp.float32), 'w1': jax.random.normal(k2, (hidden, dim), jnp.float32) * 0.02, 'act_scale': jnp.ones((1,), jnp.float32), 'act_bias': jnp.zeros((1,), jnp.float32), 'norm2_w': jnp.ones((hidden,), jnp.float32), 'w2': jax.random.normal(k3, (dim, hidden), jnp.float32) * 0.02}
    _L0_ffn_all = _L0_ffn_setup()
    _L0_ffn_in = {k: v for k, v in _L0_ffn_all.items() if k in ('norm1_w', 'w1', 'act_scale', 'act_bias', 'norm2_w', 'w2')}
    del _L0_ffn_all

    def _L1_xcond_setup():
        import jax, jax.numpy as jnp
        import numpy as np
        NL, D, H, DFF = (6, 128, 16, 512)
        HD = D // H

        def _rope(x):
            L = x.shape[1]
            half = HD // 2
            inv = 1.0 / 10000.0 ** (jnp.arange(half, dtype=jnp.float32) / half)
            ang = jnp.arange(L, dtype=jnp.float32)[:, None] * inv
            cos = jnp.cos(ang)[None, :, None, :]
            sin = jnp.sin(ang)[None, :, None, :]
            x1, x2 = (x[..., :half], x[..., half:])
            return jnp.concatenate([x1 * cos - x2 * sin, x1 * sin + x2 * cos], axis=-1)

        def _ln(x, eps=1e-05):
            m = jnp.mean(x, axis=-1, keepdims=True)
            v = jnp.var(x, axis=-1, keepdims=True)
            return (x - m) * jax.lax.rsqrt(v + eps)

        def _adaln(x, emb, w, b):
            gb = emb[:, 0, :] @ w.T + b
            g, be = jnp.split(gb, 2, axis=-1)
            return _ln(x) * (1.0 + g[:, None, :]) + be[:, None, :]

        def _attn(q, k, v, mask):
            scores = jnp.einsum('bqhd,bkhd->bhqk', q, k) / np.float32(np.sqrt(HD))
            scores = jnp.where(mask[:, None, None, :], jnp.float32(-jnp.inf), scores)
            w = jax.nn.softmax(scores, axis=-1)
            return jnp.einsum('bhqk,bkhd->bqhd', w, v)
        key = jax.random.key(seed)
        ks = jax.random.split(key, 20)
        B, L, LC = (4, 128, 64)
        s = 0.02
        inp = {'x': jax.random.normal(ks[0], (B, L, D), jnp.float32), 'noise_emb': jax.random.normal(ks[1], (B, 1, D), jnp.float32), 'context': jax.random.normal(ks[2], (B, LC, D), jnp.float32), 'src_mask': jnp.zeros((B, L), bool), 'ctx_mask': jnp.zeros((B, LC), bool), 'n1_w': jax.random.normal(ks[3], (NL, 2 * D, D), jnp.float32) * s, 'n1_b': jnp.zeros((NL, 2 * D), jnp.float32), 'n2_w': jax.random.normal(ks[4], (NL, 2 * D, D), jnp.float32) * s, 'n2_b': jnp.zeros((NL, 2 * D), jnp.float32), 'n3_w': jax.random.normal(ks[5], (NL, 2 * D, D), jnp.float32) * s, 'n3_b': jnp.zeros((NL, 2 * D), jnp.float32), 'qkv_w': jax.random.normal(ks[6], (NL, 3 * D, D), jnp.float32) * s, 'so_w': jax.random.normal(ks[7], (NL, D, D), jnp.float32) * s, 'cq_w': jax.random.normal(ks[8], (NL, D, D), jnp.float32) * s, 'ck_w': jax.random.normal(ks[9], (NL, D, D), jnp.float32) * s, 'cv_w': jax.random.normal(ks[10], (NL, D, D), jnp.float32) * s, 'co_w': jax.random.normal(ks[11], (NL, D, D), jnp.float32) * s, 'f1_w': jax.random.normal(ks[12], (NL, DFF, D), jnp.float32) * s, 'f1_b': jnp.zeros((NL, DFF), jnp.float32), 'f2_w': jax.random.normal(ks[13], (NL, D, DFF), jnp.float32) * s, 'f2_b': jnp.zeros((NL, D), jnp.float32)}
        return inp
    _L1_xcond_all = _L1_xcond_setup()
    _L1_xcond_in = {k: v for k, v in _L1_xcond_all.items() if k in ('n1_w', 'n1_b', 'n2_w', 'n2_b', 'n3_w', 'n3_b', 'qkv_w', 'so_w', 'cq_w', 'ck_w', 'cv_w', 'co_w', 'f1_w', 'f1_b', 'f2_w', 'f2_b')}
    del _L1_xcond_all

    def _L1_ffn_setup():
        import jax, jax.numpy as jnp
        import numpy as np
        B, S, H, I, E = (2, 512, 128, 64, 8)
        key = jax.random.key(seed)
        ks = jax.random.split(key, 5)
        scale_h = 1.0 / np.sqrt(H)
        scale_i = 1.0 / np.sqrt(I)
        return {'hidden_states': jax.random.normal(ks[0], (B, S, H), dtype=jnp.float32), 'gate_w': jax.random.normal(ks[1], (E, H), dtype=jnp.float32) * scale_h, 'w_gate': jax.random.normal(ks[2], (E, I, H), dtype=jnp.float32) * scale_h, 'w_up': jax.random.normal(ks[3], (E, I, H), dtype=jnp.float32) * scale_h, 'w_down': jax.random.normal(ks[4], (E, H, I), dtype=jnp.float32) * scale_i}
    _L1_ffn_all = _L1_ffn_setup()
    _L1_ffn_in = {k: v for k, v in _L1_ffn_all.items() if k in ('gate_w', 'w_gate', 'w_up', 'w_down')}
    del _L1_ffn_all
    return {'x': x, 'ctx_1024': ctx_1024, 'cond_1024': cond_1024, 'mask_BxS_bf0': mask_BxS_bf0, 'mask_BxS2_bf0': mask_BxS2_bf0, 'L0_xcond_ln1_w': _L0_xcond_in['ln1_w'], 'L0_xcond_ln1_b': _L0_xcond_in['ln1_b'], 'L0_xcond_ln2_w': _L0_xcond_in['ln2_w'], 'L0_xcond_ln2_b': _L0_xcond_in['ln2_b'], 'L0_xcond_Wq': _L0_xcond_in['Wq'], 'L0_xcond_Wkv': _L0_xcond_in['Wkv'], 'L0_xcond_Wo': _L0_xcond_in['Wo'], 'L0_ffn_norm1_w': _L0_ffn_in['norm1_w'], 'L0_ffn_w1': _L0_ffn_in['w1'], 'L0_ffn_act_scale': _L0_ffn_in['act_scale'], 'L0_ffn_act_bias': _L0_ffn_in['act_bias'], 'L0_ffn_norm2_w': _L0_ffn_in['norm2_w'], 'L0_ffn_w2': _L0_ffn_in['w2'], 'L1_xcond_n1_w': _L1_xcond_in['n1_w'], 'L1_xcond_n1_b': _L1_xcond_in['n1_b'], 'L1_xcond_n2_w': _L1_xcond_in['n2_w'], 'L1_xcond_n2_b': _L1_xcond_in['n2_b'], 'L1_xcond_n3_w': _L1_xcond_in['n3_w'], 'L1_xcond_n3_b': _L1_xcond_in['n3_b'], 'L1_xcond_qkv_w': _L1_xcond_in['qkv_w'], 'L1_xcond_so_w': _L1_xcond_in['so_w'], 'L1_xcond_cq_w': _L1_xcond_in['cq_w'], 'L1_xcond_ck_w': _L1_xcond_in['ck_w'], 'L1_xcond_cv_w': _L1_xcond_in['cv_w'], 'L1_xcond_co_w': _L1_xcond_in['co_w'], 'L1_xcond_f1_w': _L1_xcond_in['f1_w'], 'L1_xcond_f1_b': _L1_xcond_in['f1_b'], 'L1_xcond_f2_w': _L1_xcond_in['f2_w'], 'L1_xcond_f2_b': _L1_xcond_in['f2_b'], 'L1_ffn_gate_w': _L1_ffn_in['gate_w'], 'L1_ffn_w_gate': _L1_ffn_in['w_gate'], 'L1_ffn_w_up': _L1_ffn_in['w_up'], 'L1_ffn_w_down': _L1_ffn_in['w_down']}

def reference(x, ctx_1024, cond_1024, mask_BxS_bf0, mask_BxS2_bf0, L0_xcond_ln1_w, L0_xcond_ln1_b, L0_xcond_ln2_w, L0_xcond_ln2_b, L0_xcond_Wq, L0_xcond_Wkv, L0_xcond_Wo, L0_ffn_norm1_w, L0_ffn_w1, L0_ffn_act_scale, L0_ffn_act_bias, L0_ffn_norm2_w, L0_ffn_w2, L1_xcond_n1_w, L1_xcond_n1_b, L1_xcond_n2_w, L1_xcond_n2_b, L1_xcond_n3_w, L1_xcond_n3_b, L1_xcond_qkv_w, L1_xcond_so_w, L1_xcond_cq_w, L1_xcond_ck_w, L1_xcond_cv_w, L1_xcond_co_w, L1_xcond_f1_w, L1_xcond_f1_b, L1_xcond_f2_w, L1_xcond_f2_b, L1_ffn_gate_w, L1_ffn_w_gate, L1_ffn_w_up, L1_ffn_w_down):
    import jax
    import jax.numpy as jnp

    def _L0_xcond_ref(x, latents, shift, scale, ln1_w, ln1_b, ln2_w, ln2_b, Wq, Wkv, Wo):
        import jax, jax.numpy as jnp
        import numpy as np
        DIM = 128
        DIM_HEAD = 64
        HEADS = 16
        INNER = DIM_HEAD * HEADS
        B, N1, N2 = (8, 512, 32)
        EPS = 1e-05

        def layer_norm(x, w, b):
            mu = jnp.mean(x, axis=-1, keepdims=True)
            var = jnp.var(x, axis=-1, keepdims=True)
            return (x - mu) * jax.lax.rsqrt(var + EPS) * w + b
        x = layer_norm(x, ln1_w, ln1_b)
        lat = layer_norm(latents, ln2_w, ln2_b)
        lat = lat * (1.0 + scale[:, None, :]) + shift[:, None, :]
        b, n2, _ = lat.shape
        q = jnp.einsum('bld,ed->ble', lat, Wq)
        kv_in = jnp.concatenate((x, lat), axis=-2)
        kv = jnp.einsum('bld,ed->ble', kv_in, Wkv)
        k, v = jnp.split(kv, 2, axis=-1)

        def to_heads(t):
            bsz, L, _ = t.shape
            return t.reshape(bsz, L, HEADS, DIM_HEAD).transpose(0, 2, 1, 3)
        q, k, v = (to_heads(q), to_heads(k), to_heads(v))
        attn_scale = 1.0 / np.sqrt(np.sqrt(DIM_HEAD)).astype(np.float32)
        logits = jnp.einsum('bhqd,bhkd->bhqk', q * attn_scale, k * attn_scale)
        w = jax.nn.softmax(logits.astype(jnp.float32), axis=-1).astype(logits.dtype)
        out = jnp.einsum('bhqk,bhkd->bhqd', w, v)
        out = out.transpose(0, 2, 1, 3).reshape(b, n2, INNER)
        return jnp.einsum('ble,de->bld', out, Wo)

    def _L0_ffn_ref(x, norm1_w, w1, act_scale, act_bias, norm2_w, w2):
        import jax, jax.numpy as jnp
        import numpy as np
        EPS_NORM = 1e-08
        EPS_Q = 1e-05

        def rmsnorm(x, w):
            v = jnp.mean(jnp.square(x.astype(jnp.float32)), axis=-1, keepdims=True)
            x_hat = x * jax.lax.rsqrt(v + EPS_NORM)
            return (x_hat * w).astype(x.dtype)

        def activation_quant(x):
            scale = 127.0 / jnp.clip(jnp.max(jnp.abs(x), axis=-1, keepdims=True), EPS_Q, None)
            return jnp.clip(jnp.round(x * scale), -128, 127) / scale

        def weight_quant(w):
            scale = 1.0 / jnp.clip(jnp.mean(jnp.abs(w)), EPS_Q, None)
            return jnp.clip(jnp.round(w * scale), -1, 1) / scale

        def bitlinear(x, norm_w, w):
            x_norm = rmsnorm(x, norm_w)
            x_q = x_norm + jax.lax.stop_gradient(activation_quant(x_norm) - x_norm)
            w_q = w + jax.lax.stop_gradient(weight_quant(w) - w)
            return jnp.einsum('bsd,hd->bsh', x_q, w_q)
        h = bitlinear(x, norm1_w, w1)
        h = act_scale * jnp.square(jax.nn.relu(h)) + act_bias
        y = bitlinear(h, norm2_w, w2)
        return y

    def _L1_xcond_ref(x, noise_emb, context, src_mask, ctx_mask, n1_w, n1_b, n2_w, n2_b, n3_w, n3_b, qkv_w, so_w, cq_w, ck_w, cv_w, co_w, f1_w, f1_b, f2_w, f2_b):
        import jax, jax.numpy as jnp
        import numpy as np
        NL, D, H, DFF = (6, 128, 16, 512)
        HD = D // H

        def _rope(x):
            L = x.shape[1]
            half = HD // 2
            inv = 1.0 / 10000.0 ** (jnp.arange(half, dtype=jnp.float32) / half)
            ang = jnp.arange(L, dtype=jnp.float32)[:, None] * inv
            cos = jnp.cos(ang)[None, :, None, :]
            sin = jnp.sin(ang)[None, :, None, :]
            x1, x2 = (x[..., :half], x[..., half:])
            return jnp.concatenate([x1 * cos - x2 * sin, x1 * sin + x2 * cos], axis=-1)

        def _ln(x, eps=1e-05):
            m = jnp.mean(x, axis=-1, keepdims=True)
            v = jnp.var(x, axis=-1, keepdims=True)
            return (x - m) * jax.lax.rsqrt(v + eps)

        def _adaln(x, emb, w, b):
            gb = emb[:, 0, :] @ w.T + b
            g, be = jnp.split(gb, 2, axis=-1)
            return _ln(x) * (1.0 + g[:, None, :]) + be[:, None, :]

        def _attn(q, k, v, mask):
            scores = jnp.einsum('bqhd,bkhd->bhqk', q, k) / np.float32(np.sqrt(HD))
            scores = jnp.where(mask[:, None, None, :], jnp.float32(-jnp.inf), scores)
            w = jax.nn.softmax(scores, axis=-1)
            return jnp.einsum('bhqk,bkhd->bqhd', w, v)
        B, L, _ = x.shape
        LC = context.shape[1]
        for i in range(NL):
            xn = _adaln(x, noise_emb, n1_w[i], n1_b[i])
            qkv = xn @ qkv_w[i].T
            q, k, v = jnp.split(qkv, 3, axis=-1)
            q = _rope(q.reshape(B, L, H, HD))
            k = _rope(k.reshape(B, L, H, HD))
            v = v.reshape(B, L, H, HD)
            a = _attn(q, k, v, src_mask).reshape(B, L, D) @ so_w[i].T
            x = x + a
            xn = _adaln(x, noise_emb, n2_w[i], n2_b[i])
            q = _rope((xn @ cq_w[i].T).reshape(B, L, H, HD))
            k = _rope((context @ ck_w[i].T).reshape(B, LC, H, HD))
            v = (context @ cv_w[i].T).reshape(B, LC, H, HD)
            a = _attn(q, k, v, ctx_mask).reshape(B, L, D) @ co_w[i].T
            x = x + a
            xn = _adaln(x, noise_emb, n3_w[i], n3_b[i])
            h = jax.nn.gelu(xn @ f1_w[i].T + f1_b[i], approximate=False)
            x = x + (h @ f2_w[i].T + f2_b[i])
        return x

    def _L1_ffn_ref(hidden_states, gate_w, w_gate, w_up, w_down):
        import jax, jax.numpy as jnp
        import numpy as np
        B, S, H, I, E = (2, 512, 128, 64, 8)
        b, s, h = hidden_states.shape
        x = hidden_states.reshape(-1, h)
        logits = x @ gate_w.T
        top_v = jnp.max(logits, axis=-1)
        sel = jnp.argmax(logits, axis=-1)
        rw = jax.nn.sigmoid(top_v)
        out = jnp.zeros_like(x)
        n_exp = gate_w.shape[0]
        for e in range(n_exp):
            mask = (sel == e).astype(x.dtype)
            xs = x * (rw * mask)[:, None]
            g = xs @ w_gate[e].T
            u = xs @ w_up[e].T
            out = out + u * jax.nn.silu(g) @ w_down[e].T
        return out.reshape(b, s, h)
    x = x + _L0_xcond_ref(ctx_1024, _layernorm(x, axis=-1), cond_1024, cond_1024, L0_xcond_ln1_w, L0_xcond_ln1_b, L0_xcond_ln2_w, L0_xcond_ln2_b, L0_xcond_Wq, L0_xcond_Wkv, L0_xcond_Wo)
    x = x + _L0_ffn_ref(_layernorm(x, axis=-1), L0_ffn_norm1_w, L0_ffn_w1, L0_ffn_act_scale, L0_ffn_act_bias, L0_ffn_norm2_w, L0_ffn_w2)
    x = x + _L1_xcond_ref(_layernorm(x, axis=-1), cond_1024[:, None, :], ctx_1024, mask_BxS_bf0, mask_BxS2_bf0, L1_xcond_n1_w, L1_xcond_n1_b, L1_xcond_n2_w, L1_xcond_n2_b, L1_xcond_n3_w, L1_xcond_n3_b, L1_xcond_qkv_w, L1_xcond_so_w, L1_xcond_cq_w, L1_xcond_ck_w, L1_xcond_cv_w, L1_xcond_co_w, L1_xcond_f1_w, L1_xcond_f1_b, L1_xcond_f2_w, L1_xcond_f2_b)
    x = x + _L1_ffn_ref(_layernorm(x, axis=-1), L1_ffn_gate_w, L1_ffn_w_gate, L1_ffn_w_up, L1_ffn_w_down)
    return x

_drawn_inputs = setup_inputs


def setup_inputs(seed=0):
    import zlib

    import numpy as np

    out = dict(_drawn_inputs(seed))
    spreads = {'L0_xcond_ln1_w': (1.0, 0.6),
     'L0_xcond_ln1_b': (0.0, 2.0),
     'L0_xcond_ln2_w': (1.0, 0.6),
     'L0_xcond_ln2_b': (0.0, 0.1),
     'L0_ffn_norm1_w': (1.0, 0.2),
     'L0_ffn_norm2_w': (1.0, 0.2),
     'L1_xcond_n1_b': (0.0, 0.488),
     'L1_xcond_n2_b': (0.0, 0.8),
     'L1_xcond_n3_b': (0.0, 0.423),
     'L1_xcond_f1_b': (0.0, 0.1),
     'L1_xcond_f2_b': (0.0, 0.1)}
    factors = {'L0_xcond_Wq': 5.353, 'L1_xcond_n2_w': 8.0, 'L1_xcond_cq_w': 8.0, 'L1_xcond_ck_w': 8.0}
    for name, (base, spread) in spreads.items():
        noise = np.random.default_rng([zlib.crc32(name.encode()), seed]).standard_normal(out[name].shape)
        drawn = base * np.exp(spread * noise) if base else spread * noise
        out[name] = jnp.asarray(drawn.astype(out[name].dtype))
    for name, factor in factors.items():
        out[name] = (out[name] * factor).astype(out[name].dtype)
    return out
```

```python
import numpy as np
import concourse.bass as bass
from concourse import mybir
from concourse.alu_op_type import AluOpType as ALU
from contextlib import ExitStack

fp32 = mybir.dt.float32
bf16 = mybir.dt.bfloat16
ACT = mybir.ActivationFunctionType
AX = mybir.AxisListType

B, S, D = 4, 512, 128
P = 128
QT = S // P
C = 77
H0, HD0 = 16, 64
INNER = H0 * HD0
NP0 = INNER // P
KV = S + C
KT0 = (KV + P - 1) // P
NL, H1, HD1 = 6, 16, 8
DFF = 512
FC = DFF // P
E, I = 8, 64
GROUP = 4
NG = H1 // GROUP
SLOT_Q = (0, 0, 0, 1, 1, 2)
SLOT_K = (0, 1, 2, 0, 1, 0)
MROW = len(SLOT_Q) * HD1
STACK = 64
NMAX, NALL = MROW + 1, MROW + 4
MAGIC = 1.5 * 2.0 ** 23

W_QKV, W_SO, W_CQ, W_CKV, W_CO, W_F1, W_F2, W_COLS = 0, 384, 512, 640, 896, 1024, 1536, 2048


class Program:

    ENGINES = ("tensor", "vector", "scalar", "gpsimd")

    def __init__(self):
        self.n = {e: 0 for e in self.ENGINES}
        self.segment = 0
        self.stack = {e: [[]] for e in self.ENGINES}

    def add(self, engine, fn, after=(), count=True):
        self.stack[engine][-1].append(("do", fn, [t for t in after if t is not None], count, self.segment))
        if not count:
            return None
        self.n[engine] += 1
        return (engine, self.n[engine], self.segment)

    def pe(self, fn, after=(), count=True):
        return self.add("tensor", fn, after, count)

    def dve(self, fn, after=()):
        return self.add("vector", fn, after)

    def act(self, fn, after=()):
        return self.add("scalar", fn, after)

    def pool(self, fn, after=()):
        return self.add("gpsimd", fn, after)

    def meet(self, phase=False):
        for e in self.ENGINES:
            self.stack[e][-1].append(("meet", dict(self.n), phase))
        self.n = {e: 0 for e in self.ENGINES}
        self.segment += 1

    def begin(self, name, times):
        self.meet()
        for e in self.ENGINES:
            body = []
            self.stack[e][-1].append(("loop", name, times, body))
            self.stack[e].append(body)

    def end(self):
        self.meet()
        for e in self.ENGINES:
            self.stack[e].pop()

    def emit(self, engine, handle, sems, queue=None, env=None):
        done, arrived, go, phase_sem = sems
        env = {} if env is None else env
        seen = {}
        for item in self.stack[engine][0] if queue is None else queue:
            if item[0] == "loop":
                _, name, times, body = item
                with handle.Fori(0, times) as i:
                    self.emit(engine, handle, sems, body, {**env, name: i})
            elif item[0] == "meet":
                _, counts, phase = item
                for e in self.ENGINES:
                    if counts[e] > seen.get(e, 0):
                        handle.wait_ge(done[e], counts[e])
                if engine == "gpsimd":
                    handle.wait_ge(arrived, len(self.ENGINES) - 1)
                    handle.sem_clear(arrived)
                    for e in self.ENGINES:
                        handle.sem_clear(done[e])
                    if phase:
                        handle.sem_inc(phase_sem, 1)
                    for e in self.ENGINES:
                        if e != engine:
                            handle.sem_inc(go[e], 1)
                else:
                    handle.sem_inc(arrived, 1)
                    handle.wait_ge(go[engine], 1)
                    handle.sem_clear(go[engine])
                seen = {}
            else:
                _, fn, after, count, segment = item
                need = {}
                for e, local, seg in after:
                    if seg == segment and local > seen.get(e, 0):
                        need[e] = max(need.get(e, 0), local)
                for e, local in need.items():
                    handle.wait_ge(done[e], local)
                    seen[e] = local
                ins = fn(handle, env)
                if count:
                    ins.then_inc(done[engine], 1)


def rope_tables():
    half = HD1 // 2
    inv = (1.0 / np.float32(10000.0) ** (np.arange(half, dtype=np.float32) / np.float32(half))).astype(np.float32)
    ang = np.arange(S, dtype=np.float32)[:, None] * inv
    cos, sin = np.cos(ang).astype(np.float32), np.sin(ang).astype(np.float32)
    table = np.concatenate([cos, cos, -sin, sin], axis=1)
    return np.ascontiguousarray(table.reshape(QT, P, 16).transpose(1, 0, 2)).reshape(P, QT * 16)


def build(nc, a, out):
    pr = Program()
    pe, dve, act, pool = pr.pe, pr.dve, pr.act, pr.pool
    ctx = ExitStack()
    with ctx:
        def sb(name, shape, dt=fp32):
            return ctx.enter_context(nc.sbuf_tensor(name, shape, dt))

        psum = ctx.enter_context(nc.psum_tensor("psum", [P, 8, 512], fp32))

        def bank(i, n=1):
            return psum[:, i:i + n, :] if n > 1 else psum[:, i, :]

        def bank16(i):
            return psum[:, i, :].bitcast(bf16)

        x_res = sb("x_res", [P, B * QT, D])
        x_st = sb("x_st", [P, B * QT, D])
        ctx_sb = sb("ctx_sb", [P, B, D])
        ctxT = sb("ctxT", [P, B, C])
        condT = sb("condT", [P, B])
        ident = sb("ident", [P, P])
        ident16 = sb("ident16", [P, P], bf16)
        rope = sb("rope", [P, QT, 16])
        ones_sq = sb("ones_sq", [P, P])
        neg_half = sb("neg_half", [P, QT])
        sel = sb("sel", [6, 2, P], bf16)
        mask_in = sb("mask_in", [P, B * QT], mybir.dt.int32)
        maskc_in = sb("maskc_in", [P, B], mybir.dt.int32)
        mask_row = sb("mask_row", [P, B * QT])
        maskc_row = sb("maskc_row", [P, B])
        vec = sb("vec", [P, 4])
        lat_g = sb("lat_g", [P, B])
        lat_b = sb("lat_b", [P, B])
        n1w_bc = sb("n1w_bc", [P, D])
        n2w_bc = sb("n2w_bc", [P, DFF])
        act_sb = sb("act_sb", [P, 2])
        gb = sb("gb", [P, NL * 6, B])
        nb = sb("nb", [P, NL * 6])
        f1b = sb("f1b", [P, NL * FC])
        f2b = sb("f2b", [1, NL * D])
        wq1 = sb("wq1", [P, DFF], bf16)
        wq2 = sb("wq2", [P, FC, D], bf16)
        wscale = sb("wscale", [P, 2])
        A0 = sb("A0", [P, 26624])
        A1 = sb("A1", [P, 12288])
        stats = sb("stats", [P, QT, 6])
        mv = sb("mv", [P, QT, 2])
        ve = sb("ve", [P, QT])
        rstd = sb("rstd", [P, QT])
        y = sb("y", [P, QT, D])
        z = sb("z", [P, QT, D])
        zc = sb("zc", [P, D])
        zq = sb("zq", [P, QT, D], bf16)
        xnT = sb("xnT", [P, 640])
        wsum = sb("wsum", [P, 2])
        small = sb("small", [P, 8, QT])

        def sem(name):
            return ctx.enter_context(nc.semaphore(name))

        done = {e: sem(f"done_{e}") for e in Program.ENGINES}
        go = {e: sem(f"go_{e}") for e in Program.ENGINES if e != "gpsimd"}
        arrived, phase = sem("arrived"), sem("phase")
        s_first, s_w0, s_wl, s_wm, s_out = sem("s_first"), sem("s_w0"), sem("s_wl"), sem("s_wm"), sem("s_out")

        loads = {"first": 0, "w0": 0, "wl": 0, "wm": 0}
        sems = {"first": s_first, "w0": s_w0, "wl": s_wl, "wm": s_wm}
        dma_list = []

        def load(group, dst, src, after=0):
            loads[group] += 16
            dma_list.append((sems[group], dst, src, after))

        def loaded(engine, group):
            pr.stack[engine][-1].append(("do", lambda e, v: e.wait_ge(sems[group], loads[group]), [], False, pr.segment))

        wqT = A0[:, 0:1024]
        wkT = A0[:, 1024:2048]
        wvT = A0[:, 2048:3072]
        woT = A0[:, 3072:4096].rearrange("p (u d) -> p u d", d=D)
        q_pair = A0[:, 4096:5120].rearrange("p (n t) -> p n t", n=2)
        k_pair = A0[:, 5120:6400].rearrange("p (n t) -> p n t", n=2)
        v0 = A0[:, 6400:6400 + KT0 * H0 * 65].rearrange("p (k h d) -> p k h d", k=KT0, h=H0)
        p0 = A0[:, 11600:11600 + 2 * KT0 * S].rearrange("p (n k t) -> p n k t", n=2, k=KT0)
        att0 = A0[:, 16720:16720 + QT * INNER].rearrange("p (q c) -> p q c", q=QT)
        att0T = A0[:, 20816:20816 + NP0 * S].rearrange("p (u t) -> p u t", u=NP0)
        kvT = xnT
        nm0 = sb("nm0", [P, 2, QT])
        nm0r = sb("nm0r", [P, 2, QT])
        m3 = sb("m3", [P, QT, 2, 3], bf16)
        m3T = sb("m3T", [6, 2, S], bf16)
        rd0 = sb("rd0", [P, QT])
        wl = A1[:, 0:NL * W_COLS].rearrange("p (l c) -> p l c", l=NL)
        nT = A0[:, 0:NL * 3 * 2 * D].rearrange("p (j o) -> p j o", o=D)
        w1T = A0[:, 4608:5120]
        w2T = A0[:, 5120:5632].rearrange("p (c d) -> p c d", d=D)
        hh = A0[:, 0:QT * DFF].rearrange("p (q f) -> p q f", q=QT)
        hr = A0[:, 2048:2048 + QT * DFF].rearrange("p (q f) -> p q f", q=QT)
        hq = A0[:, 4096:5120].bitcast(bf16).rearrange("p (q f) -> p q f", q=QT)
        hqT = A0[:, 5120:6144].bitcast(bf16).rearrange("p (c t) -> p c t", c=FC)
        zqT = A0[:, 6144:6400].bitcast(bf16)
        qk = A0[:, 0:1024].rearrange("p (w q c) -> p w q c", w=2, q=QT)
        rot = A0[:, 1024:2048].rearrange("p (w q c) -> p w q c", w=2, q=QT)
        tmp = A0[:, 2048:3072].rearrange("p (w q c) -> p w q c", w=2, q=QT)
        gq = A0[:, 3072:5120].bitcast(bf16).rearrange("p (q h r) -> p q h r", q=QT, h=H1)
        gk = A0[:, 5120:7168].bitcast(bf16).rearrange("p (q h r) -> p q h r", q=QT, h=H1)
        q_st = A0[:, 7168:9216].bitcast(bf16).rearrange("p (u t) -> p u t", u=8)
        k_st = A0[:, 9216:11264].bitcast(bf16).rearrange("p (u t) -> p u t", u=8)
        q_m = A0[:, 11264:12288].bitcast(bf16).rearrange("p (n u t) -> p n u t", n=2, u=2)
        pT = A0[:, 12288:16384].rearrange("p (n j t) -> p n j t", n=2, j=GROUP)
        v_self = A0[:, 16384:16384 + QT * H1 * 32].rearrange("p (k h d) -> p k h d", k=QT, h=H1)
        v_cross = A0[:, 18432:18432 + H1 * 32].rearrange("p (k h d) -> p k h d", k=1, h=H1)
        o_sb = A0[:, 18944:19968].rearrange("p (n t) -> p n t", n=2)
        att = A0[:, 19968:20480].rearrange("p (q c) -> p q c", q=QT)
        attT = A0[:, 20480:20992]
        ctx_b = A0[:, 20992:21120]
        f1s = A0[:, 21120:21632]
        hT = A0[:, 21632:23680].rearrange("p (c t) -> p c t", c=FC)
        nm = A0[:, 23680:23744].rearrange("p (g q j) -> p g q j", g=NG, q=QT)
        nmr = A0[:, 23744:23808].rearrange("p (g q j) -> p g q j", g=NG, q=QT)
        rd = A0[:, 23808:23872].rearrange("p (g q j) -> p g q j", g=NG, q=QT)
        wgT = A1[:, 0:512]
        wuT = A1[:, 512:1024]
        wdT = A1[:, 1024:1536].rearrange("p (c d) -> p c d", d=D)
        gateT = A1[:, 1536:1544]
        rank = A1[:, 1544:1552]
        eg = A0[:, 0:QT * E * I].rearrange("p (q f) -> p q f", q=QT)
        eu = A0[:, 2048:4096].rearrange("p (q f) -> p q f", q=QT)
        es = A0[:, 4096:6144].rearrange("p (q f) -> p q f", q=QT)
        ehT = A0[:, 6144:8192].rearrange("p (c t) -> p c t", c=FC)
        lg = A0[:, 8192:8224].rearrange("p (q e) -> p q e", q=QT)
        oh = A0[:, 8224:8256].rearrange("p (q e) -> p q e", q=QT)
        top = A0[:, 8256:8272].rearrange("p (k q) -> p k q", k=4)

        x_dram = a["x"].rearrange("b (q p) d -> p (b q) d", p=P)
        load("first", x_res[:, :, :], x_dram)
        load("first", ctx_sb[0:C, :, :], a["ctx"].rearrange("b c d -> c b d"))
        load("first", ctxT[:, :, :], a["ctxT"])
        load("first", condT[:, :], a["condT"])
        load("first", ident[:, :], a["ident"])
        load("first", rope[:, :, :], a["rope"].rearrange("p (q r) -> p q r", q=QT))
        load("first", mask_in[:, :], a["mask"])
        load("first", maskc_in[0:C, :], a["maskc"])
        load("first", vec[:, :], a["vec"])
        load("first", n1w_bc[:, :], a["n1w"].rearrange("(o n) -> o n", o=1).to_broadcast([P, D]))
        load("first", n2w_bc[:, :], a["n2w"].rearrange("(o n) -> o n", o=1).to_broadcast([P, DFF]))
        load("first", act_sb[:, :], a["actsb"].rearrange("(o n) -> o n", o=1).to_broadcast([P, 2]))
        load("first", nb[:, :], a["nb"])
        load("first", f1b[:, :], a["f1b"])
        load("first", f2b[:, :], a["f2b"])
        load("first", nT.rearrange("p j o -> p (j o)"), a["nT"])
        load("first", w1T, a["w1T"])
        load("first", w2T.rearrange("p c d -> p (c d)"), a["w2T"])

        for e in Program.ENGINES:
            loaded(e, "first")
        ones_t = dve(lambda e, v: e.memset(ones_sq[:, :], 1.0))
        dve(lambda e, v: e.memset(neg_half[:, :], -0.5))
        id16 = dve(lambda e, v: e.tensor_copy(ident16[:, :], ident[:, :]))
        t = dve(lambda e, v: e.tensor_reduce(small[0:6, 0:2, 0:1], ident[0:6, 0:6].rearrange("p (n k) -> p n k", n=2), AX.X, ALU.add))
        for n in range(2):
            dve(lambda e, v, n=n: e.tensor_scalar(sel[:, n, :], ones_sq[0:6, :], small[0:6, n, 0:1], None, ALU.mult),
                [t, ones_t])
        for raw, row, k in ((mask_in, mask_row, P), (maskc_in, maskc_row, C)):
            t = dve(lambda e, v, raw=raw, row=row, k=k: e.tensor_copy(row[0:k, :], raw[0:k, :]))
            dve(lambda e, v, row=row, k=k: e.tensor_scalar(row[0:k, :], row[0:k, :], -3.0e38, 3.0e38, ALU.mult, ALU.mult), [t])
        t0 = dve(lambda e, v: e.tensor_scalar(lat_b[:, :], condT[:, :], 1.0, None, ALU.add))
        t1 = dve(lambda e, v: e.tensor_scalar(lat_g[:, :], lat_b[:, :], vec[:, 2:3], None, ALU.mult), [t0])
        t2 = dve(lambda e, v: e.tensor_scalar(lat_b[:, :], lat_b[:, :], vec[:, 3:4], None, ALU.mult), [t1])
        dve(lambda e, v: e.tensor_tensor(lat_b[:, :], lat_b[:, :], condT[:, :], ALU.add), [t2])
        t0 = dve(lambda e, v: e.tensor_reduce(wsum[:, 0:1], w1T, AX.X, ALU.add, apply_absolute_value=True))
        t1 = dve(lambda e, v: e.tensor_reduce(wsum[:, 1:2], w2T, AX.XY, ALU.add, apply_absolute_value=True))
        t = pe(lambda e, v: e.matmul(psum[:, 0, 0:2], ones_sq[:, :], wsum[:, :], start=True, stop=True), [t0, t1, ones_t])
        t = dve(lambda e, v: e.tensor_scalar(wscale[:, :], psum[:, 0, 0:2], 1.0 / (D * DFF), 1e-5, ALU.mult, ALU.max), [t])
        t = dve(lambda e, v: e.reciprocal(wsum[:, :], wscale[:, :]), [t])
        for w, k, dst in ((w1T, 0, wq1[:, :]), (w2T, 1, wq2[:, :, :])):
            u = dve(lambda e, v, w=w, k=k: e.tensor_scalar(w, w, wsum[:, k:k + 1], MAGIC, ALU.mult, ALU.add), [t])
            u = dve(lambda e, v, w=w: e.tensor_scalar(w, w, -MAGIC, 1.0, ALU.add, ALU.min), [u])
            dve(lambda e, v, w=w, dst=dst: e.tensor_scalar(dst, w, -1.0, None, ALU.max), [u])
        for j in range(NL * 6):
            t = pe(lambda e, v, j=j: e.matmul(psum[:, 1, j * B:(j + 1) * B], nT[:, j, :], condT[:, :], start=True, stop=True))
        t = dve(lambda e, v: e.tensor_tensor(gb[:, :, :], psum[:, 1, 0:NL * 6 * B].rearrange("p (j b) -> p j b", b=B),
                                             nb[:, :].unsqueeze(2).to_broadcast([P, NL * 6, B]), ALU.add), [t])
        gview = gb[:, :, :].rearrange("p (l h) b -> p l h b", h=2)
        prep_end = dve(lambda e, v: e.tensor_scalar(gview[:, :, 0, :], gview[:, :, 0, :], 1.0, None, ALU.add), [t])

        pr.meet(phase=True)
        load("w0", A0[:, 0:4096], a["w0"], 1)
        load("wl", wl.rearrange("p l c -> p (l c)"), a["wl"])

        def norm(src, dst, n, parts, eps, after=(), keep=None):
            for q in range(n):
                t = dve(lambda e, v, q=q: e.bn_stats(stats[0:parts, q, :], src(v)[:, q, :]), after)
            for q in range(n):
                t1 = dve(lambda e, v, q=q: e.bn_aggr(mv[0:parts, q, :], stats[0:parts, q, :]), [t])
            t2 = dve(lambda e, v: e.tensor_scalar(ve[0:parts, 0:n], mv[0:parts, 0:n, 1], eps, None, ALU.add), [t1])
            t3 = pool(lambda e, v: e.tensor_tensor(rstd[0:parts, 0:n], ve[0:parts, 0:n], neg_half[0:parts, 0:n], ALU.pow), [t2])
            for q in range(n):
                t4 = dve(lambda e, v, q=q: e.tensor_scalar(dst[0:parts, q, :], src(v)[:, q, :], mv[0:parts, q, 0:1],
                                                           rstd[0:parts, q:q + 1], ALU.subtract, ALU.mult), [t3])
            return t4

        def transposes(b, src, n, after):
            for q in range(n):
                t = pe(lambda e, v, q=q: e.transpose(psum[:, b, q * P:(q + 1) * P], src[:, q, :], ident[:, :]),
                       after, count=q == n - 1)
            return t

        loaded("tensor", "w0")
        pr.begin("b0", B)
        tv = dve(lambda e, v: e.memset(v0[:, :, :, HD0:HD0 + 1], 1.0))
        xb = lambda v: x_res[:, bass.ds(v["b0"] * QT, QT), :]
        t = norm(xb, y, QT, P, 1e-5)
        t = norm(lambda v: y[:, :, :], z, QT, P, 1e-5, [t])
        t = transposes(0, z, QT, [t])
        t_lat = dve(lambda e, v: e.tensor_scalar(kvT[:, 0:S], bank(0), lat_g[:, bass.ds(v["b0"], 1)],
                                                 lat_b[:, bass.ds(v["b0"], 1)], ALU.mult, ALU.add), [t])
        t = norm(lambda v: ctx_sb[0:C, bass.ds(v["b0"], 1), :], zc[:, :].unsqueeze(1), 1, C, 1e-5, [t])
        t = pe(lambda e, v: e.transpose(psum[:, 1, 0:C], zc[0:C, :], ident[0:C, 0:C]), [t])
        t_ctx = dve(lambda e, v: e.tensor_scalar(kvT[:, S:KV], psum[:, 1, 0:C], vec[:, 0:1], vec[:, 1:2],
                                                 ALU.mult, ALU.add), [t])
        t_v = [None] * 4
        i = 0
        for k in range(KT0):
            rows = min(P, KV - k * P)
            for half in range(2):
                t = pe(lambda e, v, k=k, half=half, i=i, rows=rows: e.matmul(
                    psum[0:rows, 2 + i % 4, :], kvT[:, k * P:k * P + rows], wvT[:, half * 512:(half + 1) * 512],
                    start=True, stop=True), [t_lat, t_ctx, t_v[i % 4]])
                t_v[i % 4] = act(lambda e, v, k=k, half=half, i=i, rows=rows: e.activation(
                    v0[0:rows, k, half * 8:(half + 1) * 8, 0:HD0],
                    psum[0:rows, 2 + i % 4, :].rearrange("p (h d) -> p h d", h=8), ACT.Copy), [t])
                i += 1
        t_vlast = t_v[(i - 1) % 4]

        free = {i: t_vlast for i in range(8)}
        qk_free = [None, None]
        pt_free = [None, None]
        qk_ready = {}
        m_ready = {}

        def project(u):
            n = u % 2
            w = [t_lat, t_ctx, free[0]]
            t = pe(lambda e, v: e.matmul(bank(0), wqT[:, u * P:(u + 1) * P], kvT[:, 0:S], start=True, stop=True), w)
            free[0] = tq = act(lambda e, v: e.activation(q_pair[:, n, :], bank(0), ACT.Copy), [t, qk_free[n]])
            t = pe(lambda e, v: e.matmul(bank(1), wkT[:, u * P:(u + 1) * P], kvT[:, 0:S], start=True, stop=True), [free[1]])
            free[1] = act(lambda e, v: e.activation(k_pair[:, n, 0:S], bank(1), ACT.Copy), [t, qk_free[n]])
            t = pe(lambda e, v: e.matmul(psum[:, 0, 0:C], wkT[:, u * P:(u + 1) * P], kvT[:, S:KV], start=True, stop=True), [free[0]])
            free[0] = tk = act(lambda e, v: e.activation(k_pair[:, n, S:KV], psum[:, 0, 0:C], ACT.Copy), [t, qk_free[n]])
            qk_ready[u] = tk

        def maxima(u, j):
            n = u % 2
            lo = j * HD0
            for q in range(QT):
                w = [qk_ready[u], free[0], free[1]]
                pe(lambda e, v, q=q: e.matmul(bank(0), q_pair[lo:lo + HD0, n, q * P:(q + 1) * P],
                                              k_pair[lo:lo + HD0, n, 0:S], start=True, stop=True), w, count=False)
                t = pe(lambda e, v, q=q: e.matmul(psum[:, 1, 0:C], q_pair[lo:lo + HD0, n, q * P:(q + 1) * P],
                                                  k_pair[lo:lo + HD0, n, S:KV], start=True, stop=True))
                free[0] = free[1] = dve(lambda e, v, q=q: e.tensor_reduce(
                    nm0[:, j, q:q + 1], psum[:, 0:2, :].rearrange("p n t -> p (n t)")[:, 0:KV], AX.X, ALU.max, negate=True), [t])
            return free[0]

        def maxima_to_rows(u, t):
            n = u % 2
            src = nm0[:, :, :].rearrange("p n q -> p q n")
            rem = nm0r[:, :, :].rearrange("p n q -> p q n")
            t = dve(lambda e, v: e.tensor_copy(m3[:, :, :, 0], src), [t])
            t = dve(lambda e, v: e.tensor_tensor(rem, src, m3[:, :, :, 0], ALU.subtract), [t])
            t = dve(lambda e, v: e.tensor_copy(m3[:, :, :, 1], rem), [t])
            t = dve(lambda e, v: e.tensor_tensor(m3[:, :, :, 2], rem, m3[:, :, :, 1], ALU.subtract), [t])
            for q in range(QT):
                tt = pe(lambda e, v, q=q: e.transpose(bank16(7)[0:6, q * P:(q + 1) * P],
                                                      m3[:, q, :, :].rearrange("p n k -> p (n k)"), ident16[:, :]),
                        [t, free[7]], count=q == QT - 1)
            free[7] = m_ready[u] = dve(lambda e, v: e.tensor_copy(m3T[:, n, :], bank16(7)[0:6, 0:S]), [tt, qk_free[n]])

        st_i = [0]

        def attend(u, j):
            n, h, lo = u % 2, 2 * u + j, j * HD0
            buf = h % 2
            for k in range(KT0):
                rows = min(P, KV - k * P)
                b = 2 + st_i[0] % 4
                st_i[0] += 1
                pe(lambda e, v, k=k, b=b, rows=rows: e.matmul(psum[0:rows, b, :], k_pair[lo:lo + HD0, n, k * P:k * P + rows],
                                                              q_pair[lo:lo + HD0, n, :], start=True, stop=False),
                   [m_ready[u], free[b]], count=False)
                t = pe(lambda e, v, b=b, rows=rows: e.matmul(psum[0:rows, b, :], sel[:, j, 0:rows], m3T[:, n, :],
                                                             start=False, stop=True))
                free[b] = t_e = act(lambda e, v, k=k, b=b, rows=rows: e.activation(
                    p0[0:rows, buf, k, :], psum[0:rows, b, :], ACT.Exp, scale=HD0 ** -0.5), [t, pt_free[buf]])
            qk_free[n] = t
            return t_e

        def values(u, j, t_e):
            h = 2 * u + j
            buf = h % 2
            for q in range(QT):
                for k in range(KT0):
                    rows = min(P, KV - k * P)
                    t = pe(lambda e, v, q=q, k=k, rows=rows: e.matmul(
                        psum[:, 6, q * 65:(q + 1) * 65], p0[0:rows, buf, k, q * P:(q + 1) * P], v0[0:rows, k, h, :],
                        start=k == 0, stop=k == KT0 - 1), [t_e, free[6], tv, t_vlast], count=k == KT0 - 1)
            pt_free[buf] = t
            o = psum[:, 6, 0:QT * 65].rearrange("p (q d) -> p q d", q=QT)
            t1 = dve(lambda e, v: e.reciprocal(rd0[:, :].unsqueeze(2), o[:, :, HD0:HD0 + 1]), [t])
            free[6] = dve(lambda e, v: e.tensor_tensor(att0[:, :, h * HD0:(h + 1) * HD0], o[:, :, 0:HD0],
                                                       rd0[:, :].unsqueeze(2).to_broadcast([P, QT, HD0]), ALU.mult), [t1])

        def att_transposed(u, b):
            for q in range(QT):
                t = pe(lambda e, v, q=q: e.transpose(psum[:, b, q * P:(q + 1) * P], att0[:, q, u * P:(u + 1) * P], ident[:, :]),
                       [free[6], free[b]], count=q == QT - 1)
            free[b] = act(lambda e, v: e.activation(att0T[:, u, :], bank(b), ACT.Copy), [t])

        project(0)
        maxima(0, 0)
        maxima_to_rows(0, maxima(0, 1))
        for u in range(NP0):
            if u + 1 < NP0:
                project(u + 1)
            for j in range(2):
                t_e = attend(u, j)
                if u + 1 < NP0:
                    t_m = maxima(u + 1, j)
                values(u, j, t_e)
            if u + 1 < NP0:
                maxima_to_rows(u + 1, t_m)
            att_transposed(u, 7)
        for q in range(QT):
            for u in range(NP0):
                t = pe(lambda e, v, q=q, u=u: e.matmul(psum[:, 0, q * P:(q + 1) * P], att0T[:, u, q * P:(q + 1) * P],
                                                       woT[:, u, :], start=u == 0, stop=u == NP0 - 1),
                       [free[7], free[0]], count=u == NP0 - 1)
        dve(lambda e, v: e.tensor_tensor(xb(v), xb(v), bank(0).rearrange("p (q d) -> p q d", q=QT), ALU.add), [t])
        pr.end()

        pr.begin("b1", B)
        xb1 = lambda v: x_res[:, bass.ds(v["b1"] * QT, QT), :]

        def mean_square(src, t):
            for q in range(QT):
                t1 = dve(lambda e, v, q=q: e.bn_stats(stats[:, q, :], src[:, q, :]), [t])
            for q in range(QT):
                t2 = dve(lambda e, v, q=q: e.bn_aggr(mv[:, q, :], stats[:, q, :]), [t1])
            t = dve(lambda e, v: e.tensor_tensor(ve[:, :], mv[:, :, 0], mv[:, :, 0], ALU.mult), [t2])
            t = dve(lambda e, v: e.tensor_tensor(ve[:, :], ve[:, :], mv[:, :, 1], ALU.add), [t])
            t = dve(lambda e, v: e.tensor_scalar(ve[:, :], ve[:, :], 1e-8, None, ALU.add), [t])
            return pool(lambda e, v: e.tensor_tensor(rstd[:, :], ve[:, :], neg_half[:, :], ALU.pow), [t])

        def quantise(src, work, dst, w_bc, width, wcol, t):
            for q in range(QT):
                t1 = act(lambda e, v, q=q: e.activation(work[:, q, :], src[:, q, :], ACT.Copy, scale=rstd[:, q:q + 1]), [t])
            t = dve(lambda e, v: e.tensor_tensor(work, work, w_bc.unsqueeze(1).to_broadcast([P, QT, width]), ALU.mult), [t1])
            t = dve(lambda e, v: e.tensor_reduce(small[:, 0, :], work, AX.X, ALU.max, apply_absolute_value=True), [t])
            t = dve(lambda e, v: e.tensor_scalar(small[:, 0, :], small[:, 0, :], 1e-5, None, ALU.max), [t])
            t = dve(lambda e, v: e.reciprocal(small[:, 2, :], small[:, 0, :]), [t])
            t = dve(lambda e, v: e.tensor_scalar(small[:, 2, :], small[:, 2, :], 127.0, None, ALU.mult), [t])
            t1 = dve(lambda e, v: e.tensor_scalar(small[:, 1, :], small[:, 0, :], 1.0 / 127.0, wscale[:, wcol:wcol + 1],
                                                  ALU.mult, ALU.mult), [t])
            for q in range(QT):
                t = dve(lambda e, v, q=q: e.tensor_scalar(work[:, q, :], work[:, q, :], small[:, 2, q:q + 1], MAGIC,
                                                          ALU.mult, ALU.add), [t1])
            t = dve(lambda e, v: e.tensor_scalar(work, work, -MAGIC, 127.0, ALU.add, ALU.min), [t])
            return dve(lambda e, v: e.tensor_scalar(dst, work, -128.0, None, ALU.max), [t])

        t = norm(xb1, y, QT, P, 1e-5)
        t = mean_square(y, t)
        t = quantise(y[:, :, :], z[:, :, :], zq[:, :, :], n1w_bc[:, :], D, 0, t)
        for q in range(QT):
            t1 = pe(lambda e, v, q=q: e.transpose(bank16(0)[:, q * P:(q + 1) * P], zq[:, q, :], ident16[:, :]), [t],
                    count=q == QT - 1)
        t = act(lambda e, v: e.activation(zqT, bank16(0)[:, 0:S], ACT.Copy), [t1])
        for q in range(QT):
            t1 = pe(lambda e, v, q=q: e.matmul(bank(1 + q), zqT[:, q * P:(q + 1) * P], wq1[:, :], start=True, stop=True), [t])
            t2 = act(lambda e, v, q=q: e.activation(hh[:, q, :], bank(1 + q), ACT.Relu, scale=small[:, 1, q:q + 1]), [t1])
        t = act(lambda e, v: e.activation(hh, hh, ACT.Square), [t2])
        t = dve(lambda e, v: e.tensor_scalar(hh, hh, act_sb[:, 0:1], act_sb[:, 1:2], ALU.mult, ALU.add), [t])
        t = mean_square(hh, t)
        t = quantise(hh, hr, hq, n2w_bc[:, :], DFF, 1, t)
        for c in range(FC):
            for q in range(QT):
                t1 = pe(lambda e, v, q=q, c=c: e.transpose(bank16(6 + c // 2)[:, (c % 2) * S + q * P:(c % 2) * S + (q + 1) * P],
                                                           hq[:, q, c * P:(c + 1) * P], ident16[:, :]), [t],
                        count=q == QT - 1)
            if c % 2:
                t2 = act(lambda e, v, c=c: e.activation(hqT[:, c - 1:c + 1, :].rearrange("p c t -> p (c t)"),
                                                        bank16(6 + c // 2), ACT.Copy), [t1])
        for q in range(QT):
            for c in range(FC):
                t = pe(lambda e, v, q=q, c=c: e.matmul(psum[:, 0, q * P:(q + 1) * P], hqT[:, c, q * P:(q + 1) * P],
                                                       wq2[:, c, :], start=c == 0, stop=c == FC - 1), [t2], count=c == FC - 1)
        t = dve(lambda e, v: e.tensor_tensor(z[:, :, :], bank(0).rearrange("p (q d) -> p q d", q=QT),
                                             small[:, 1, :].unsqueeze(2).to_broadcast([P, QT, D]), ALU.mult), [t])
        t = dve(lambda e, v: e.tensor_tensor(xb1(v), xb1(v), z[:, :, :], ALU.add), [t])
        t_y = norm(xb1, y, QT, P, 1e-5, [t])
        dve(lambda e, v: e.tensor_copy(x_st[:, bass.ds(v["b1"] * QT, QT), :], y[:, :, :]),
            [t_y])
        pr.end()

        pr.meet()
        for e in ("tensor", "gpsimd", "vector", "scalar"):
            loaded(e, "wl")
        for tile in (gq, gk):
            pool(lambda e, v, tile=tile: e.memset(tile.rearrange("p q h r -> p (q h r)"), 1.0))
        pool(lambda e, v: e.memset(v_self.rearrange("p k h d -> p (k h d)"), 1.0))
        pool(lambda e, v: e.memset(v_cross.rearrange("p k h d -> p (k h d)"), 1.0))
        pr.begin("l", NL)
        t_f1 = pool(lambda e, v: e.tensor_copy(f1s, wl[:, bass.ds(v["l"], 1), W_F1:W_F1 + DFF].rearrange("p o c -> p (o c)")))
        pr.begin("b", B)
        xs = lambda v: x_st[:, bass.ds(v["b"] * QT, QT), :]

        def wcols(v, lo, n):
            return wl[:, bass.ds(v["l"], 1), lo:lo + n].rearrange("p o c -> p (o c)")

        def adaptive_norm(which, bvar, src, after=()):
            t = norm(src, y, QT, P, 1e-5, after)
            t = transposes(7, y, QT, [t])
            g = lambda v, half: gb[:, bass.ds((v["l"] * 3 + which) * 2 + half, 1), bass.ds(v[bvar], 1)].rearrange("p a b -> p (a b)")
            return dve(lambda e, v: e.tensor_scalar(xnT[:, 0:S], bank(7), g(v, 0), g(v, 1), ALU.mult, ALU.add), [t])

        def rotate(eng, w, nq, rows, after):
            src = qk[0:rows, w, 0:nq, :].rearrange("p q (h d) -> p q h d", d=HD1)
            dst = rot[0:rows, w, 0:nq, :].rearrange("p q (h d) -> p q h d", d=HD1)
            tm = tmp[0:rows, w, 0:nq, :].rearrange("p q (h d) -> p q h d", d=HD1)
            tab = lambda lo, n: rope[0:rows, 0:nq, lo:lo + n].unsqueeze(2).to_broadcast([rows, nq, H1, n])
            half = HD1 // 2
            eng(lambda e, v: e.tensor_tensor(dst, src, tab(0, HD1), ALU.mult), after)
            eng(lambda e, v: e.tensor_tensor(tm[:, :, :, 0:half], src[:, :, :, half:HD1], tab(HD1, half), ALU.mult), after)
            t = eng(lambda e, v: e.tensor_tensor(tm[:, :, :, half:HD1], src[:, :, :, 0:half], tab(HD1 + half, half), ALU.mult), after)
            return eng(lambda e, v: e.tensor_tensor(rot[0:rows, w, 0:nq, :], rot[0:rows, w, 0:nq, :], tmp[0:rows, w, 0:nq, :], ALU.add), [t])

        def split3(eng, w, stack_tile, slots, nq, rows, t):
            g = stack_tile[0:rows, 0:nq, :, :].rearrange("p q h r -> p (q h) r")
            src = rot[0:rows, w, 0:nq, :].rearrange("p q (h d) -> p (q h) d", d=HD1)
            rem = tmp[0:rows, w, 0:nq, :].rearrange("p q (h d) -> p (q h) d", d=HD1)
            slot = lambda s: g[:, :, s * HD1:(s + 1) * HD1]
            where = [[s for s in range(len(slots)) if slots[s] == part] for part in range(3)]
            ends = []
            t1 = eng(lambda e, v: e.tensor_copy(slot(where[0][0]), src), [t])
            for s in where[0][1:]:
                ends.append(act(lambda e, v, s=s: e.activation(slot(s), slot(where[0][0]), ACT.Copy), [t1]))
            t2 = eng(lambda e, v: e.tensor_tensor(rem, src, slot(where[0][0]), ALU.subtract), [t1])
            t3 = eng(lambda e, v: e.tensor_copy(slot(where[1][0]), rem), [t2])
            for s in where[1][1:]:
                ends.append(act(lambda e, v, s=s: e.activation(slot(s), slot(where[1][0]), ACT.Copy), [t3]))
            ends.append(eng(lambda e, v: e.tensor_tensor(slot(where[2][0]), rem, slot(where[1][0]), ALU.subtract), [t3]))
            return ends

        def stack_up(src, dst, banks, after, bfree):
            for i, u in enumerate(range(0, 8, 2)):
                b = banks[i % len(banks)]
                for n in range(2):
                    for q in range(QT):
                        t = pe(lambda e, v, n=n, q=q, u=u, b=b: e.transpose(
                            bank16(b)[:, n * S + q * P:n * S + (q + 1) * P],
                            src[:, q, 2 * (u + n):2 * (u + n) + 2, :].rearrange("p h r -> p (h r)"), ident16[:, :]),
                            list(after) + [bfree.get(b)], count=n == 1 and q == QT - 1)
                f = act if i % 2 else dve
                cp = (lambda e, v, u=u, b=b: e.activation(dst[:, u:u + 2, :].rearrange("p u t -> p (u t)"), bank16(b), ACT.Copy)) if i % 2 \
                    else (lambda e, v, u=u, b=b: e.tensor_copy(dst[:, u:u + 2, :].rearrange("p u t -> p (u t)"), bank16(b)))
                bfree[b] = f(cp, [t])
            return [bfree[b] for b in banks]

        def attention(q_ready, k_ready, kt_n, key_rows, vst, v_ready, bfree):
            nkeys = (kt_n - 1) * P + key_rows
            cnt = [0]
            qm_free = [None, None]
            pt_free = [None, None]
            o_free = [None, None]
            q_after = {}

            def max_step(g, i):
                j, q = divmod(i, QT)
                u, lo = (GROUP * g + j) // 2, ((GROUP * g + j) % 2) * STACK
                if kt_n > 1:
                    b = cnt[0] % 2
                    cnt[0] += 1
                    t = pe(lambda e, v: e.matmul(bank(b), q_st[lo:lo + NMAX, u, q * P:(q + 1) * P], k_st[lo:lo + NMAX, u, 0:S],
                                                 start=True, stop=True), list(q_ready) + list(k_ready) + [bfree.get(b)])
                    bfree[b] = dve(lambda e, v: e.tensor_reduce(nm[:, g, q, j:j + 1], bank(b), AX.X, ALU.max, negate=True), [t])
                else:
                    b = cnt[0] % 2
                    t = pe(lambda e, v: e.matmul(psum[:, b, q * P:q * P + nkeys], q_st[lo:lo + NMAX, u, q * P:(q + 1) * P],
                                                 k_st[lo:lo + NMAX, u, 0:nkeys], start=True, stop=True),
                           list(q_ready) + list(k_ready) + [bfree.get(b)])
                    if q == QT - 1:
                        cnt[0] += 1
                        bfree[b] = dve(lambda e, v: e.tensor_reduce(
                            nm[:, g, :, j:j + 1], bank(b).rearrange("p (q k) -> p q k", q=QT)[:, :, 0:nkeys], AX.X, ALU.max,
                            negate=True), [t])
                return bfree.get(b)

            def shift(g, t):
                heads = gq[:, :, GROUP * g:GROUP * (g + 1), :]
                col = lambda c: heads[:, :, :, MROW + 1 + c]
                t = pool(lambda e, v: e.tensor_copy(col(0), nm[:, g, :, :]), [t])
                t = pool(lambda e, v: e.tensor_tensor(nmr[:, g, :, :], nm[:, g, :, :], col(0), ALU.subtract), [t])
                t = pool(lambda e, v: e.tensor_copy(col(1), nmr[:, g, :, :]), [t])
                t = pool(lambda e, v: e.tensor_tensor(col(2), nmr[:, g, :, :], col(1), ALU.subtract), [t])
                for n in range(2):
                    for q in range(QT):
                        t1 = pe(lambda e, v, n=n, q=q: e.transpose(
                            bank16(7)[:, n * S + q * P:n * S + (q + 1) * P],
                            gq[:, q, 4 * g + 2 * n:4 * g + 2 * n + 2, :].rearrange("p h r -> p (h r)"), ident16[:, :]),
                            [t, bfree.get(7)], count=n == 1 and q == QT - 1)
                bfree[7] = act(lambda e, v: e.activation(q_m[:, g % 2, :, :].rearrange("p u t -> p (u t)"), bank16(7), ACT.Copy),
                               [t1, qm_free[g % 2]])
                q_after[g] = bfree[7]

            step = [0]

            def exp_step(g, k, half):
                s = step[0] % 2
                step[0] += 1
                rows = P if k < kt_n - 1 else key_rows
                buf = (g * kt_n + k) % 2
                b0 = 2 + 2 * s
                for n in range(2):
                    t = pe(lambda e, v, n=n: e.matmul(psum[0:rows, b0 + n, :],
                                                      k_st[n * STACK:n * STACK + NALL, 2 * g + half, k * P:k * P + rows],
                                                      q_m[n * STACK:n * STACK + NALL, g % 2, half, :], start=True, stop=True),
                           [q_after[g], bfree.get(b0), bfree.get(b0 + 1)], count=n == 1)
                qm_free[g % 2] = t
                bfree[b0] = bfree[b0 + 1] = act(lambda e, v: e.activation(
                    pT[0:rows, buf, 2 * half:2 * half + 2, :].rearrange("p j t -> p (j t)"),
                    psum[0:rows, b0:b0 + 2, :].rearrange("p n t -> p (n t)"), ACT.Exp, scale=HD1 ** -0.5),
                    [t, pt_free[buf]])
                return bfree[b0]

            def pv(g, k, t):
                rows = P if k < kt_n - 1 else key_rows
                buf = (g * kt_n + k) % 2
                for j in range(GROUP):
                    t1 = pe(lambda e, v, j=j: e.matmul(psum[32 * j:32 * j + 32, 6, :], vst[0:rows, k, GROUP * g + j, :],
                                                       pT[0:rows, buf, j, :], start=k == 0, stop=k == kt_n - 1),
                            [t, bfree.get(6)] + list(v_ready), count=j == GROUP - 1)
                pt_free[buf] = t1
                return t1

            def finish(g, t):
                bfree[6] = t = act(lambda e, v: e.activation(o_sb[:, g % 2, :], bank(6), ACT.Copy), [t, o_free[g % 2]])
                for q in range(QT):
                    t1 = pe(lambda e, v, q=q: e.transpose(psum[:, 7, q * P:(q + 1) * P], o_sb[:, g % 2, q * P:(q + 1) * P], ident[:, :]),
                            [t, bfree.get(7)], count=q == QT - 1)
                o_free[g % 2] = t1
                o = bank(7).rearrange("p (q j d) -> p q j d", q=QT, j=GROUP)
                t2 = dve(lambda e, v: e.reciprocal(rd[:, g, :, :], o[:, :, :, HD1]), [t1])
                w = GROUP * HD1
                bfree[7] = dve(lambda e, v: e.tensor_tensor(
                    att[:, :, g * w:(g + 1) * w].rearrange("p q (j d) -> p q j d", d=HD1), o[:, :, :, 0:HD1],
                    rd[:, g, :, :].unsqueeze(3).to_broadcast([P, QT, GROUP, HD1]), ALU.mult), [t2])
                return bfree[7]

            for i in range(16):
                t = max_step(0, i)
            shift(0, t)
            n_steps = 2 * kt_n
            for g in range(NG):
                i = 0
                pend = None
                for k in range(kt_n):
                    for half in range(2):
                        t = exp_step(g, k, half)
                        if g + 1 < NG:
                            upto = 16 * (2 * k + half + 1) // n_steps
                            while i < upto:
                                t_m = max_step(g + 1, i)
                                i += 1
                        if half == 0 and pend is not None:
                            pv(*pend)
                            pend = None
                    pend = (g, k, t)
                if g + 1 < NG:
                    shift(g + 1, t_m)
                t = pv(*pend)
                t = finish(g, t)
            return t

        def project_out(wcol, t, bfree):
            t = transposes(7, att, QT, [t])
            t = act(lambda e, v: e.activation(attT, bank(7), ACT.Copy), [t])
            for q in range(QT):
                t1 = pe(lambda e, v, q=q: e.matmul(psum[:, 0, q * P:(q + 1) * P], attT[:, q * P:(q + 1) * P], wcols(v, wcol, D),
                                                   start=True, stop=True), [t, bfree.get(0)])
            bfree[0] = dve(lambda e, v: e.tensor_tensor(xs(v), xs(v), bank(0).rearrange("p (q d) -> p q d", q=QT), ALU.add), [t1])
            return bfree[0]

        t_cb = pool(lambda e, v: e.tensor_copy(ctx_b[:, 0:C], ctxT[:, bass.ds(v["b"], 1), :].rearrange("p o c -> p (o c)")))
        t = adaptive_norm(0, "b", xs)
        ready = []
        t_vs = None
        for q in range(QT):
            t1 = pe(lambda e, v, q=q: e.matmul(psum[:, 2 + q, 0:384], xnT[:, q * P:(q + 1) * P], wcols(v, W_QKV, 384),
                                               start=True, stop=True), [t])
            t2 = act(lambda e, v, q=q: e.activation(qk[:, :, q, :], psum[:, 2 + q, 0:256].rearrange("p (w c) -> p w c", w=2),
                                                    ACT.Copy), [t1])
            t_vs = act(lambda e, v, q=q: e.activation(v_self[:, q, :, 0:HD1],
                                                      psum[:, 2 + q, 256:384].rearrange("p (h d) -> p h d", h=H1), ACT.Copy), [t1])
        bfree = {}
        tq = rotate(dve, 0, QT, P, [t2])
        tk = rotate(pool, 1, QT, P, [t2])
        t_mk = dve(lambda e, v: e.tensor_copy(
            gk[:, :, :, MROW], mask_row[:, bass.ds(v["b"] * QT, QT)].unsqueeze(2).to_broadcast([P, QT, H1])))
        eq = split3(dve, 0, gq, SLOT_Q, QT, P, tq)
        ek = split3(pool, 1, gk, SLOT_K, QT, P, tk)
        for b in (2, 3, 4, 5):
            bfree[b] = t_vs
        rq = stack_up(gq, q_st, (2, 3), eq, bfree)
        rk = stack_up(gk, k_st, (4, 5), ek + [t_mk], bfree)
        t = attention(rq, rk, QT, P, v_self, [t_vs], bfree)
        t = project_out(W_SO, t, bfree)
        pr.meet()
        t = adaptive_norm(1, "b", xs, [t])
        for q in range(QT):
            t1 = pe(lambda e, v, q=q: e.matmul(psum[:, 2, q * P:(q + 1) * P], xnT[:, q * P:(q + 1) * P], wcols(v, W_CQ, D),
                                               start=True, stop=True), [t])
        t2 = act(lambda e, v: e.activation(qk[:, 0, :, :], bank(2).rearrange("p (q c) -> p q c", q=QT), ACT.Copy), [t1])
        t1 = pe(lambda e, v: e.matmul(psum[0:C, 3, 0:256], ctx_b[:, 0:C], wcols(v, W_CKV, 256), start=True, stop=True), [t_cb])
        t3 = act(lambda e, v: e.activation(qk[0:C, 1, 0, :], psum[0:C, 3, 0:128], ACT.Copy), [t1])
        t_vc = act(lambda e, v: e.activation(v_cross[0:C, 0, :, 0:HD1],
                                             psum[0:C, 3, 128:256].rearrange("p (h d) -> p h d", h=H1), ACT.Copy), [t1])
        bfree = {2: t2, 3: t_vc}
        tq = rotate(dve, 0, QT, P, [t2])
        tk = rotate(pool, 1, 1, C, [t3])
        t_mk = dve(lambda e, v: e.tensor_copy(
            gk[0:C, 0, :, MROW], maskc_row[0:C, bass.ds(v["b"], 1)].to_broadcast([C, H1])))
        eq = split3(dve, 0, gq, SLOT_Q, QT, P, tq)
        ek = split3(pool, 1, gk, SLOT_K, 1, C, tk)
        rq = stack_up(gq, q_st, (2, 3), eq, bfree)
        for u in range(8):
            t1 = pe(lambda e, v, u=u: e.transpose(bank16(4)[:, u * P:u * P + C], gk[0:C, 0, 2 * u:2 * u + 2, :].rearrange("p h r -> p (h r)"),
                                                  ident16[0:C, 0:C]), ek + [t_mk], count=u == 7)
        bfree[4] = act(lambda e, v: e.activation(k_st[:, :, 0:C], bank16(4).rearrange("p (u c) -> p u c", u=8)[:, :, 0:C], ACT.Copy), [t1])
        t = attention(rq, [bfree[4]], 1, C, v_cross, [t_vc], bfree)
        t = project_out(W_CO, t, bfree)
        pr.end()
        pr.begin("f", B)
        xf = lambda v: x_st[:, bass.ds(v["f"] * QT, QT), :]
        t = adaptive_norm(2, "f", xf)
        for c in range(FC):
            t1 = pe(lambda e, v, c=c: e.matmul(bank(1 + c), f1s[:, c * P:(c + 1) * P], xnT[:, 0:S], start=True, stop=True), [t, t_f1])
            t2 = act(lambda e, v, c=c: e.activation(hT[:, c, :], bank(1 + c), ACT.Gelu, bias=f1b[:, bass.ds(v["l"] * FC + c, 1)]), [t1])
        for q in range(QT):
            for c in range(FC):
                pe(lambda e, v, q=q, c=c: e.matmul(psum[:, 0, q * P:(q + 1) * P], hT[:, c, q * P:(q + 1) * P],
                                                   wcols(v, W_F2 + c * D, D), start=c == 0, stop=False), [t2], count=False)
            t = pe(lambda e, v, q=q: e.matmul(psum[:, 0, q * P:(q + 1) * P], ones_sq[0:1, :], f2b[0:1, bass.ds(v["l"] * D, D)],
                                              start=False, stop=True))
        dve(lambda e, v: e.tensor_tensor(xf(v), xf(v), bank(0).rearrange("p (q d) -> p q d", q=QT), ALU.add), [t])
        pr.end()
        pr.end()
        pr.meet(phase=True)

        load("wm", A1[:, 0:1552], a["wm"], 2)
        for e in ("tensor", "vector"):
            loaded(e, "wm")
        pr.begin("m", B)
        xm = lambda v: x_res[:, bass.ds(v["m"] * QT, QT), :]
        t = dve(lambda e, v: e.tensor_tensor(xm(v), xm(v), x_st[:, bass.ds(v["m"] * QT, QT), :], ALU.add))
        t = norm(xm, y, QT, P, 1e-5, [t])
        t = transposes(7, y, QT, [t])
        t = act(lambda e, v: e.activation(xnT[:, 0:S], bank(7), ACT.Copy), [t])
        for q in range(QT):
            t1 = pe(lambda e, v, q=q: e.matmul(psum[:, 0, q * E:(q + 1) * E], xnT[:, q * P:(q + 1) * P], gateT, start=True, stop=True), [t])
        lgv = psum[:, 0, 0:QT * E].rearrange("p (q e) -> p q e", q=QT)
        t = dve(lambda e, v: e.tensor_copy(lg, lgv), [t1])
        t = dve(lambda e, v: e.tensor_reduce(top[:, 0, :], lg, AX.X, ALU.max), [t])
        t_rw = act(lambda e, v: e.activation(top[:, 1, :], top[:, 0, :], ACT.Sigmoid), [t])
        t = dve(lambda e, v: e.tensor_tensor(oh, lg, top[:, 0, :].unsqueeze(2).to_broadcast([P, QT, E]), ALU.is_equal), [t])
        t = dve(lambda e, v: e.tensor_tensor(oh, oh, rank.unsqueeze(1).to_broadcast([P, QT, E]), ALU.mult), [t])
        t = dve(lambda e, v: e.tensor_reduce(top[:, 2, :], oh, AX.X, ALU.max), [t])
        t_oh = dve(lambda e, v: e.tensor_tensor(oh, oh, top[:, 2, :].unsqueeze(2).to_broadcast([P, QT, E]), ALU.is_equal), [t])
        t2 = None
        gates, ups = [], []
        for q in range(QT):
            t1 = pe(lambda e, v, q=q: e.matmul(bank(1 + q % 2), xnT[:, q * P:(q + 1) * P], wgT, start=True, stop=True),
                    [ups[q - 2]] if q >= 2 else [])
            gates.append(act(lambda e, v, q=q: e.activation(eg[:, q, :], bank(1 + q % 2), ACT.Copy, scale=top[:, 1, q:q + 1]), [t1, t_rw]))
            t1 = pe(lambda e, v, q=q: e.matmul(bank(3 + q % 2), xnT[:, q * P:(q + 1) * P], wuT, start=True, stop=True),
                    [ups[q - 2]] if q >= 2 else [])
            ups.append(act(lambda e, v, q=q: e.activation(eu[:, q, :], bank(3 + q % 2), ACT.Copy, scale=top[:, 1, q:q + 1]), [t1]))
        t = act(lambda e, v: e.activation(es, eg, ACT.Sigmoid), [ups[-1]])
        t1 = dve(lambda e, v: e.tensor_tensor(eu, eu, eg, ALU.mult), [ups[-1]])
        t1 = dve(lambda e, v: e.tensor_tensor(eu, eu, es, ALU.mult), [t, t1])
        for q in range(QT):
            t = dve(lambda e, v, q=q: e.tensor_tensor(es[:, q, :].rearrange("p (e i) -> p e i", e=E), eu[:, q, :].rearrange("p (e i) -> p e i", e=E),
                                                      oh[:, q, :].unsqueeze(2).to_broadcast([P, E, I]), ALU.mult), [t1, t_oh])
        for c in range(FC):
            for q in range(QT):
                t1 = pe(lambda e, v, q=q, c=c: e.transpose(psum[:, 3 + c, q * P:(q + 1) * P], es[:, q, c * P:(c + 1) * P], ident[:, :]),
                        [t], count=q == QT - 1)
            t2 = act(lambda e, v, c=c: e.activation(ehT[:, c, :], bank(3 + c), ACT.Copy), [t1])
        for q in range(QT):
            for c in range(FC):
                t = pe(lambda e, v, q=q, c=c: e.matmul(psum[:, 0, q * P:(q + 1) * P], ehT[:, c, q * P:(q + 1) * P], wdT[:, c, :],
                                                       start=c == 0, stop=c == FC - 1), [t2, t_oh], count=c == FC - 1)
        dve(lambda e, v: e.tensor_tensor(xm(v), xm(v), bank(0).rearrange("p (q d) -> p q d", q=QT), ALU.add), [t])
        pr.end()
        pr.meet(phase=True)

        block = ctx.enter_context(nc.Block())

        @block.sync
        def _(eng):
            for s, dst, src, after in dma_list:
                if after:
                    eng.wait_ge(phase, after)
                eng.dma_start(dst, src).then_inc(s, 16)
            eng.wait_ge(phase, 3)
            eng.dma_start(out.rearrange("b (q p) d -> p (b q) d", p=P), x_res[:, :, :]).then_inc(s_out, 16)
            eng.wait_ge(s_out, 16)

        @block.tensor
        def _(eng):
            pr.emit("tensor", eng, (done, arrived, go, phase))

        @block.vector
        def _(eng):
            pr.emit("vector", eng, (done, arrived, go, phase))

        @block.scalar
        def _(eng):
            pr.emit("scalar", eng, (done, arrived, go, phase))

        @block.gpsimd
        def _(eng):
            pr.emit("gpsimd", eng, (done, arrived, go, phase))


def kernel(**inputs):
    import concourse.bacc as _bacc
    from concourse.bass_utils import run_bass_kernel_spmd as _run

    g = {k: np.asarray(v) for k, v in inputs.items()}
    c = np.ascontiguousarray

    def cols(*parts):
        return c(np.concatenate([p.reshape(P, -1) for p in parts], axis=1))

    def chunks(w):
        return w.reshape(-1, P, w.shape[-1]).transpose(1, 0, 2).reshape(P, -1)

    def words(m):
        wide = np.zeros(m.shape + (4,), m.dtype)
        wide[..., 0] = m
        return wide.view(np.int32)[..., 0].copy()

    L = "L1_xcond_"
    layer = [cols(g[L + "qkv_w"][l].T, g[L + "so_w"][l].T, g[L + "cq_w"][l].T, g[L + "ck_w"][l].T, g[L + "cv_w"][l].T,
                  g[L + "co_w"][l].T, g[L + "f1_w"][l].T, chunks(g[L + "f2_w"][l].T)) for l in range(NL)]
    norms_w = np.stack([g[L + f"n{n}_w"] for n in (1, 2, 3)], axis=1).reshape(NL * 6, D, D)
    norms_b = np.stack([g[L + f"n{n}_b"] for n in (1, 2, 3)], axis=1).reshape(NL * 6, D)
    wkv = g["L0_xcond_Wkv"]
    arrays = {
        "x": c(g["x"]),
        "ctx": c(g["ctx_1024"]),
        "ctxT": c(g["ctx_1024"].transpose(2, 0, 1)),
        "condT": c(g["cond_1024"].T),
        "ident": np.eye(P, dtype=np.float32),
        "rope": rope_tables(),
        "mask": words(g["mask_BxS_bf0"].reshape(B * QT, P).T),
        "maskc": words(g["mask_BxS2_bf0"].T),
        "vec": c(np.stack([g["L0_xcond_ln1_w"], g["L0_xcond_ln1_b"], g["L0_xcond_ln2_w"], g["L0_xcond_ln2_b"]], axis=1)),
        "n1w": c(g["L0_ffn_norm1_w"]),
        "n2w": c(g["L0_ffn_norm2_w"]),
        "actsb": c(np.concatenate([g["L0_ffn_act_scale"], g["L0_ffn_act_bias"]])),
        "nb": c(norms_b.T),
        "f1b": c(g[L + "f1_b"].reshape(NL * FC, P).T),
        "f2b": c(g[L + "f2_b"].reshape(1, NL * D)),
        "nT": cols(norms_w.transpose(2, 0, 1)),
        "w1T": c(g["L0_ffn_w1"].T),
        "w2T": c(chunks(g["L0_ffn_w2"].T)),
        "w0": cols(g["L0_xcond_Wq"].T, wkv[:INNER].T, wkv[INNER:].T, chunks(g["L0_xcond_Wo"].T)),
        "wl": cols(*layer),
        "wm": cols(g["L1_ffn_w_gate"].reshape(E * I, D).T, g["L1_ffn_w_up"].reshape(E * I, D).T,
                   chunks(g["L1_ffn_w_down"].transpose(0, 2, 1).reshape(E * I, D)), g["L1_ffn_gate_w"].T,
                   np.tile(np.arange(E, 0, -1, dtype=np.float32), (P, 1))),
        "rank": np.tile(np.arange(E, 0, -1, dtype=np.float32), (P, 1)),
    }
    nc = _bacc.Bacc("TRN2", target_bir_lowering=False, num_devices=1)
    aps, feed = {}, {}
    for name, v in arrays.items():
        aps[name] = nc.dram_tensor("in_" + name, v.shape, mybir.dt.from_np(v.dtype), kind="ExternalInput").ap()
        feed["in_" + name] = v
    out = nc.dram_tensor("out_0", (B, S, D), fp32, kind="ExternalOutput").ap()
    build(nc, aps, out)
    r = _run(nc, [feed], core_ids=[0])
    return r.results[0]["out_0"]
```

```python
import numpy as np
import concourse.bass as bass
from concourse import mybir
from concourse.alu_op_type import AluOpType as ALU
from contextlib import ExitStack

fp32 = mybir.dt.float32
bf16 = mybir.dt.bfloat16
ACT = mybir.ActivationFunctionType
AX = mybir.AxisListType

B, S, D = 4, 512, 128
P = 128
QT = S // P
C = 77
H0, HD0 = 16, 64
INNER = H0 * HD0
NP0 = INNER // P
KV = S + C
KT0 = (KV + P - 1) // P
NL, H1, HD1 = 6, 16, 8
DFF = 512
FC = DFF // P
E, I = 8, 64
V_COLS = 168
GROUP = 4
NG = H1 // GROUP
SLOT_Q = (0, 0, 0, 1, 1, 2)
SLOT_K = (0, 1, 2, 0, 1, 0)
MROW = len(SLOT_Q) * HD1
STACK = 64
MAGIC = 1.5 * 2.0 ** 23

A_WORDS = 34440
W_QKV, W_SO, W_CQ, W_CKV, W_CO, W_F1, W_F2, W_COLS = 0, 384, 512, 640, 896, 1024, 1536, 2048


class Program:

    ENGINES = ("tensor", "vector", "scalar", "gpsimd")

    def __init__(self):
        self.n = {e: 0 for e in self.ENGINES}
        self.segment = 0
        self.stack = {e: [[]] for e in self.ENGINES}

    def add(self, engine, fn, after=(), count=True):
        self.stack[engine][-1].append(("do", fn, [t for t in after if t is not None], count, self.segment))
        if not count:
            return None
        self.n[engine] += 1
        return (engine, self.n[engine], self.segment)

    def pe(self, fn, after=(), count=True):
        return self.add("tensor", fn, after, count)

    def dve(self, fn, after=()):
        return self.add("vector", fn, after)

    def act(self, fn, after=()):
        return self.add("scalar", fn, after)

    def pool(self, fn, after=()):
        return self.add("gpsimd", fn, after)

    def meet(self, phase=False):
        for e in self.ENGINES:
            self.stack[e][-1].append(("meet", dict(self.n), phase))
        self.n = {e: 0 for e in self.ENGINES}
        self.segment += 1

    def begin(self, name, times, first=0):
        self.meet()
        for e in self.ENGINES:
            body = []
            self.stack[e][-1].append(("loop", name, first, times, body))
            self.stack[e].append(body)

    def end(self):
        self.meet()
        for e in self.ENGINES:
            self.stack[e].pop()

    def emit(self, engine, handle, sems, queue=None, env=None):
        done, arrived, go, phase_sem = sems
        env = {} if env is None else env
        seen = {}
        for item in self.stack[engine][0] if queue is None else queue:
            if item[0] == "loop":
                _, name, first, times, body = item
                with handle.Fori(first, first + times) as i:
                    self.emit(engine, handle, sems, body, {name: i})
            elif item[0] == "set":
                env = {item[1]: item[2]}
            elif item[0] == "meet":
                _, counts, phase = item
                for e in self.ENGINES:
                    if counts[e] > seen.get(e, 0):
                        handle.wait_ge(done[e], counts[e])
                if engine == "gpsimd":
                    handle.wait_ge(arrived, len(self.ENGINES) - 1)
                    handle.sem_clear(arrived)
                    for e in self.ENGINES:
                        handle.sem_clear(done[e])
                    if phase:
                        handle.sem_inc(phase_sem, 1)
                    for e in self.ENGINES:
                        if e != engine:
                            handle.sem_inc(go[e], 1)
                else:
                    handle.sem_inc(arrived, 1)
                    handle.wait_ge(go[engine], 1)
                    handle.sem_clear(go[engine])
                seen = {}
            else:
                _, fn, after, count, segment = item
                need = {}
                for e, local, seg in after:
                    if seg == segment and local > seen.get(e, 0):
                        need[e] = max(need.get(e, 0), local)
                for e, local in need.items():
                    handle.wait_ge(done[e], local)
                    seen[e] = local
                ins = fn(handle, env)
                if count:
                    ins.then_inc(done[engine], 1)


def at(e, v, back, what):
    key = (back, what)
    if key not in v:
        n = v["n"] - back
        got = {"batch": lambda: n % B, "layer": lambda: n // B, "step": lambda: n}[what]()
        v[key] = got if isinstance(got, int) else e.snap(got)
    return v[key]


def run_beside(core, *others):
    live = list(others)
    for _ in core:
        for g in list(live):
            if next(g, "end") == "end":
                live.remove(g)
    while live:
        for g in list(live):
            if next(g, "end") == "end":
                live.remove(g)


def rope_tables():
    half = HD1 // 2
    inv = (1.0 / np.float32(10000.0) ** (np.arange(half, dtype=np.float32) / np.float32(half))).astype(np.float32)
    ang = np.arange(S, dtype=np.float32)[:, None] * inv
    cos, sin = np.cos(ang).astype(np.float32), np.sin(ang).astype(np.float32)
    table = np.concatenate([cos, cos, -sin, sin], axis=1)
    return np.ascontiguousarray(table.reshape(QT, P, 16).transpose(1, 0, 2)).reshape(P, QT * 16)


def build(nc, a, out):
    pr = Program()
    pe, dve, act, pool = pr.pe, pr.dve, pr.act, pr.pool
    ctx = ExitStack()
    with ctx:
        def sb(name, shape, dt=fp32):
            return ctx.enter_context(nc.sbuf_tensor(name, shape, dt))

        psum = ctx.enter_context(nc.psum_tensor("psum", [P, 8, 512], fp32))

        def bank(i, n=1):
            return psum[:, i:i + n, :] if n > 1 else psum[:, i, :]

        def bank16(i):
            return psum[:, i, :].bitcast(bf16)

        x_res = sb("x_res", [P, B * QT, D])
        x_st = sb("x_st", [P, B * QT, D])
        ctxT = sb("ctxT", [P, B, C])
        condT = sb("condT", [P, B])
        ident = sb("ident", [P, P])
        ident16 = sb("ident16", [P, P], bf16)
        rope = sb("rope", [P, QT, 16])
        ones_sq = sb("ones_sq", [P, P])
        neg_half = sb("neg_half", [P, QT])
        sel = sb("sel", [6, 2, P], bf16)
        mask_in = sb("mask_in", [P, B * QT], mybir.dt.int32)
        maskc_in = sb("maskc_in", [P, B], mybir.dt.int32)
        mask_row = sb("mask_row", [P, B * QT])
        maskc_row = sb("maskc_row", [P, B])
        vec = sb("vec", [P, 4])
        lat_g = sb("lat_g", [P, B])
        lat_b = sb("lat_b", [P, B])
        act_sb = sb("act_sb", [P, 2])
        gb = sb("gb", [P, 6 * NL * B])
        nb = sb("nb", [P, NL * 6])
        f1b = sb("f1b", [P, NL * FC])
        f2b = sb("f2b", [1, NL * D])
        wscale = sb("wscale", [P, 2])
        A0 = sb("A0", [P, A_WORDS])
        A1 = sb("A1", [P, 12288])
        stats = sb("stats", [P, QT, 6])
        mv = sb("mv", [P, QT, 2])
        ve = sb("ve", [P, QT])
        rstd = sb("rstd", [P, QT])
        wsum = sb("wsum", [P, 2])
        small = sb("small", [P, 8, QT])

        def sem(name):
            return ctx.enter_context(nc.semaphore(name))

        done = {e: sem(f"done_{e}") for e in Program.ENGINES}
        go = {e: sem(f"go_{e}") for e in Program.ENGINES if e != "gpsimd"}
        arrived, phase = sem("arrived"), sem("phase")
        s_first, s_w0, s_wl, s_wm, s_out = sem("s_first"), sem("s_w0"), sem("s_wl"), sem("s_wm"), sem("s_out")

        loads = {"first": 0, "w0": 0, "wl": 0, "wm": 0}
        sems = {"first": s_first, "w0": s_w0, "wl": s_wl, "wm": s_wm}
        dma_list = []

        def load(group, dst, src, after=0):
            loads[group] += 16
            dma_list.append((sems[group], dst, src, after))

        def loaded(engine, group):
            pr.stack[engine][-1].append(("do", lambda e, v: e.wait_ge(sems[group], loads[group]), [], False, pr.segment))

        above = [25000]

        def tile(*shape, dt=fp32):
            n = int(np.prod(shape)) * (1 if dt == fp32 else 2) // (1 if dt == fp32 else 4)
            above[0] += n
            flat = A0[:, above[0] - n:above[0]]
            flat = flat if dt == fp32 else flat.bitcast(dt)
            return flat if len(shape) == 1 else flat.rearrange("p (a b) -> p a b", b=shape[-1])

        ctx_sb = tile(B, D)
        n1w_bc = tile(D)
        n2w_bc = tile(DFF)
        wq1 = tile(DFF, dt=bf16)
        wq2 = tile(FC, D, dt=bf16)
        y = tile(QT, D)
        z = tile(QT, D)
        zc = tile(D)
        zq = tile(QT, D, dt=bf16)
        xnT = tile(640)
        m3T = tile(2, S, dt=bf16)[0:6]
        wqT = A0[:, 0:1024]
        wkT = A0[:, 1024:2048]
        wvT = A0[:, 2048:3072]
        woT = A0[:, 3072:4096].rearrange("p (u d) -> p u d", d=D)
        q_pair = A0[:, 4096:5120].rearrange("p (n t) -> p n t", n=2)
        k_pair = A0[:, 5120:6400].rearrange("p (n t) -> p n t", n=2)
        v0 = A0[:, 6400:6400 + KT0 * H0 * 65].rearrange("p (k h d) -> p k h d", k=KT0, h=H0)
        p0 = A0[:, 11600:11600 + 2 * KT0 * S].rearrange("p (n k t) -> p n k t", n=2, k=KT0)
        att0 = A0[:, 16720:16720 + QT * INNER].rearrange("p (q c) -> p q c", q=QT)
        att0T = A0[:, 20816:20816 + NP0 * S].rearrange("p (u t) -> p u t", u=NP0)
        kvT = xnT
        nm0 = sb("nm0", [P, 2, QT])
        nm0r = sb("nm0r", [P, 2, QT])
        m3 = sb("m3", [P, QT, 2, 3], bf16)
        rd0 = sb("rd0", [P, QT])
        wl = A1[:, 0:NL * W_COLS].rearrange("p (l c) -> p l c", l=NL)
        nT = A0[:, 0:NL * 3 * 2 * D].rearrange("p (j o) -> p j o", o=D)
        w1T = A0[:, 4608:5120]
        w2T = A0[:, 5120:5632].rearrange("p (c d) -> p c d", d=D)
        hh = A0[:, 0:QT * DFF].rearrange("p (q f) -> p q f", q=QT)
        hr = A0[:, 2048:2048 + QT * DFF].rearrange("p (q f) -> p q f", q=QT)
        hq = A0[:, 4096:5120].bitcast(bf16).rearrange("p (q f) -> p q f", q=QT)
        hqT = A0[:, 5120:6144].bitcast(bf16).rearrange("p (c t) -> p c t", c=FC)
        zqT = A0[:, 6144:6400].bitcast(bf16)
        place = [0]

        def words(n):
            place[0] += n
            assert place[0] <= A_WORDS
            return A0[:, place[0] - n:place[0]]

        class Set:
            pass

        so, co = Set(), Set()
        for w, kt_n, keys in ((so, QT, S), (co, 1, C + C % 2)):
            w.kt_n, w.keys = kt_n, keys
            w.gq_raw = words(2048)
            w.gq = w.gq_raw.bitcast(bf16).rearrange("p (q h r) -> p q h r", q=QT, h=H1)
            w.gk_raw = words(kt_n * 768)
            w.gk = w.gk_raw.bitcast(bf16).rearrange("p (q u c) -> p q u c", q=kt_n, u=H1 // 2)
            w.q_st = words(2048).bitcast(bf16).rearrange("p (u t) -> p u t", u=8)
            w.k_st = words(H1 * keys // 2).bitcast(bf16).rearrange("p (h t) -> p h t", h=H1)
            w.v_raw = words(kt_n * V_COLS)
            w.v = w.v_raw.rearrange("p (k c) -> p k c", k=kt_n)
            w.att = words(512).rearrange("p (q c) -> p q c", q=QT)
            w.nm = words(64).rearrange("p (g q j) -> p g q j", g=NG, q=QT)
            w.nmr = words(64).rearrange("p (g q j) -> p g q j", g=NG, q=QT)
            w.rd = words(64).rearrange("p (g q j) -> p g q j", g=NG, q=QT)
            kq = kt_n * P
            w.raw = words(3 * (512 + kq))
            w.qk = [w.raw[:, 0:512], w.raw[:, 512:512 + kq]]
            w.rot = [w.raw[:, 512 + kq:1024 + kq], w.raw[:, 1024 + kq:1024 + 2 * kq]]
            w.tmp = [w.raw[:, 1024 + 2 * kq:1536 + 2 * kq], w.raw[:, 1536 + 2 * kq:1536 + 3 * kq]]
            w.xnT = words(512)
            w.stats = words(QT * 6).rearrange("p (q c) -> p q c", q=QT)
            w.mv = words(QT * 2).rearrange("p (q c) -> p q c", q=QT)
            w.ve, w.rstd = words(QT), words(QT)
        hT = so.raw[:, 0:2048].rearrange("p (c t) -> p c t", c=FC)
        q_m = words(1024).bitcast(bf16).rearrange("p (n u t) -> p n u t", n=2, u=2)
        so.pT = words(4096).rearrange("p (n j t) -> p n j t", n=2, j=GROUP)
        co.pT = words(2048).rearrange("p (n j t) -> p n j t", n=1, j=GROUP)
        so.o = words(512)
        attT = words(512)
        co.o = words(512)
        ctx_b = words(P)
        f1s = words(512)
        wgT = A1[:, 0:512]
        wuT = A1[:, 512:1024]
        wdT = A1[:, 1024:1536].rearrange("p (c d) -> p c d", d=D)
        gateT = A1[:, 1536:1544]
        rank = A1[:, 1544:1552]
        eg = A0[:, 0:QT * E * I].rearrange("p (q f) -> p q f", q=QT)
        eu = A0[:, 2048:4096].rearrange("p (q f) -> p q f", q=QT)
        es = A0[:, 4096:6144].rearrange("p (q f) -> p q f", q=QT)
        ehT = A0[:, 6144:8192].rearrange("p (c t) -> p c t", c=FC)
        lg = A0[:, 8192:8224].rearrange("p (q e) -> p q e", q=QT)
        oh = A0[:, 8224:8256].rearrange("p (q e) -> p q e", q=QT)
        top = A0[:, 8256:8272].rearrange("p (k q) -> p k q", k=4)

        x_dram = a["x"].rearrange("b (q p) d -> p (b q) d", p=P)
        load("first", x_res[:, :, :], x_dram)
        load("first", ctx_sb[0:C, :, :], a["ctx"].rearrange("b c d -> c b d"))
        load("first", ctxT[:, :, :], a["ctxT"])
        load("first", condT[:, :], a["condT"])
        load("first", ident[:, :], a["ident"])
        load("first", rope[:, :, :], a["rope"].rearrange("p (q r) -> p q r", q=QT))
        load("first", mask_in[:, :], a["mask"])
        load("first", maskc_in[0:C, :], a["maskc"])
        load("first", vec[:, :], a["vec"])
        load("first", n1w_bc[:, :], a["n1w"].rearrange("(o n) -> o n", o=1).to_broadcast([P, D]))
        load("first", n2w_bc[:, :], a["n2w"].rearrange("(o n) -> o n", o=1).to_broadcast([P, DFF]))
        load("first", act_sb[:, :], a["actsb"].rearrange("(o n) -> o n", o=1).to_broadcast([P, 2]))
        load("first", nb[:, :], a["nb"])
        load("first", f1b[:, :], a["f1b"])
        load("first", f2b[:, :], a["f2b"])
        load("first", nT.rearrange("p j o -> p (j o)"), a["nT"])
        load("first", w1T, a["w1T"])
        load("first", w2T.rearrange("p c d -> p (c d)"), a["w2T"])

        for e in Program.ENGINES:
            loaded(e, "first")
        ones_t = dve(lambda e, v: e.memset(ones_sq[:, :], 1.0))
        dve(lambda e, v: e.memset(neg_half[:, :], -0.5))
        id16 = dve(lambda e, v: e.tensor_copy(ident16[:, :], ident[:, :]))
        t = dve(lambda e, v: e.tensor_reduce(small[0:6, 0:2, 0:1], ident[0:6, 0:6].rearrange("p (n k) -> p n k", n=2), AX.X, ALU.add))
        for n in range(2):
            dve(lambda e, v, n=n: e.tensor_scalar(sel[:, n, :], ones_sq[0:6, :], small[0:6, n, 0:1], None, ALU.mult),
                [t, ones_t])
        for raw, row, k in ((mask_in, mask_row, P), (maskc_in, maskc_row, C)):
            t = dve(lambda e, v, raw=raw, row=row, k=k: e.tensor_copy(row[0:k, :], raw[0:k, :]))
            dve(lambda e, v, row=row, k=k: e.tensor_scalar(row[0:k, :], row[0:k, :], -3.0e38, 3.0e38, ALU.mult, ALU.mult), [t])
        t0 = dve(lambda e, v: e.tensor_scalar(lat_b[:, :], condT[:, :], 1.0, None, ALU.add))
        t1 = dve(lambda e, v: e.tensor_scalar(lat_g[:, :], lat_b[:, :], vec[:, 2:3], None, ALU.mult), [t0])
        t2 = dve(lambda e, v: e.tensor_scalar(lat_b[:, :], lat_b[:, :], vec[:, 3:4], None, ALU.mult), [t1])
        dve(lambda e, v: e.tensor_tensor(lat_b[:, :], lat_b[:, :], condT[:, :], ALU.add), [t2])
        t0 = dve(lambda e, v: e.tensor_reduce(wsum[:, 0:1], w1T, AX.X, ALU.add, apply_absolute_value=True))
        t1 = dve(lambda e, v: e.tensor_reduce(wsum[:, 1:2], w2T, AX.XY, ALU.add, apply_absolute_value=True))
        t = pe(lambda e, v: e.matmul(psum[:, 0, 0:2], ones_sq[:, :], wsum[:, :], start=True, stop=True), [t0, t1, ones_t])
        t = dve(lambda e, v: e.tensor_scalar(wscale[:, :], psum[:, 0, 0:2], 1.0 / (D * DFF), 1e-5, ALU.mult, ALU.max), [t])
        t = dve(lambda e, v: e.reciprocal(wsum[:, :], wscale[:, :]), [t])
        for w, k, dst in ((w1T, 0, wq1[:, :]), (w2T, 1, wq2[:, :, :])):
            u = dve(lambda e, v, w=w, k=k: e.tensor_scalar(w, w, wsum[:, k:k + 1], MAGIC, ALU.mult, ALU.add), [t])
            u = dve(lambda e, v, w=w: e.tensor_scalar(w, w, -MAGIC, 1.0, ALU.add, ALU.min), [u])
            dve(lambda e, v, w=w, dst=dst: e.tensor_scalar(dst, w, -1.0, None, ALU.max), [u])
        for j in range(NL * 6):
            t = pe(lambda e, v, j=j: e.matmul(psum[:, 1, j * B:(j + 1) * B], nT[:, j, :], condT[:, :], start=True, stop=True))
        by_norm = gb[:, :].rearrange("p (w l b) -> p w l b", w=6, b=B)
        for h in range(6):
            t1 = dve(lambda e, v, h=h: e.tensor_tensor(
                by_norm[:, h, :, :], psum[:, 1, 0:NL * 6 * B].rearrange("p (l w b) -> p l w b", w=6, b=B)[:, :, h, :],
                nb[:, :].rearrange("p (l w) -> p l w", w=6)[:, :, h:h + 1].to_broadcast([P, NL, B]), ALU.add), [t])
        prep_end = dve(lambda e, v: e.tensor_scalar(gb[:, :].rearrange("p (w h c) -> p w h c", w=3, h=2)[:, :, 0, :],
                                                    gb[:, :].rearrange("p (w h c) -> p w h c", w=3, h=2)[:, :, 0, :],
                                                    1.0, None, ALU.add), [t1])

        pr.meet(phase=True)
        load("w0", A0[:, 0:4096], a["w0"], 1)
        load("wl", wl.rearrange("p l c -> p (l c)"), a["wl"])

        def norm(src, dst, n, parts, eps, after=(), keep=None):
            for q in range(n):
                t = dve(lambda e, v, q=q: e.bn_stats(stats[0:parts, q, :], src(v)[:, q, :]), after)
            for q in range(n):
                t1 = dve(lambda e, v, q=q: e.bn_aggr(mv[0:parts, q, :], stats[0:parts, q, :]), [t])
            t2 = dve(lambda e, v: e.tensor_scalar(ve[0:parts, 0:n], mv[0:parts, 0:n, 1], eps, None, ALU.add), [t1])
            t3 = pool(lambda e, v: e.tensor_tensor(rstd[0:parts, 0:n], ve[0:parts, 0:n], neg_half[0:parts, 0:n], ALU.pow), [t2])
            for q in range(n):
                t4 = dve(lambda e, v, q=q: e.tensor_scalar(dst[0:parts, q, :], src(v)[:, q, :], mv[0:parts, q, 0:1],
                                                           rstd[0:parts, q:q + 1], ALU.subtract, ALU.mult), [t3])
            return t4

        def transposes(b, src, n, after):
            for q in range(n):
                t = pe(lambda e, v, q=q: e.transpose(psum[:, b, q * P:(q + 1) * P], src[:, q, :], ident[:, :]),
                       after, count=q == n - 1)
            return t

        loaded("tensor", "w0")
        pr.begin("b0", B)
        tv = dve(lambda e, v: e.memset(v0[:, :, :, HD0:HD0 + 1], 1.0))
        xb = lambda v: x_res[:, bass.ds(v["b0"] * QT, QT), :]
        t = norm(xb, y, QT, P, 1e-5)
        t = norm(lambda v: y[:, :, :], z, QT, P, 1e-5, [t])
        t = transposes(0, z, QT, [t])
        t_lat = dve(lambda e, v: e.tensor_scalar(kvT[:, 0:S], bank(0), lat_g[:, bass.ds(v["b0"], 1)],
                                                 lat_b[:, bass.ds(v["b0"], 1)], ALU.mult, ALU.add), [t])
        t = norm(lambda v: ctx_sb[0:C, bass.ds(v["b0"], 1), :], zc[:, :].unsqueeze(1), 1, C, 1e-5, [t])
        t = pe(lambda e, v: e.transpose(psum[:, 1, 0:C], zc[0:C, :], ident[0:C, 0:C]), [t])
        t_ctx = dve(lambda e, v: e.tensor_scalar(kvT[:, S:KV], psum[:, 1, 0:C], vec[:, 0:1], vec[:, 1:2],
                                                 ALU.mult, ALU.add), [t])
        t_v = [None] * 4
        i = 0
        for k in range(KT0):
            rows = min(P, KV - k * P)
            for half in range(2):
                t = pe(lambda e, v, k=k, half=half, i=i, rows=rows: e.matmul(
                    psum[0:rows, 2 + i % 4, :], kvT[:, k * P:k * P + rows], wvT[:, half * 512:(half + 1) * 512],
                    start=True, stop=True), [t_lat, t_ctx, t_v[i % 4]])
                t_v[i % 4] = act(lambda e, v, k=k, half=half, i=i, rows=rows: e.activation(
                    v0[0:rows, k, half * 8:(half + 1) * 8, 0:HD0],
                    psum[0:rows, 2 + i % 4, :].rearrange("p (h d) -> p h d", h=8), ACT.Copy), [t])
                i += 1
        t_vlast = t_v[(i - 1) % 4]

        free = {i: t_vlast for i in range(8)}
        qk_free = [None, None]
        pt_free = [None, None]
        qk_ready = {}
        m_ready = {}

        def project(u):
            n = u % 2
            w = [t_lat, t_ctx, free[0]]
            t = pe(lambda e, v: e.matmul(bank(0), wqT[:, u * P:(u + 1) * P], kvT[:, 0:S], start=True, stop=True), w)
            free[0] = tq = act(lambda e, v: e.activation(q_pair[:, n, :], bank(0), ACT.Copy), [t, qk_free[n]])
            t = pe(lambda e, v: e.matmul(bank(1), wkT[:, u * P:(u + 1) * P], kvT[:, 0:S], start=True, stop=True), [free[1]])
            free[1] = act(lambda e, v: e.activation(k_pair[:, n, 0:S], bank(1), ACT.Copy), [t, qk_free[n]])
            t = pe(lambda e, v: e.matmul(psum[:, 0, 0:C], wkT[:, u * P:(u + 1) * P], kvT[:, S:KV], start=True, stop=True), [free[0]])
            free[0] = tk = act(lambda e, v: e.activation(k_pair[:, n, S:KV], psum[:, 0, 0:C], ACT.Copy), [t, qk_free[n]])
            qk_ready[u] = tk

        def maxima(u, j):
            n = u % 2
            lo = j * HD0
            for q in range(QT):
                w = [qk_ready[u], free[0], free[1]]
                pe(lambda e, v, q=q: e.matmul(bank(0), q_pair[lo:lo + HD0, n, q * P:(q + 1) * P],
                                              k_pair[lo:lo + HD0, n, 0:S], start=True, stop=True), w, count=False)
                t = pe(lambda e, v, q=q: e.matmul(psum[:, 1, 0:C], q_pair[lo:lo + HD0, n, q * P:(q + 1) * P],
                                                  k_pair[lo:lo + HD0, n, S:KV], start=True, stop=True))
                free[0] = free[1] = dve(lambda e, v, q=q: e.tensor_reduce(
                    nm0[:, j, q:q + 1], psum[:, 0:2, :].rearrange("p n t -> p (n t)")[:, 0:KV], AX.X, ALU.max, negate=True), [t])
            return free[0]

        def maxima_to_rows(u, t):
            n = u % 2
            src = nm0[:, :, :].rearrange("p n q -> p q n")
            rem = nm0r[:, :, :].rearrange("p n q -> p q n")
            t = dve(lambda e, v: e.tensor_copy(m3[:, :, :, 0], src), [t])
            t = dve(lambda e, v: e.tensor_tensor(rem, src, m3[:, :, :, 0], ALU.subtract), [t])
            t = dve(lambda e, v: e.tensor_copy(m3[:, :, :, 1], rem), [t])
            t = dve(lambda e, v: e.tensor_tensor(m3[:, :, :, 2], rem, m3[:, :, :, 1], ALU.subtract), [t])
            for q in range(QT):
                tt = pe(lambda e, v, q=q: e.transpose(bank16(7)[0:6, q * P:(q + 1) * P],
                                                      m3[:, q, :, :].rearrange("p n k -> p (n k)"), ident16[:, :]),
                        [t, free[7]], count=q == QT - 1)
            free[7] = m_ready[u] = dve(lambda e, v: e.tensor_copy(m3T[:, n, :], bank16(7)[0:6, 0:S]), [tt, qk_free[n]])

        st_i = [0]

        def attend(u, j):
            n, h, lo = u % 2, 2 * u + j, j * HD0
            buf = h % 2
            for k in range(KT0):
                rows = min(P, KV - k * P)
                b = 2 + st_i[0] % 4
                st_i[0] += 1
                pe(lambda e, v, k=k, b=b, rows=rows: e.matmul(psum[0:rows, b, :], k_pair[lo:lo + HD0, n, k * P:k * P + rows],
                                                              q_pair[lo:lo + HD0, n, :], start=True, stop=False),
                   [m_ready[u], free[b]], count=False)
                t = pe(lambda e, v, b=b, rows=rows: e.matmul(psum[0:rows, b, :], sel[:, j, 0:rows], m3T[:, n, :],
                                                             start=False, stop=True))
                free[b] = t_e = act(lambda e, v, k=k, b=b, rows=rows: e.activation(
                    p0[0:rows, buf, k, :], psum[0:rows, b, :], ACT.Exp, scale=HD0 ** -0.5), [t, pt_free[buf]])
            qk_free[n] = t
            return t_e

        def values(u, j, t_e):
            h = 2 * u + j
            buf = h % 2
            for q in range(QT):
                for k in range(KT0):
                    rows = min(P, KV - k * P)
                    t = pe(lambda e, v, q=q, k=k, rows=rows: e.matmul(
                        psum[:, 6, q * 65:(q + 1) * 65], p0[0:rows, buf, k, q * P:(q + 1) * P], v0[0:rows, k, h, :],
                        start=k == 0, stop=k == KT0 - 1), [t_e, free[6], tv, t_vlast], count=k == KT0 - 1)
            pt_free[buf] = t
            o = psum[:, 6, 0:QT * 65].rearrange("p (q d) -> p q d", q=QT)
            t1 = dve(lambda e, v: e.reciprocal(rd0[:, :].unsqueeze(2), o[:, :, HD0:HD0 + 1]), [t])
            free[6] = dve(lambda e, v: e.tensor_tensor(att0[:, :, h * HD0:(h + 1) * HD0], o[:, :, 0:HD0],
                                                       rd0[:, :].unsqueeze(2).to_broadcast([P, QT, HD0]), ALU.mult), [t1])

        def att_transposed(u, b):
            for q in range(QT):
                t = pe(lambda e, v, q=q: e.transpose(psum[:, b, q * P:(q + 1) * P], att0[:, q, u * P:(u + 1) * P], ident[:, :]),
                       [free[6], free[b]], count=q == QT - 1)
            free[b] = act(lambda e, v: e.activation(att0T[:, u, :], bank(b), ACT.Copy), [t])

        project(0)
        maxima(0, 0)
        maxima_to_rows(0, maxima(0, 1))
        for u in range(NP0):
            if u + 1 < NP0:
                project(u + 1)
            for j in range(2):
                t_e = attend(u, j)
                if u + 1 < NP0:
                    t_m = maxima(u + 1, j)
                values(u, j, t_e)
            if u + 1 < NP0:
                maxima_to_rows(u + 1, t_m)
            att_transposed(u, 7)
        for q in range(QT):
            for u in range(NP0):
                t = pe(lambda e, v, q=q, u=u: e.matmul(psum[:, 0, q * P:(q + 1) * P], att0T[:, u, q * P:(q + 1) * P],
                                                       woT[:, u, :], start=u == 0, stop=u == NP0 - 1),
                       [free[7], free[0]], count=u == NP0 - 1)
        dve(lambda e, v: e.tensor_tensor(xb(v), xb(v), bank(0).rearrange("p (q d) -> p q d", q=QT), ALU.add), [t])
        pr.end()

        pr.begin("b1", B)
        xb1 = lambda v: x_res[:, bass.ds(v["b1"] * QT, QT), :]

        def mean_square(src, t):
            for q in range(QT):
                t1 = dve(lambda e, v, q=q: e.bn_stats(stats[:, q, :], src[:, q, :]), [t])
            for q in range(QT):
                t2 = dve(lambda e, v, q=q: e.bn_aggr(mv[:, q, :], stats[:, q, :]), [t1])
            t = dve(lambda e, v: e.tensor_tensor(ve[:, :], mv[:, :, 0], mv[:, :, 0], ALU.mult), [t2])
            t = dve(lambda e, v: e.tensor_tensor(ve[:, :], ve[:, :], mv[:, :, 1], ALU.add), [t])
            t = dve(lambda e, v: e.tensor_scalar(ve[:, :], ve[:, :], 1e-8, None, ALU.add), [t])
            return pool(lambda e, v: e.tensor_tensor(rstd[:, :], ve[:, :], neg_half[:, :], ALU.pow), [t])

        def quantise(src, work, dst, w_bc, width, wcol, t):
            for q in range(QT):
                t1 = act(lambda e, v, q=q: e.activation(work[:, q, :], src[:, q, :], ACT.Copy, scale=rstd[:, q:q + 1]), [t])
            t = dve(lambda e, v: e.tensor_tensor(work, work, w_bc.unsqueeze(1).to_broadcast([P, QT, width]), ALU.mult), [t1])
            t = dve(lambda e, v: e.tensor_reduce(small[:, 0, :], work, AX.X, ALU.max, apply_absolute_value=True), [t])
            t = dve(lambda e, v: e.tensor_scalar(small[:, 0, :], small[:, 0, :], 1e-5, None, ALU.max), [t])
            t = dve(lambda e, v: e.reciprocal(small[:, 2, :], small[:, 0, :]), [t])
            t = dve(lambda e, v: e.tensor_scalar(small[:, 2, :], small[:, 2, :], 127.0, None, ALU.mult), [t])
            t1 = dve(lambda e, v: e.tensor_scalar(small[:, 1, :], small[:, 0, :], 1.0 / 127.0, wscale[:, wcol:wcol + 1],
                                                  ALU.mult, ALU.mult), [t])
            for q in range(QT):
                t = dve(lambda e, v, q=q: e.tensor_scalar(work[:, q, :], work[:, q, :], small[:, 2, q:q + 1], MAGIC,
                                                          ALU.mult, ALU.add), [t1])
            t = dve(lambda e, v: e.tensor_scalar(work, work, -MAGIC, 127.0, ALU.add, ALU.min), [t])
            return dve(lambda e, v: e.tensor_scalar(dst, work, -128.0, None, ALU.max), [t])

        t = norm(xb1, y, QT, P, 1e-5)
        t = mean_square(y, t)
        t = quantise(y[:, :, :], z[:, :, :], zq[:, :, :], n1w_bc[:, :], D, 0, t)
        for q in range(QT):
            t1 = pe(lambda e, v, q=q: e.transpose(bank16(0)[:, q * P:(q + 1) * P], zq[:, q, :], ident16[:, :]), [t],
                    count=q == QT - 1)
        t = act(lambda e, v: e.activation(zqT, bank16(0)[:, 0:S], ACT.Copy), [t1])
        for q in range(QT):
            t1 = pe(lambda e, v, q=q: e.matmul(bank(1 + q), zqT[:, q * P:(q + 1) * P], wq1[:, :], start=True, stop=True), [t])
            t2 = act(lambda e, v, q=q: e.activation(hh[:, q, :], bank(1 + q), ACT.Relu, scale=small[:, 1, q:q + 1]), [t1])
        t = act(lambda e, v: e.activation(hh, hh, ACT.Square), [t2])
        t = dve(lambda e, v: e.tensor_scalar(hh, hh, act_sb[:, 0:1], act_sb[:, 1:2], ALU.mult, ALU.add), [t])
        t = mean_square(hh, t)
        t = quantise(hh, hr, hq, n2w_bc[:, :], DFF, 1, t)
        for c in range(FC):
            for q in range(QT):
                t1 = pe(lambda e, v, q=q, c=c: e.transpose(bank16(6 + c // 2)[:, (c % 2) * S + q * P:(c % 2) * S + (q + 1) * P],
                                                           hq[:, q, c * P:(c + 1) * P], ident16[:, :]), [t],
                        count=q == QT - 1)
            if c % 2:
                t2 = act(lambda e, v, c=c: e.activation(hqT[:, c - 1:c + 1, :].rearrange("p c t -> p (c t)"),
                                                        bank16(6 + c // 2), ACT.Copy), [t1])
        for q in range(QT):
            for c in range(FC):
                t = pe(lambda e, v, q=q, c=c: e.matmul(psum[:, 0, q * P:(q + 1) * P], hqT[:, c, q * P:(q + 1) * P],
                                                       wq2[:, c, :], start=c == 0, stop=c == FC - 1), [t2], count=c == FC - 1)
        t = dve(lambda e, v: e.tensor_tensor(z[:, :, :], bank(0).rearrange("p (q d) -> p q d", q=QT),
                                             small[:, 1, :].unsqueeze(2).to_broadcast([P, QT, D]), ALU.mult), [t])
        t = dve(lambda e, v: e.tensor_tensor(xb1(v), xb1(v), z[:, :, :], ALU.add), [t])
        t_y = norm(xb1, y, QT, P, 1e-5, [t])
        dve(lambda e, v: e.tensor_copy(x_st[:, bass.ds(v["b1"] * QT, QT), :], y[:, :, :]),
            [t_y])
        pr.end()

        pr.meet()
        for e in Program.ENGINES:
            loaded(e, "wl")
        for w in (so, co):
            t = pool(lambda e, v, w=w: e.memset(w.gq_raw, 0.0))
            pool(lambda e, v, w=w: e.memset(w.gq.rearrange("p q h r -> p (q h) r")[:, :, MROW:MROW + 1], 1.0), [t])
            t = pool(lambda e, v, w=w: e.memset(w.gk_raw, 0.0))
            for j in range(2):
                lo = 2 * STACK * j + MROW + 1
                pool(lambda e, v, w=w, lo=lo: e.memset(w.gk.rearrange("p q u c -> p (q u) c")[:, :, lo:lo + 3], 1.0), [t])
            pool(lambda e, v, w=w: e.memset(w.v_raw, 1.0))
        pr.meet()

        bfree = {}
        last = {}
        count = {"max": 0, "exp": 0, "misc": 0}
        where_core = [0]

        def new_pass():
            bfree.clear()
            last.clear()
            where_core[0] = -1

        def bank_max():
            count["max"] += 1
            return count["max"] % 2

        def bank_exp():
            count["exp"] += 1
            return 2 + count["exp"] % 3

        def bank_misc():
            count["misc"] += 1
            return (5, 7)[count["misc"] % 2]

        def xs(e, v, back):
            return x_st[:, bass.ds(at(e, v, back, "batch") * QT, QT), :]

        def wcols(e, v, back, lo, n):
            return wl[:, bass.ds(at(e, v, back, "layer"), 1), lo:lo + n].rearrange("p o c -> p (o c)")

        def reads(*keys):
            got = []
            for k in keys:
                t = last.get(k)
                got += t if isinstance(t, list) else [t]
            return got

        def g_norm(w, which, back, after):
            y1 = w.rot[0].rearrange("p (q c) -> p q c", q=QT)
            for q in range(QT):
                t = dve(lambda e, v, q=q: e.bn_stats(w.stats[:, q, :], xs(e, v, back)[:, q, :]), after)
            for q in range(QT):
                t1 = dve(lambda e, v, q=q: e.bn_aggr(w.mv[:, q, :], w.stats[:, q, :]), [t])
            yield
            t2 = dve(lambda e, v: e.tensor_scalar(w.ve, w.mv[:, :, 1], 1e-5, None, ALU.add), [t1])
            t3 = pool(lambda e, v: e.tensor_tensor(w.rstd, w.ve, neg_half[:, :], ALU.pow), [t2])
            yield
            yield
            for q in range(QT):
                t4 = dve(lambda e, v, q=q: e.tensor_scalar(y1[:, q, :], xs(e, v, back)[:, q, :], w.mv[:, q, 0:1],
                                                           w.rstd[:, q:q + 1], ALU.subtract, ALU.mult),
                         [t3] + reads("hT", ("raw", id(w))))
            last["x read"] = t4
            yield
            yield
            b = bank_misc()
            for q in range(QT):
                t = pe(lambda e, v, q=q: e.transpose(psum[:, b, q * P:(q + 1) * P], y1[:, q, :], ident[:, :]),
                       [t4, bfree.get(b)], count=q == QT - 1)
            g = lambda e, v, half: gb[:, bass.ds((which * 2 + half) * NL * B + at(e, v, back, "step"), 1)]
            bfree[b] = act(lambda e, v: e.activation(w.xnT, bank(b), ACT.Identity, scale=g(e, v, 0), bias=g(e, v, 1)),
                           [t] + reads(("xnT", id(w))))
            last["xn", id(w)] = bfree[b]
            yield
            yield

        def g_rotate(w, k, rows):
            nq = w.kt_n if k else QT
            heads = lambda t: t[0:rows, :].rearrange("p (q h d) -> p q h d", q=nq, d=HD1)
            src, dst, tm = heads(w.qk[k]), heads(w.rot[k]), heads(w.tmp[k])
            tab = lambda lo, n: rope[0:rows, 0:nq, lo:lo + n].unsqueeze(2).to_broadcast([rows, nq, H1, n])
            half = HD1 // 2
            ready = [last["qk", id(w), k]]
            pool(lambda e, v: e.tensor_tensor(dst, src, tab(0, HD1), ALU.mult), ready)
            yield
            pool(lambda e, v: e.tensor_tensor(tm[:, :, :, 0:half], src[:, :, :, half:HD1], tab(HD1, half), ALU.mult))
            t = pool(lambda e, v: e.tensor_tensor(tm[:, :, :, half:HD1], src[:, :, :, 0:half], tab(HD1 + half, half), ALU.mult))
            yield
            last["rot", id(w), k] = pool(lambda e, v: e.tensor_tensor(w.rot[k][0:rows, :], w.rot[k][0:rows, :], w.tmp[k][0:rows, :], ALU.add), [t])
            yield

        def g_split(w, k, rows, pairs, after=()):
            slots = SLOT_K if k else SLOT_Q
            nq = w.kt_n if k else QT
            lo, n = pairs
            every = n == H1 // 2
            if k == 0:
                g = w.gq[0:rows].rearrange("p q (u j) r -> p q u j r", j=2)
            else:
                g = w.gk[0:rows].rearrange("p q u (j r) -> p q u j r", r=STACK)[:, :, :, 0:3:2, :]
            def slot(s):
                t = g[:, :, lo:lo + n, :, s * HD1:(s + 1) * HD1]
                return t.rearrange("p q u j d -> p (q u) j d") if every else t.rearrange("p q u j d -> p q (u j) d")
            def flat(t):
                t = t[0:rows, :].rearrange("p (q u j d) -> p q u j d", q=nq, j=2, d=HD1)[:, :, lo:lo + n]
                return t.rearrange("p q u j d -> p (q u) j d") if every else t.rearrange("p q u j d -> p q (u j) d")
            src, rem = flat(w.rot[k]), flat(w.tmp[k])
            where = [[s for s in range(len(slots)) if slots[s] == part] for part in range(3)]
            ends = []
            t1 = pool(lambda e, v: e.tensor_copy(slot(where[0][0]), src), [last["rot", id(w), k]] + list(after))
            yield
            t2 = pool(lambda e, v: e.tensor_tensor(rem, src, slot(where[0][0]), ALU.subtract), [t1])
            for s in where[0][1:]:
                ends.append(act(lambda e, v, s=s: e.activation(slot(s), slot(where[0][0]), ACT.Copy), [t1]))
            yield
            t3 = pool(lambda e, v: e.tensor_copy(slot(where[1][0]), rem), [t2])
            yield
            ends.append(pool(lambda e, v: e.tensor_tensor(slot(where[2][0]), rem, slot(where[1][0]), ALU.subtract), [t3]))
            for s in where[1][1:]:
                ends.append(act(lambda e, v, s=s: e.activation(slot(s), slot(where[1][0]), ACT.Copy), [t3]))
            last["split", id(w), k] = ends
            last["raw", id(w)] = ends[:]
            yield
            yield

        def stack_up(w, k, i, after, evac):
            if k == 0:
                block = lambda q, u: w.gq[:, q, 2 * u:2 * u + 2, :].rearrange("p h r -> p (h r)")
                dst = w.q_st
            else:
                block = lambda q, h: w.gk[:, q, h // 2, (h % 2) * STACK:(h % 2) * STACK + P]
                dst = w.k_st
            b = bank_misc()
            for n in range(2):
                for q in range(QT):
                    t = pe(lambda e, v, n=n, q=q: e.transpose(
                        bank16(b)[:, n * S + q * P:n * S + (q + 1) * P], block(q, i + n), ident16[:, :]),
                        after + [bfree.get(b)], count=n == 1 and q == QT - 1)
            to = dst[:, i:i + 2, :].rearrange("p u t -> p (u t)")
            if evac == "act":
                bfree[b] = act(lambda e, v: e.activation(to, bank16(b), ACT.Copy), [t] + after)
            else:
                bfree[b] = dve(lambda e, v: e.tensor_copy(to, bank16(b)), [t] + after)
            last["stack", id(w), k, i // 2] = bfree[b]
            last["stacked", id(w), k] = t
            return bfree[b]

        def g_mask(w, rows, src):
            ends = []
            for j in range(2):
                ends.append(dve(lambda e, v, j=j: e.tensor_copy(w.gk[0:rows, :, :, 2 * STACK * j + MROW],
                                                                src(e, v).unsqueeze(2).to_broadcast([rows, w.kt_n, H1 // 2])),
                                reads(("stacked", id(w), 1))))
            last["mask", id(w)] = ends
            yield

        def clear_shift(w, lo, n):
            last["cleared", id(w), lo] = pool(
                lambda e, v: e.memset(w.gq[:, :, lo:lo + n, MROW + 1:MROW + 4], 0.0),
                reads(("shift", id(w)), ("shift up", id(w))))

        def g_self_a(back):
            w = so
            yield from g_norm(w, 0, back, [])
            for i in range(2):
                b = bank_misc()
                for q in range(2 * i, 2 * i + 2):
                    t = pe(lambda e, v, q=q, b=b: e.matmul(psum[:, b, (q % 2) * 256:(q % 2) * 256 + 256], w.xnT[:, q * P:(q + 1) * P],
                                                           wcols(e, v, back, W_QKV, 256), start=True, stop=True),
                           [last["xn", id(w)], bfree.get(b)])
                for k in range(2):
                    bfree[b] = act(lambda e, v, i=i, k=k, b=b: e.activation(
                        w.qk[k].rearrange("p (q c) -> p q c", q=QT)[:, 2 * i:2 * i + 2, :],
                        bank(b).rearrange("p (q k c) -> p q k c", q=2, k=2)[:, :, k, :], ACT.Copy), [t] + reads("hT"))
                    last["qk", id(w), k] = bfree[b]
                yield
            yield from g_rotate(w, 1, P)
            yield from g_rotate(w, 0, P)

        def core_at(g):
            while where_core[0] < g:
                yield

        def g_self_b(back):
            w = so
            yield from g_mask(w, P, lambda e, v: mask_row[:, bass.ds(at(e, v, back, "batch") * QT, QT)])
            yield from g_split(w, 1, P, (0, H1 // 2), reads(("stacked", id(w), 1)))
            k_ready = reads(("split", id(w), 1), ("mask", id(w)))
            yield from core_at(1)
            clear_shift(w, 0, H1 // 2)
            yield from g_split(w, 0, P, (0, H1 // 4), reads(("shift up", id(w))))
            for i in (0, 2):
                stack_up(w, 0, i, reads(("split", id(w), 0), ("cleared", id(w), 0), "q read"), "dve")
                yield
            for i in (0, 2):
                stack_up(w, 1, i, k_ready + reads(("k read", 0)), "act")
                yield
            yield from core_at(2)
            for i in (4, 6):
                stack_up(w, 1, i, k_ready + reads(("k read", 1)), "act")
                yield
            yield from core_at(3)
            clear_shift(w, H1 // 2, H1 // 2)
            yield from g_split(w, 0, P, (H1 // 4, H1 // 4), reads(("shift up", id(w))))
            for i in (8, 10):
                stack_up(w, 1, i, k_ready + reads(("k read", 2)), "act")
                yield
            for i in (4, 6):
                stack_up(w, 0, i, reads(("split", id(w), 0), ("cleared", id(w), H1 // 2), "q read"), "dve")
                yield

        def values_of(w, back):
            b = bank_misc()
            for q in range(QT):
                t = pe(lambda e, v, q=q: e.matmul(psum[:, b, q * P:(q + 1) * P], w.xnT[:, q * P:(q + 1) * P],
                                                  wcols(e, v, back, W_QKV + 256, D), start=True, stop=True), [bfree.get(b)])
            last["xnT", id(w)] = t
            for q in range(QT):
                bfree[b] = act(lambda e, v, q=q: e.activation(
                    w.v[:, q, 0:H1 * (HD1 + 1)].rearrange("p (h d) -> p h d", d=HD1 + 1)[:, :, 0:HD1],
                    psum[:, b, q * P:(q + 1) * P].rearrange("p (h d) -> p h d", d=HD1), ACT.Copy), [t])
            last["v", id(w)] = bfree[b]

        def g_start():
            values_of(so, 0)
            yield
            yield
            for i in (12, 14):
                stack_up(so, 1, i, [], "act")
                yield

        def g_cross(back):
            w = co
            t_cb = pool(lambda e, v: e.tensor_copy(ctx_b[:, 0:C], ctxT[:, bass.ds(at(e, v, back, "batch"), 1), :].rearrange("p o c -> p (o c)")))
            clear_shift(w, 0, H1)
            yield from g_norm(w, 1, back, reads("x"))
            b0 = bank_misc()
            t = pe(lambda e, v: e.matmul(psum[0:C, b0, 0:256], ctx_b[:, 0:C], wcols(e, v, back, W_CKV, 256), start=True, stop=True),
                   [t_cb, bfree.get(b0)])
            last["qk", id(w), 1] = act(lambda e, v: e.activation(w.qk[1][0:C, :], psum[0:C, b0, 0:P], ACT.Copy), [t])
            bfree[b0] = act(lambda e, v: e.activation(
                w.v[0:C, 0, 0:H1 * (HD1 + 1)].rearrange("p (h d) -> p h d", d=HD1 + 1)[:, :, 0:HD1],
                psum[0:C, b0, P:2 * P].rearrange("p (h d) -> p h d", d=HD1), ACT.Copy), [t])
            last["v", id(w)] = bfree[b0]
            b1 = bank_misc()
            for q in range(QT):
                t = pe(lambda e, v, q=q: e.matmul(psum[:, b1, q * P:(q + 1) * P], w.xnT[:, q * P:(q + 1) * P],
                                                  wcols(e, v, back, W_CQ, D), start=True, stop=True), [last["xn", id(w)], bfree.get(b1)])
            last["qk", id(w), 0] = bfree[b1] = act(lambda e, v: e.activation(w.qk[0], bank(b1), ACT.Copy), [t])
            yield
            yield from g_rotate(w, 0, P)
            yield from g_mask(w, C, lambda e, v: maskc_row[0:C, bass.ds(at(e, v, back, "batch"), 1)])
            yield from g_split(w, 0, P, (0, H1 // 2))
            yield from g_rotate(w, 1, C)
            for i in (0, 2, 4, 6):
                stack_up(w, 0, i, reads(("split", id(w), 0), ("cleared", id(w), 0)), "dve")
                yield
            yield from g_split(w, 1, C, (0, H1 // 2))
            for n in range(2):
                b = bank_misc()
                for i in range(8):
                    h = 8 * n + i
                    t = pe(lambda e, v, h=h, i=i, b=b: e.transpose(bank16(b)[:, i * P:i * P + C],
                                                                   w.gk[0:C, 0, h // 2, (h % 2) * STACK:(h % 2) * STACK + P],
                                                                   ident16[0:C, 0:C]),
                           reads(("split", id(w), 1), ("mask", id(w))) + [bfree.get(b)], count=i == 7)
                bfree[b] = act(lambda e, v, n=n, b=b: e.activation(
                    w.k_st[:, 8 * n:8 * n + 8, 0:C], bank16(b).rearrange("p (u c) -> p u c", u=8)[:, :, 0:C], ACT.Copy), [t])
                last["k stacks", n] = bfree[b]
                yield

        def g_project(w, wcol, back):
            b = bank_misc()
            for q in range(QT):
                t = pe(lambda e, v, q=q: e.transpose(psum[:, b, q * P:(q + 1) * P], w.att[:, q, :], ident[:, :]),
                       reads(("att ready", id(w))) + [bfree.get(b)], count=q == QT - 1)
            last["att", id(w)] = t
            bfree[b] = t = act(lambda e, v: e.activation(attT, bank(b), ACT.Copy), [t] + reads("attT"))
            yield
            yield
            b1 = bank_misc()
            for q in range(QT):
                t1 = pe(lambda e, v, q=q: e.matmul(psum[:, b1, q * P:(q + 1) * P], attT[:, q * P:(q + 1) * P],
                                                   wcols(e, v, back, wcol, D), start=True, stop=True), [t, bfree.get(b1)])
            last["attT"] = t1
            bfree[b1] = dve(lambda e, v: e.tensor_tensor(xs(e, v, back), xs(e, v, back), bank(b1).rearrange("p (q d) -> p q d", q=QT),
                                                         ALU.add), [t1] + reads("x read"))
            last["x"] = bfree[b1]
            yield
            yield

        def g_ffn(back):
            w = so
            t_f1 = pool(lambda e, v: e.tensor_copy(f1s, wcols(e, v, back, W_F1, DFF)))
            yield from g_norm(w, 2, back, [])
            for c in range(FC):
                b = bank_misc()
                t = pe(lambda e, v, c=c, b=b: e.matmul(bank(b), f1s[:, c * P:(c + 1) * P], w.xnT, start=True, stop=True),
                       [last["xn", id(w)], t_f1, bfree.get(b)])
                last["xnT", id(w)] = t
                bfree[b] = t2 = act(lambda e, v, c=c, b=b: e.activation(hT[:, c, :], bank(b), ACT.Gelu,
                                                                        bias=f1b[:, bass.ds(at(e, v, back, "layer") * FC + c, 1)]), [t])
            yield
            yield
            b = bank_misc()
            for q in range(QT):
                for c in range(FC):
                    pe(lambda e, v, q=q, c=c: e.matmul(psum[:, b, q * P:(q + 1) * P], hT[:, c, q * P:(q + 1) * P],
                                                       wcols(e, v, back, W_F2 + c * D, D), start=c == 0, stop=False),
                       [t2, bfree.get(b)], count=False)
                t = pe(lambda e, v, q=q: e.matmul(psum[:, b, q * P:(q + 1) * P], ones_sq[0:1, :],
                                                  f2b[0:1, bass.ds(at(e, v, back, "layer") * D, D)], start=False, stop=True))
            last["hT"] = t
            bfree[b] = dve(lambda e, v: e.tensor_tensor(
                xs(e, v, back), xs(e, v, back), bank(b).rearrange("p (q d) -> p q d", q=QT), ALU.add), [t] + reads("x read"))
            yield

        def max_step(g, i):
            w = so
            j, q = divmod(i, QT)
            h = GROUP * g + j
            b = bank_max()
            t = pe(lambda e, v: e.matmul(bank(b), w.q_st[:, h // 2, q * P:(q + 1) * P], w.k_st[:, h, 0:S], start=True, stop=True),
                   reads(("stack", id(w), 0, h // 4), ("stack", id(w), 1, h // 2)) + [bfree.get(b)])
            bfree[b] = dve(lambda e, v: e.tensor_reduce(w.nm[:, g, q, j:j + 1], bank(b), AX.X, ALU.max, negate=True), [t])
            last["q read"] = t
            return bfree[b]

        def shift(w, lo, n, t):
            heads = w.gq[:, :, lo:lo + n, :].rearrange("p q (g j) r -> p g q j r", j=GROUP)
            g0, g1 = lo // GROUP, (lo + n) // GROUP
            same = g1 - g0 == 1
            col = lambda c: heads[:, 0, :, :, MROW + 1 + c] if same else heads[:, :, :, :, MROW + 1 + c]
            nm = w.nm[:, g0, :, :] if same else w.nm
            nmr = w.nmr[:, g0, :, :] if same else w.nmr
            t = pool(lambda e, v: e.tensor_copy(col(0), nm), [t])
            t = pool(lambda e, v: e.tensor_tensor(nmr, nm, col(0), ALU.subtract), [t])
            t = pool(lambda e, v: e.tensor_copy(col(1), nmr), [t])
            last["shift", id(w)] = pool(lambda e, v: e.tensor_tensor(col(2), nmr, col(1), ALU.subtract), [t])

        def shift_up(g):
            w = so
            b = bank_misc()
            for n in range(2):
                for q in range(QT):
                    t1 = pe(lambda e, v, n=n, q=q: e.transpose(
                        bank16(b)[:, n * S + q * P:n * S + (q + 1) * P],
                        w.gq[:, q, 4 * g + 2 * n:4 * g + 2 * n + 2, :].rearrange("p h r -> p (h r)"), ident16[:, :]),
                        reads(("shift", id(w))) + [bfree.get(b)], count=n == 1 and q == QT - 1)
            last["shift up", id(w)] = t1
            s = g % 2
            last["q_m ready", s] = bfree[b] = dve(lambda e, v: e.tensor_copy(
                q_m[:, s, :, :].rearrange("p u t -> p (u t)"), bank16(b)), [t1] + reads(("q_m", s)))

        def exp_step(w, h, k, buf, queries, after):
            rows = P if w.kt_n > 1 else C
            j = h % GROUP
            b = bank_exp()
            t = pe(lambda e, v: e.matmul(psum[0:rows, b, :], w.k_st[:, h, k * P:k * P + rows], queries, start=True, stop=True),
                   after + [bfree.get(b)])
            last["pT ready", id(w), buf] = bfree[b] = act(
                lambda e, v: e.activation(w.pT[0:rows, buf, j, :], psum[0:rows, b, :], ACT.Exp, scale=HD1 ** -0.5),
                [t] + reads(("pT", id(w), buf)))
            return t

        def weighted(w, g, k, buf, b):
            rows = P if w.kt_n > 1 else C
            for j in range(GROUP):
                lo = (GROUP * g + j) * (HD1 + 1)
                t1 = pe(lambda e, v, j=j, lo=lo: e.matmul(psum[32 * j:32 * j + 32, b, :], w.v[0:rows, k, lo:lo + 32],
                                                          w.pT[0:rows, buf, j, :], start=k == 0, stop=k == w.kt_n - 1),
                        reads(("pT ready", id(w), buf), ("v", id(w))) + [bfree.get(b)], count=j == GROUP - 1)
            last["pT", id(w), buf] = t1
            last["sum", id(w)] = t1

        def finish_a(w, b):
            bfree[b] = last["o", id(w)] = act(lambda e, v: e.activation(w.o, bank(b), ACT.Copy),
                                              reads(("sum", id(w)), ("o free", id(w))))

        def finish_b(w, g):
            b = bank_misc()
            for q in range(QT):
                t1 = pe(lambda e, v, q=q: e.transpose(psum[:, b, q * P:(q + 1) * P], w.o[:, q * P:(q + 1) * P], ident[:, :]),
                        reads(("o", id(w))) + [bfree.get(b)], count=q == QT - 1)
            last["o free", id(w)] = t1
            o = bank(b).rearrange("p (q j d) -> p q j d", q=QT, j=GROUP)
            t2 = dve(lambda e, v: e.reciprocal(w.rd[:, g, :, :], o[:, :, :, HD1]), [t1])
            n = GROUP * HD1
            last["att ready", id(w)] = bfree[b] = dve(lambda e, v: e.tensor_tensor(
                w.att[:, :, g * n:(g + 1) * n].rearrange("p q (j d) -> p q j d", d=HD1), o[:, :, :, 0:HD1],
                w.rd[:, g, :, :].unsqueeze(3).to_broadcast([P, QT, GROUP, HD1]), ALU.mult), [t2] + reads(("att", id(w))))

        MAX_STEPS = 12

        def g_core(has_next):
            w = so
            pend = None
            for g in range(NG):
                where_core[0] = g
                nxt = (g + 1) % NG
                more = g + 1 < NG or has_next
                i = 0
                for k in range(w.kt_n):
                    for j in range(GROUP):
                        n = GROUP * k + j
                        t = exp_step(w, GROUP * g + j, k, k % 2, q_m[:, g % 2, j // 2, :],
                                     reads(("q_m ready", g % 2), ("stack", id(w), 1, (GROUP * g + j) // 2)))
                        last["k read", g] = last["q_m", g % 2] = t
                        while more and i < min(GROUP * QT, GROUP * QT * (n + 1) // MAX_STEPS):
                            t_m = max_step(nxt, i)
                            i += 1
                        if j == 1 and pend is not None:
                            weighted(w, *pend, 6)
                            if pend[1] == w.kt_n - 1:
                                finish_a(w, 6)
                            pend = None
                        if j == 0 and k == 1 and g > 0:
                            finish_b(w, g - 1)
                        if more and n == MAX_STEPS:
                            shift(w, GROUP * nxt, GROUP, t_m)
                        if more and n == MAX_STEPS + 2:
                            shift_up(nxt)
                        yield
                    pend = (g, k, k % 2)
            weighted(w, *pend, 6)
            finish_a(w, 6)
            yield

        def g_cross_core():
            w = co
            for h in range(H1):
                b = bank_max()
                for q in range(QT):
                    t = pe(lambda e, v, q=q, h=h, b=b: e.matmul(
                        psum[:, b, q * P:q * P + C], w.q_st[:, h // 2, q * P:(q + 1) * P], w.k_st[:, h, 0:C], start=True, stop=True),
                        reads(("stack", id(w), 0, h // 4), ("k stacks", h // 8)) + [bfree.get(b)], count=q == QT - 1)
                t_m = bfree[b] = dve(lambda e, v, h=h, b=b: e.tensor_reduce(
                    w.nm[:, h // GROUP, :, h % GROUP:h % GROUP + 1], bank(b).rearrange("p (q k) -> p q k", q=QT)[:, :, 0:C],
                    AX.X, ALU.max, negate=True), [t])
                if h % 2:
                    yield
            for g in range(NG):
                shift(w, GROUP * g, GROUP, t_m)
            yield
            yield
            for i in (0, 2, 4, 6):
                stack_up(w, 0, i, reads(("shift", id(w))) + [t], "dve")
                yield
            for g in range(NG):
                for j in range(GROUP):
                    h = GROUP * g + j
                    exp_step(w, h, 0, 0, w.q_st[:, h // 2, :], reads(("stack", id(w), 0, h // 4)))
                    if j % 2:
                        yield
                if g:
                    finish_b(w, g - 1)
                b = bank_misc()
                weighted(w, g, 0, 0, b)
                finish_a(w, b)
                yield
            yield
            finish_b(w, NG - 1)
            yield

        def g_then(*makes):
            for make in makes:
                yield from make()

        def step(has_prev, has_ffn, has_next, is_step=True):
            new_pass()
            one, two = [], []
            if is_step:
                two.append(g_start)
            if has_prev:
                def end_self():
                    finish_b(so, NG - 1)
                    yield
                    yield
                one += [end_self, lambda: g_project(so, W_SO, 1), lambda: g_cross(1), g_cross_core, lambda: g_project(co, W_CO, 1)]
            if has_ffn:
                two.append(lambda: g_ffn(2))
            if has_next:
                two += [lambda: g_self_a(-1), lambda: g_self_b(-1)]
            run_beside(g_core(has_next) if is_step else iter(()), g_then(*one), g_then(*two))

        def at_step(n):
            for e in Program.ENGINES:
                pr.stack[e][-1].append(("set", "n", n))

        steps = NL * B
        at_step(-1)
        new_pass()
        where_core[0] = NG
        run_beside(g_then(lambda: g_self_a(-1), lambda: g_self_b(-1)))
        for i in range(GROUP * QT):
            t_m = max_step(0, i)
        shift(so, 0, GROUP, t_m)
        shift_up(0)
        pr.meet()
        for n in range(2):
            at_step(n)
            step(n > 0, False, True)
            pr.meet()
        pr.begin("n", steps - 3, 2)
        step(True, True, True)
        pr.end()
        at_step(steps - 1)
        step(True, True, False)
        pr.meet()
        at_step(steps)
        step(True, True, False, is_step=False)
        pr.meet()
        at_step(steps + 1)
        step(False, True, False, is_step=False)
        pr.meet(phase=True)

        load("wm", A1[:, 0:1552], a["wm"], 2)
        for e in ("tensor", "vector"):
            loaded(e, "wm")
        pr.begin("m", B)
        xm = lambda v: x_res[:, bass.ds(v["m"] * QT, QT), :]
        t = dve(lambda e, v: e.tensor_tensor(xm(v), xm(v), x_st[:, bass.ds(v["m"] * QT, QT), :], ALU.add))
        t = norm(xm, y, QT, P, 1e-5, [t])
        t = transposes(7, y, QT, [t])
        t = act(lambda e, v: e.activation(xnT[:, 0:S], bank(7), ACT.Copy), [t])
        for q in range(QT):
            t1 = pe(lambda e, v, q=q: e.matmul(psum[:, 0, q * E:(q + 1) * E], xnT[:, q * P:(q + 1) * P], gateT, start=True, stop=True), [t])
        lgv = psum[:, 0, 0:QT * E].rearrange("p (q e) -> p q e", q=QT)
        t = dve(lambda e, v: e.tensor_copy(lg, lgv), [t1])
        t = dve(lambda e, v: e.tensor_reduce(top[:, 0, :], lg, AX.X, ALU.max), [t])
        t_rw = act(lambda e, v: e.activation(top[:, 1, :], top[:, 0, :], ACT.Sigmoid), [t])
        t = dve(lambda e, v: e.tensor_tensor(oh, lg, top[:, 0, :].unsqueeze(2).to_broadcast([P, QT, E]), ALU.is_equal), [t])
        t = dve(lambda e, v: e.tensor_tensor(oh, oh, rank.unsqueeze(1).to_broadcast([P, QT, E]), ALU.mult), [t])
        t = dve(lambda e, v: e.tensor_reduce(top[:, 2, :], oh, AX.X, ALU.max), [t])
        t_oh = dve(lambda e, v: e.tensor_tensor(oh, oh, top[:, 2, :].unsqueeze(2).to_broadcast([P, QT, E]), ALU.is_equal), [t])
        t2 = None
        gates, ups = [], []
        for q in range(QT):
            t1 = pe(lambda e, v, q=q: e.matmul(bank(1 + q % 2), xnT[:, q * P:(q + 1) * P], wgT, start=True, stop=True),
                    [ups[q - 2]] if q >= 2 else [])
            gates.append(act(lambda e, v, q=q: e.activation(eg[:, q, :], bank(1 + q % 2), ACT.Copy, scale=top[:, 1, q:q + 1]), [t1, t_rw]))
            t1 = pe(lambda e, v, q=q: e.matmul(bank(3 + q % 2), xnT[:, q * P:(q + 1) * P], wuT, start=True, stop=True),
                    [ups[q - 2]] if q >= 2 else [])
            ups.append(act(lambda e, v, q=q: e.activation(eu[:, q, :], bank(3 + q % 2), ACT.Copy, scale=top[:, 1, q:q + 1]), [t1]))
        t = act(lambda e, v: e.activation(es, eg, ACT.Sigmoid), [ups[-1]])
        t1 = dve(lambda e, v: e.tensor_tensor(eu, eu, eg, ALU.mult), [ups[-1]])
        t1 = dve(lambda e, v: e.tensor_tensor(eu, eu, es, ALU.mult), [t, t1])
        for q in range(QT):
            t = dve(lambda e, v, q=q: e.tensor_tensor(es[:, q, :].rearrange("p (e i) -> p e i", e=E), eu[:, q, :].rearrange("p (e i) -> p e i", e=E),
                                                      oh[:, q, :].unsqueeze(2).to_broadcast([P, E, I]), ALU.mult), [t1, t_oh])
        for c in range(FC):
            for q in range(QT):
                t1 = pe(lambda e, v, q=q, c=c: e.transpose(psum[:, 3 + c, q * P:(q + 1) * P], es[:, q, c * P:(c + 1) * P], ident[:, :]),
                        [t], count=q == QT - 1)
            t2 = act(lambda e, v, c=c: e.activation(ehT[:, c, :], bank(3 + c), ACT.Copy), [t1])
        for q in range(QT):
            for c in range(FC):
                t = pe(lambda e, v, q=q, c=c: e.matmul(psum[:, 0, q * P:(q + 1) * P], ehT[:, c, q * P:(q + 1) * P], wdT[:, c, :],
                                                       start=c == 0, stop=c == FC - 1), [t2, t_oh], count=c == FC - 1)
        dve(lambda e, v: e.tensor_tensor(xm(v), xm(v), bank(0).rearrange("p (q d) -> p q d", q=QT), ALU.add), [t])
        pr.end()
        pr.meet(phase=True)

        block = ctx.enter_context(nc.Block())

        @block.sync
        def _(eng):
            for s, dst, src, after in dma_list:
                if after:
                    eng.wait_ge(phase, after)
                eng.dma_start(dst, src).then_inc(s, 16)
            eng.wait_ge(phase, 3)
            eng.dma_start(out.rearrange("b (q p) d -> p (b q) d", p=P), x_res[:, :, :]).then_inc(s_out, 16)
            eng.wait_ge(s_out, 16)

        @block.tensor
        def _(eng):
            pr.emit("tensor", eng, (done, arrived, go, phase))

        @block.vector
        def _(eng):
            pr.emit("vector", eng, (done, arrived, go, phase))

        @block.scalar
        def _(eng):
            pr.emit("scalar", eng, (done, arrived, go, phase))

        @block.gpsimd
        def _(eng):
            pr.emit("gpsimd", eng, (done, arrived, go, phase))


def kernel(**inputs):
    import concourse.bacc as _bacc
    from concourse.bass_utils import run_bass_kernel_spmd as _run

    g = {k: np.asarray(v) for k, v in inputs.items()}
    c = np.ascontiguousarray

    def cols(*parts):
        return c(np.concatenate([p.reshape(P, -1) for p in parts], axis=1))

    def chunks(w):
        return w.reshape(-1, P, w.shape[-1]).transpose(1, 0, 2).reshape(P, -1)

    def words(m):
        wide = np.zeros(m.shape + (4,), m.dtype)
        wide[..., 0] = m
        return wide.view(np.int32)[..., 0].copy()

    L = "L1_xcond_"
    layer = [cols(g[L + "qkv_w"][l].T, g[L + "so_w"][l].T, g[L + "cq_w"][l].T, g[L + "ck_w"][l].T, g[L + "cv_w"][l].T,
                  g[L + "co_w"][l].T, g[L + "f1_w"][l].T, chunks(g[L + "f2_w"][l].T)) for l in range(NL)]
    norms_w = np.stack([g[L + f"n{n}_w"] for n in (1, 2, 3)], axis=1).reshape(NL * 6, D, D)
    norms_b = np.stack([g[L + f"n{n}_b"] for n in (1, 2, 3)], axis=1).reshape(NL * 6, D)
    wkv = g["L0_xcond_Wkv"]
    arrays = {
        "x": c(g["x"]),
        "ctx": c(g["ctx_1024"]),
        "ctxT": c(g["ctx_1024"].transpose(2, 0, 1)),
        "condT": c(g["cond_1024"].T),
        "ident": np.eye(P, dtype=np.float32),
        "rope": rope_tables(),
        "mask": words(g["mask_BxS_bf0"].reshape(B * QT, P).T),
        "maskc": words(g["mask_BxS2_bf0"].T),
        "vec": c(np.stack([g["L0_xcond_ln1_w"], g["L0_xcond_ln1_b"], g["L0_xcond_ln2_w"], g["L0_xcond_ln2_b"]], axis=1)),
        "n1w": c(g["L0_ffn_norm1_w"]),
        "n2w": c(g["L0_ffn_norm2_w"]),
        "actsb": c(np.concatenate([g["L0_ffn_act_scale"], g["L0_ffn_act_bias"]])),
        "nb": c(norms_b.T),
        "f1b": c(g[L + "f1_b"].reshape(NL * FC, P).T),
        "f2b": c(g[L + "f2_b"].reshape(1, NL * D)),
        "nT": cols(norms_w.transpose(2, 0, 1)),
        "w1T": c(g["L0_ffn_w1"].T),
        "w2T": c(chunks(g["L0_ffn_w2"].T)),
        "w0": cols(g["L0_xcond_Wq"].T, wkv[:INNER].T, wkv[INNER:].T, chunks(g["L0_xcond_Wo"].T)),
        "wl": cols(*layer),
        "wm": cols(g["L1_ffn_w_gate"].reshape(E * I, D).T, g["L1_ffn_w_up"].reshape(E * I, D).T,
                   chunks(g["L1_ffn_w_down"].transpose(0, 2, 1).reshape(E * I, D)), g["L1_ffn_gate_w"].T,
                   np.tile(np.arange(E, 0, -1, dtype=np.float32), (P, 1))),
        "rank": np.tile(np.arange(E, 0, -1, dtype=np.float32), (P, 1)),
    }
    nc = _bacc.Bacc("TRN2", target_bir_lowering=False, num_devices=1)
    aps, feed = {}, {}
    for name, v in arrays.items():
        aps[name] = nc.dram_tensor("in_" + name, v.shape, mybir.dt.from_np(v.dtype), kind="ExternalInput").ap()
        feed["in_" + name] = v
    out = nc.dram_tensor("out_0", (B, S, D), fp32, kind="ExternalOutput").ap()
    build(nc, aps, out)
    r = _run(nc, [feed], core_ids=[0])
    return r.results[0]["out_0"]
```

```python
import numpy as np
import concourse.bass as bass
from concourse import mybir
from concourse.alu_op_type import AluOpType as ALU
from contextlib import ExitStack

fp32 = mybir.dt.float32
bf16 = mybir.dt.bfloat16
ACT = mybir.ActivationFunctionType
AX = mybir.AxisListType

B, S, D = 4, 512, 128
P = 128
QT = S // P
C = 77
H0, HD0 = 16, 64
INNER = H0 * HD0
NP0 = INNER // P
KV = S + C
KT0 = (KV + P - 1) // P
NL, H1, HD1 = 6, 16, 8
DFF = 512
FC = DFF // P
E, I = 8, 64
V_COLS = 168
GROUP = 4
NG = H1 // GROUP
SLOT_Q = (0, 0, 0, 1, 1, 2)
SLOT_K = (0, 1, 2, 0, 1, 0)
MROW = len(SLOT_Q) * HD1
STACK = 64
MAGIC = 1.5 * 2.0 ** 23

A_WORDS = 34440
W_QKV, W_SO, W_CQ, W_CKV, W_CO, W_F1, W_F2, W_COLS = 0, 384, 512, 640, 896, 1024, 1536, 2048


class Program:

    ENGINES = ("tensor", "vector", "scalar", "gpsimd")

    def __init__(self):
        self.n = {e: 0 for e in self.ENGINES}
        self.segment = 0
        self.stack = {e: [[]] for e in self.ENGINES}

    def add(self, engine, fn, after=(), count=True):
        self.stack[engine][-1].append(("do", fn, [t for t in after if t is not None], count, self.segment))
        if not count:
            return None
        self.n[engine] += 1
        return (engine, self.n[engine], self.segment)

    def pe(self, fn, after=(), count=True):
        return self.add("tensor", fn, after, count)

    def dve(self, fn, after=()):
        return self.add("vector", fn, after)

    def act(self, fn, after=()):
        return self.add("scalar", fn, after)

    def pool(self, fn, after=()):
        return self.add("gpsimd", fn, after)

    def meet(self, phase=False):
        for e in self.ENGINES:
            self.stack[e][-1].append(("meet", dict(self.n), phase))
        self.n = {e: 0 for e in self.ENGINES}
        self.segment += 1

    def begin(self, name, times, first=0):
        self.meet()
        for e in self.ENGINES:
            body = []
            self.stack[e][-1].append(("loop", name, first, times, body))
            self.stack[e].append(body)

    def end(self):
        self.meet()
        for e in self.ENGINES:
            self.stack[e].pop()

    def emit(self, engine, handle, sems, queue=None, env=None):
        done, arrived, go, phase_sem = sems
        env = {} if env is None else env
        seen = {}
        for item in self.stack[engine][0] if queue is None else queue:
            if item[0] == "loop":
                _, name, first, times, body = item
                with handle.Fori(first, first + times) as i:
                    self.emit(engine, handle, sems, body, {name: i})
            elif item[0] == "set":
                env = {item[1]: item[2]}
            elif item[0] == "meet":
                _, counts, phase = item
                for e in self.ENGINES:
                    if counts[e] > seen.get(e, 0):
                        handle.wait_ge(done[e], counts[e])
                if engine == "gpsimd":
                    handle.wait_ge(arrived, len(self.ENGINES) - 1)
                    handle.sem_clear(arrived)
                    for e in self.ENGINES:
                        handle.sem_clear(done[e])
                    if phase:
                        handle.sem_inc(phase_sem, 1)
                    for e in self.ENGINES:
                        if e != engine:
                            handle.sem_inc(go[e], 1)
                else:
                    handle.sem_inc(arrived, 1)
                    handle.wait_ge(go[engine], 1)
                    handle.sem_clear(go[engine])
                seen = {}
            else:
                _, fn, after, count, segment = item
                need = {}
                for e, local, seg in after:
                    if seg == segment and local > seen.get(e, 0):
                        need[e] = max(need.get(e, 0), local)
                for e, local in need.items():
                    handle.wait_ge(done[e], local)
                    seen[e] = local
                ins = fn(handle, env)
                if count:
                    ins.then_inc(done[engine], 1)


def at(e, v, back, what):
    key = (back, what)
    if key not in v:
        n = v["n"] - back
        got = {"batch": lambda: n % B, "layer": lambda: n // B, "step": lambda: n}[what]()
        v[key] = got if isinstance(got, int) else e.snap(got)
    return v[key]


def run_beside(core, *others):
    live = list(others)
    for _ in core:
        for g in list(live):
            if next(g, "end") == "end":
                live.remove(g)
    while live:
        for g in list(live):
            if next(g, "end") == "end":
                live.remove(g)


def rope_tables():
    half = HD1 // 2
    inv = (1.0 / np.float32(10000.0) ** (np.arange(half, dtype=np.float32) / np.float32(half))).astype(np.float32)
    ang = np.arange(S, dtype=np.float32)[:, None] * inv
    cos, sin = np.cos(ang).astype(np.float32), np.sin(ang).astype(np.float32)
    table = np.concatenate([cos, cos, -sin, sin], axis=1)
    return np.ascontiguousarray(table.reshape(QT, P, 16).transpose(1, 0, 2)).reshape(P, QT * 16)


def build(nc, a, out):
    pr = Program()
    pe, dve, act, pool = pr.pe, pr.dve, pr.act, pr.pool
    ctx = ExitStack()
    with ctx:
        def sb(name, shape, dt=fp32):
            return ctx.enter_context(nc.sbuf_tensor(name, shape, dt))

        psum = ctx.enter_context(nc.psum_tensor("psum", [P, 8, 512], fp32))

        def bank(i, n=1):
            return psum[:, i:i + n, :] if n > 1 else psum[:, i, :]

        def bank16(i):
            return psum[:, i, :].bitcast(bf16)

        x_res = sb("x_res", [P, B * QT, D])
        x_st = sb("x_st", [P, B * QT, D])
        ctxT = sb("ctxT", [P, B, C])
        condT = sb("condT", [P, B])
        ident = sb("ident", [P, P])
        ident16 = sb("ident16", [P, P], bf16)
        rope = sb("rope", [P, QT, 16])
        ones_sq = sb("ones_sq", [P, P])
        neg_half = sb("neg_half", [P, QT])
        mask_in = sb("mask_in", [P, B * QT], mybir.dt.int32)
        maskc_in = sb("maskc_in", [P, B], mybir.dt.int32)
        mask_row = sb("mask_row", [P, B * QT])
        maskc_row = sb("maskc_row", [P, B])
        vec = sb("vec", [P, 4])
        lat_g = sb("lat_g", [P, B])
        lat_b = sb("lat_b", [P, B])
        act_sb = sb("act_sb", [P, 2])
        gb = sb("gb", [P, 6 * NL * B])
        nb = sb("nb", [P, NL * 6])
        f1b = sb("f1b", [P, NL * FC])
        f2b = sb("f2b", [1, NL * D])
        wscale = sb("wscale", [P, 2])
        A0 = sb("A0", [P, A_WORDS])
        A1 = sb("A1", [P, 12288])
        stats = sb("stats", [P, QT, 6])
        mv = sb("mv", [P, QT, 2])
        ve = sb("ve", [P, QT])
        rstd = sb("rstd", [P, QT])
        wsum = sb("wsum", [P, 2])
        small = sb("small", [P, 8, QT])

        def sem(name):
            return ctx.enter_context(nc.semaphore(name))

        done = {e: sem(f"done_{e}") for e in Program.ENGINES}
        go = {e: sem(f"go_{e}") for e in Program.ENGINES if e != "gpsimd"}
        arrived, phase = sem("arrived"), sem("phase")
        s_first, s_w0, s_wl, s_wm, s_out = sem("s_first"), sem("s_w0"), sem("s_wl"), sem("s_wm"), sem("s_out")

        loads = {"first": 0, "w0": 0, "wl": 0, "wm": 0}
        sems = {"first": s_first, "w0": s_w0, "wl": s_wl, "wm": s_wm}
        dma_list = []

        def load(group, dst, src, after=0):
            loads[group] += 16
            dma_list.append((sems[group], dst, src, after))

        def loaded(engine, group):
            pr.stack[engine][-1].append(("do", lambda e, v: e.wait_ge(sems[group], loads[group]), [], False, pr.segment))

        above = [25000]

        def tile(*shape, dt=fp32):
            n = int(np.prod(shape)) * (1 if dt == fp32 else 2) // (1 if dt == fp32 else 4)
            above[0] += n
            flat = A0[:, above[0] - n:above[0]]
            flat = flat if dt == fp32 else flat.bitcast(dt)
            return flat if len(shape) == 1 else flat.rearrange("p (a b) -> p a b", b=shape[-1])

        ctx_sb = tile(B, D)
        n1w_bc = tile(D)
        n2w_bc = tile(DFF)
        wq1 = tile(DFF, dt=bf16)
        wq2 = tile(FC, D, dt=bf16)
        y = tile(QT, D)
        z = tile(QT, D)
        zc = tile(D)
        zq = tile(QT, D, dt=bf16)
        xnT = tile(640)
        wqT = A0[:, 0:1024]
        wkT = A0[:, 1024:2048]
        wvT = A0[:, 2048:3072]
        woT = A0[:, 3072:4096].rearrange("p (u d) -> p u d", d=D)
        q_pair = A0[:, 4096:5120].rearrange("p (n t) -> p n t", n=2)
        k_pair = A0[:, 5120:6400].rearrange("p (n t) -> p n t", n=2)
        v0 = A0[:, 6400:6400 + KT0 * INNER].rearrange("p (k c) -> p k c", k=KT0)
        p0 = A0[:, 11520:11520 + 3 * 2 * S].rearrange("p (r j t) -> p r j t", r=3, j=2)
        c_sc = A0[:, 14592:14592 + 16 * C].rearrange("p (n j q t) -> p n j q t", n=2, j=2, q=QT)
        c_p = A0[:, 15824:15824 + 16 * C].rearrange("p (n j q t) -> p n j q t", n=2, j=2, q=QT)
        att0T = A0[:, 20816:20816 + NP0 * S].rearrange("p (u t) -> p u t", u=NP0)
        pT0 = A1[:, 0:2 * 2 * KT0 * S].rearrange("p (n j k t) -> p n j k t", n=2, j=2, k=KT0)
        kvT = xnT
        nm0 = sb("nm0", [P, 3, 2])
        nmc = sb("nmc", [P, 2, 2, QT])
        den = sb("den", [P, 3, 2, 2])
        rden = sb("rden", [P, 2, 2, QT])
        wl = A1[:, 0:NL * W_COLS].rearrange("p (l c) -> p l c", l=NL)
        nT = A0[:, 0:NL * 3 * 2 * D].rearrange("p (j o) -> p j o", o=D)
        w1T = A0[:, 4608:5120]
        w2T = A0[:, 5120:5632].rearrange("p (c d) -> p c d", d=D)
        hh = A0[:, 0:QT * DFF].rearrange("p (q f) -> p q f", q=QT)
        hr = A0[:, 2048:2048 + QT * DFF].rearrange("p (q f) -> p q f", q=QT)
        hq = A0[:, 4096:5120].bitcast(bf16).rearrange("p (q f) -> p q f", q=QT)
        hqT = A0[:, 5120:6144].bitcast(bf16).rearrange("p (c t) -> p c t", c=FC)
        zqT = A0[:, 6144:6400].bitcast(bf16)
        place = [0]

        def words(n):
            place[0] += n
            assert place[0] <= A_WORDS
            return A0[:, place[0] - n:place[0]]

        class Set:
            pass

        so, co = Set(), Set()
        for w, kt_n, keys in ((so, QT, S), (co, 1, C + C % 2)):
            w.kt_n, w.keys = kt_n, keys
            w.gq_raw = words(2048)
            w.gq = w.gq_raw.bitcast(bf16).rearrange("p (q h r) -> p q h r", q=QT, h=H1)
            w.gk_raw = words(kt_n * 768)
            w.gk = w.gk_raw.bitcast(bf16).rearrange("p (q u c) -> p q u c", q=kt_n, u=H1 // 2)
            w.q_st = words(2048).bitcast(bf16).rearrange("p (u t) -> p u t", u=8)
            w.k_st = words(H1 * keys // 2).bitcast(bf16).rearrange("p (h t) -> p h t", h=H1)
            w.v_raw = words(kt_n * V_COLS)
            w.v = w.v_raw.rearrange("p (k c) -> p k c", k=kt_n)
            w.att = words(512).rearrange("p (q c) -> p q c", q=QT)
            w.nm = words(64).rearrange("p (g q j) -> p g q j", g=NG, q=QT)
            w.nmr = words(64).rearrange("p (g q j) -> p g q j", g=NG, q=QT)
            w.rd = words(64).rearrange("p (g q j) -> p g q j", g=NG, q=QT)
            kq = kt_n * P
            w.raw = words(3 * (512 + kq))
            w.qk = [w.raw[:, 0:512], w.raw[:, 512:512 + kq]]
            w.rot = [w.raw[:, 512 + kq:1024 + kq], w.raw[:, 1024 + kq:1024 + 2 * kq]]
            w.tmp = [w.raw[:, 1024 + 2 * kq:1536 + 2 * kq], w.raw[:, 1536 + 2 * kq:1536 + 3 * kq]]
            w.xnT = words(512)
            w.stats = words(QT * 6).rearrange("p (q c) -> p q c", q=QT)
            w.mv = words(QT * 2).rearrange("p (q c) -> p q c", q=QT)
            w.ve, w.rstd = words(QT), words(QT)
        hT = so.raw[:, 0:2048].rearrange("p (c t) -> p c t", c=FC)
        q_m = words(1024).bitcast(bf16).rearrange("p (n u t) -> p n u t", n=2, u=2)
        so.pT = words(4096).rearrange("p (n j t) -> p n j t", n=2, j=GROUP)
        co.pT = words(2048).rearrange("p (n j t) -> p n j t", n=1, j=GROUP)
        so.o = words(512)
        attT = words(512)
        co.o = words(512)
        ctx_b = words(P)
        f1s = words(512)
        wgT = A1[:, 0:512]
        wuT = A1[:, 512:1024]
        wdT = A1[:, 1024:1536].rearrange("p (c d) -> p c d", d=D)
        gateT = A1[:, 1536:1544]
        rank = A1[:, 1544:1552]
        eg = A0[:, 0:QT * E * I].rearrange("p (q f) -> p q f", q=QT)
        eu = A0[:, 2048:4096].rearrange("p (q f) -> p q f", q=QT)
        es = A0[:, 4096:6144].rearrange("p (q f) -> p q f", q=QT)
        ehT = A0[:, 6144:8192].rearrange("p (c t) -> p c t", c=FC)
        lg = A0[:, 8192:8224].rearrange("p (q e) -> p q e", q=QT)
        oh = A0[:, 8224:8256].rearrange("p (q e) -> p q e", q=QT)
        top = A0[:, 8256:8272].rearrange("p (k q) -> p k q", k=4)

        x_dram = a["x"].rearrange("b (q p) d -> p (b q) d", p=P)
        load("first", x_res[:, :, :], x_dram)
        load("first", ctx_sb[0:C, :, :], a["ctx"].rearrange("b c d -> c b d"))
        load("first", ctxT[:, :, :], a["ctxT"])
        load("first", condT[:, :], a["condT"])
        load("first", ident[:, :], a["ident"])
        load("first", rope[:, :, :], a["rope"].rearrange("p (q r) -> p q r", q=QT))
        load("first", mask_in[:, :], a["mask"])
        load("first", maskc_in[0:C, :], a["maskc"])
        load("first", vec[:, :], a["vec"])
        load("first", n1w_bc[:, :], a["n1w"].rearrange("(o n) -> o n", o=1).to_broadcast([P, D]))
        load("first", n2w_bc[:, :], a["n2w"].rearrange("(o n) -> o n", o=1).to_broadcast([P, DFF]))
        load("first", act_sb[:, :], a["actsb"].rearrange("(o n) -> o n", o=1).to_broadcast([P, 2]))
        load("first", nb[:, :], a["nb"])
        load("first", f1b[:, :], a["f1b"])
        load("first", f2b[:, :], a["f2b"])
        load("first", nT.rearrange("p j o -> p (j o)"), a["nT"])
        load("first", w1T, a["w1T"])
        load("first", w2T.rearrange("p c d -> p (c d)"), a["w2T"])

        for e in Program.ENGINES:
            loaded(e, "first")
        ones_t = dve(lambda e, v: e.memset(ones_sq[:, :], 1.0))
        dve(lambda e, v: e.memset(neg_half[:, :], -0.5))
        id16 = dve(lambda e, v: e.tensor_copy(ident16[:, :], ident[:, :]))
        for raw, row, k in ((mask_in, mask_row, P), (maskc_in, maskc_row, C)):
            t = dve(lambda e, v, raw=raw, row=row, k=k: e.tensor_copy(row[0:k, :], raw[0:k, :]))
            dve(lambda e, v, row=row, k=k: e.tensor_scalar(row[0:k, :], row[0:k, :], -3.0e38, 3.0e38, ALU.mult, ALU.mult), [t])
        t0 = dve(lambda e, v: e.tensor_scalar(lat_b[:, :], condT[:, :], 1.0, None, ALU.add))
        t1 = dve(lambda e, v: e.tensor_scalar(lat_g[:, :], lat_b[:, :], vec[:, 2:3], None, ALU.mult), [t0])
        t2 = dve(lambda e, v: e.tensor_scalar(lat_b[:, :], lat_b[:, :], vec[:, 3:4], None, ALU.mult), [t1])
        dve(lambda e, v: e.tensor_tensor(lat_b[:, :], lat_b[:, :], condT[:, :], ALU.add), [t2])
        t0 = dve(lambda e, v: e.tensor_reduce(wsum[:, 0:1], w1T, AX.X, ALU.add, apply_absolute_value=True))
        t1 = dve(lambda e, v: e.tensor_reduce(wsum[:, 1:2], w2T, AX.XY, ALU.add, apply_absolute_value=True))
        t = pe(lambda e, v: e.matmul(psum[:, 0, 0:2], ones_sq[:, :], wsum[:, :], start=True, stop=True), [t0, t1, ones_t])
        t = dve(lambda e, v: e.tensor_scalar(wscale[:, :], psum[:, 0, 0:2], 1.0 / (D * DFF), 1e-5, ALU.mult, ALU.max), [t])
        t = dve(lambda e, v: e.reciprocal(wsum[:, :], wscale[:, :]), [t])
        for w, k, dst in ((w1T, 0, wq1[:, :]), (w2T, 1, wq2[:, :, :])):
            u = dve(lambda e, v, w=w, k=k: e.tensor_scalar(w, w, wsum[:, k:k + 1], MAGIC, ALU.mult, ALU.add), [t])
            u = dve(lambda e, v, w=w: e.tensor_scalar(w, w, -MAGIC, 1.0, ALU.add, ALU.min), [u])
            dve(lambda e, v, w=w, dst=dst: e.tensor_scalar(dst, w, -1.0, None, ALU.max), [u])
        for j in range(NL * 6):
            t = pe(lambda e, v, j=j: e.matmul(psum[:, 1, j * B:(j + 1) * B], nT[:, j, :], condT[:, :], start=True, stop=True))
        by_norm = gb[:, :].rearrange("p (w l b) -> p w l b", w=6, b=B)
        for h in range(6):
            t1 = dve(lambda e, v, h=h: e.tensor_tensor(
                by_norm[:, h, :, :], psum[:, 1, 0:NL * 6 * B].rearrange("p (l w b) -> p l w b", w=6, b=B)[:, :, h, :],
                nb[:, :].rearrange("p (l w) -> p l w", w=6)[:, :, h:h + 1].to_broadcast([P, NL, B]), ALU.add), [t])
        prep_end = dve(lambda e, v: e.tensor_scalar(gb[:, :].rearrange("p (w h c) -> p w h c", w=3, h=2)[:, :, 0, :],
                                                    gb[:, :].rearrange("p (w h c) -> p w h c", w=3, h=2)[:, :, 0, :],
                                                    1.0, None, ALU.add), [t1])

        pr.meet(phase=True)
        load("w0", A0[:, 0:4096], a["w0"], 1)

        def norm(src, dst, n, parts, eps, after=(), keep=None):
            for q in range(n):
                t = dve(lambda e, v, q=q: e.bn_stats(stats[0:parts, q, :], src(v)[:, q, :]), after)
            for q in range(n):
                t1 = dve(lambda e, v, q=q: e.bn_aggr(mv[0:parts, q, :], stats[0:parts, q, :]), [t])
            t2 = dve(lambda e, v: e.tensor_scalar(ve[0:parts, 0:n], mv[0:parts, 0:n, 1], eps, None, ALU.add), [t1])
            t3 = pool(lambda e, v: e.tensor_tensor(rstd[0:parts, 0:n], ve[0:parts, 0:n], neg_half[0:parts, 0:n], ALU.pow), [t2])
            for q in range(n):
                t4 = dve(lambda e, v, q=q: e.tensor_scalar(dst[0:parts, q, :], src(v)[:, q, :], mv[0:parts, q, 0:1],
                                                           rstd[0:parts, q:q + 1], ALU.subtract, ALU.mult), [t3])
            return t4

        def transposes(b, src, n, after):
            for q in range(n):
                t = pe(lambda e, v, q=q: e.transpose(psum[:, b, q * P:(q + 1) * P], src[:, q, :], ident[:, :]),
                       after, count=q == n - 1)
            return t

        loaded("tensor", "w0")
        pr.begin("b0", B)
        xb = lambda v: x_res[:, bass.ds(v["b0"] * QT, QT), :]
        t = norm(xb, y, QT, P, 1e-5)
        t = norm(lambda v: y[:, :, :], z, QT, P, 1e-5, [t])
        t = transposes(0, z, QT, [t])
        t_lat = dve(lambda e, v: e.tensor_scalar(kvT[:, 0:S], bank(0), lat_g[:, bass.ds(v["b0"], 1)],
                                                 lat_b[:, bass.ds(v["b0"], 1)], ALU.mult, ALU.add), [t])
        t = norm(lambda v: ctx_sb[0:C, bass.ds(v["b0"], 1), :], zc[:, :].unsqueeze(1), 1, C, 1e-5, [t])
        t = pe(lambda e, v: e.transpose(psum[:, 1, 0:C], zc[0:C, :], ident[0:C, 0:C]), [t])
        t_ctx = dve(lambda e, v: e.tensor_scalar(kvT[:, S:KV], psum[:, 1, 0:C], vec[:, 0:1], vec[:, 1:2],
                                                 ALU.mult, ALU.add), [t])
        free = {i: None for i in range(8)}
        i = 0
        for k in range(KT0):
            rows = min(P, KV - k * P)
            for half in range(2):
                b = i % 4
                t = pe(lambda e, v, k=k, half=half, b=b, rows=rows: e.matmul(
                    psum[0:rows, b, :], kvT[:, k * P:k * P + rows], wvT[:, half * 512:(half + 1) * 512],
                    start=True, stop=True), [t_lat, t_ctx, free[b]])
                put = act if half else dve
                copy = ((lambda e, o, i: e.activation(o, i, ACT.Copy)) if half else (lambda e, o, i: e.tensor_copy(o, i)))
                free[b] = put(lambda e, v, k=k, half=half, b=b, rows=rows, copy=copy: copy(
                    e, v0[0:rows, k, half * 512:(half + 1) * 512], psum[0:rows, b, :]), [t])
                i += 1
        v_ready = [free[b] for b in range(4)]
        UNITS = NP0 * QT
        ready = {}
        used = {}

        def project(u, what):
            n = u % 2
            w, src, cols, dst = {
                "q": (wqT, slice(0, S), S, q_pair[:, n, :]),
                "k": (wkT, slice(0, S), S, k_pair[:, n, 0:S]),
                "c": (wkT, slice(S, KV), C, k_pair[:, n, S:KV])}[what]
            t = pe(lambda e, v: e.matmul(psum[:, 4, 0:cols], w[:, u * P:(u + 1) * P], kvT[:, src], start=True, stop=True),
                   [t_lat, t_ctx, free[4]])
            ready[what, u] = free[4] = act(lambda e, v: e.activation(dst, psum[:, 4, 0:cols], ACT.Copy),
                                           [t, used.get((what == "q", n))])

        def context_scores(u, j):
            n, lo = u % 2, j * HD0
            for q in range(QT):
                t = pe(lambda e, v, q=q: e.matmul(psum[:, 4, q * P:q * P + C], q_pair[lo:lo + HD0, n, q * P:(q + 1) * P],
                                                  k_pair[lo:lo + HD0, n, S:KV], start=True, stop=True),
                       [ready["q", u], ready["c", u], free[4]], count=q == QT - 1)
            src = bank(4).rearrange("p (q k) -> p q k", q=QT)[:, :, 0:C]
            ready["cs", u, j] = dve(lambda e, v: e.tensor_copy(c_sc[:, n, j, :, :], src), [t, used.get(("cs", n, j))])
            ready["cm", u, j] = free[4] = dve(lambda e, v: e.tensor_reduce(nmc[:, n, j, :], src, AX.X, ALU.max, negate=True), [t])

        def scores(i):
            u, q = divmod(i, QT)
            n = u % 2
            for j in range(2):
                b, lo = 2 * (i % 2) + j, j * HD0
                ready["s", i, j] = pe(lambda e, v, b=b, lo=lo: e.matmul(
                    bank(b), q_pair[lo:lo + HD0, n, q * P:(q + 1) * P], k_pair[lo:lo + HD0, n, 0:S], start=True, stop=True),
                    [ready["q", u], ready["k", u], free[b]])
            used[True, n] = used[False, n] = ready["s", i, 1]

        def maxima(i):
            u, q = divmod(i, QT)
            n, r = u % 2, i % 3
            for j in range(2):
                t = dve(lambda e, v, j=j: e.tensor_reduce(nm0[:, r, j:j + 1], bank(2 * (i % 2) + j), AX.X, ALU.max, negate=True),
                        [ready["s", i, j], used.get(("nm", r))])
            t = dve(lambda e, v: e.tensor_tensor(nm0[:, r, :], nm0[:, r, :], nmc[:, n, :, q], ALU.min),
                    [t, ready["cm", u, 0], ready["cm", u, 1]])
            ready["m", i] = dve(lambda e, v: e.tensor_scalar(nm0[:, r, :], nm0[:, r, :], HD0 ** -0.5, None, ALU.mult), [t])

        def exponentials(i):
            u, q = divmod(i, QT)
            n, r = u % 2, i % 3
            for j in range(2):
                b = 2 * (i % 2) + j
                free[b] = act(lambda e, v, j=j, b=b: e.activation(
                    p0[:, r, j, :], bank(b), ACT.Exp, scale=HD0 ** -0.5, bias=nm0[:, r, j:j + 1], accum_out=den[:, r, 0, j:j + 1]),
                    [ready["m", i], used.get(("p", r))])
                t = act(lambda e, v, j=j: e.activation(
                    c_p[:, n, j, q, :], c_sc[:, n, j, q, :], ACT.Exp, scale=HD0 ** -0.5, bias=nm0[:, r, j:j + 1],
                    accum_out=den[:, r, 1, j:j + 1]), [ready["cs", u, j], used.get(("cp", n, j))])
                used["cs", n, j] = t
            ready["e", i] = used["nm", r] = t

        def divide(i):
            u, q = divmod(i, QT)
            n, r = u % 2, i % 3
            t = dve(lambda e, v: e.tensor_tensor(den[:, r, 0, :], den[:, r, 0, :], den[:, r, 1, :], ALU.add), [ready["e", i]])
            t = dve(lambda e, v: e.reciprocal(rden[:, n, :, q], den[:, r, 0, :]), [t, used.get(("rden", n))])
            for j in range(2):
                ready["p", i, j] = pool(lambda e, v, j=j: e.tensor_tensor(
                    p0[:, r, j, :], p0[:, r, j, :], rden[:, n, j, q:q + 1].to_broadcast([P, S]), ALU.mult), [t])
            if q == QT - 1:
                for j in range(2):
                    used["rden", n] = ready["cp", u, j] = pool(lambda e, v, j=j: e.tensor_tensor(
                        c_p[:, n, j, :, :], c_p[:, n, j, :, :], rden[:, n, j, :].unsqueeze(2).to_broadcast([P, QT, C]), ALU.mult), [t])

        def turn(i):
            u, q = divmod(i, QT)
            n, r = u % 2, i % 3
            for j in range(2):
                b = 5 + j
                for k in range(QT):
                    t = pe(lambda e, v, j=j, k=k, b=b: e.transpose(psum[:, b, k * P:(k + 1) * P], p0[:, r, j, k * P:(k + 1) * P], ident[:, :]),
                           [ready["p", i, j], free[b]], count=k == QT - 1)
                dst = pT0[:, n, j, 0:QT, q * P:(q + 1) * P]
                src = bank(b).rearrange("p (k t) -> p k t", k=QT)
                if j:
                    free[b] = act(lambda e, v, dst=dst, src=src: e.activation(dst, src, ACT.Copy), [t, used.get(("pT", n))])
                else:
                    free[b] = dve(lambda e, v, dst=dst, src=src: e.tensor_copy(dst, src), [t, used.get(("pT", n))])
                ready["T", i, j] = free[b]
            used["p", r] = t

        def turn_context(u, j):
            n = u % 2
            for q in range(QT):
                t = pe(lambda e, v, q=q: e.transpose(psum[0:C, 4, q * P:(q + 1) * P], c_p[:, n, j, q, :], ident[:, :]),
                       [ready["cp", u, j], free[4]], count=q == QT - 1)
            used["cp", n, j] = t
            ready["Tc", u, j] = free[4] = dve(lambda e, v: e.tensor_copy(pT0[0:C, n, j, QT, :], psum[0:C, 4, :]),
                                              [t, used.get(("pT", n))])

        def values(u, k):
            n, rows = u % 2, min(P, KV - k * P)
            for j in range(2):
                after = [ready["T", QT * u + q, j] for q in range(QT)] if k < QT else [ready["Tc", u, j]]
                t = pe(lambda e, v, j=j: e.matmul(psum[j * HD0:(j + 1) * HD0, 7, :], v0[0:rows, k, (2 * u + j) * HD0:(2 * u + j + 1) * HD0],
                                                  pT0[0:rows, n, j, k, :], start=k == 0, stop=k == KT0 - 1),
                       after + v_ready + [free[7]], count=j == 1)
            if k == KT0 - 1:
                used["pT", n] = t
                free[7] = ready["att", u] = act(lambda e, v: e.activation(att0T[:, u, :], bank(7), ACT.Copy), [t])

        for what in ("q", "k", "c"):
            project(0, what)
        context_scores(0, 0)
        context_scores(0, 1)
        scores(0)
        maxima(0)
        for i in range(UNITS + 7):
            u, q = divmod(i, QT)
            more = u + 1 < NP0
            if more and q == 0:
                project(u + 1, "q")
            if more and q == 1:
                project(u + 1, "c")
            if more and q == 2:
                context_scores(u + 1, 1)
            if q == 3 and 1 <= u <= NP0:
                turn_context(u - 1, 1)
            if i < UNITS:
                exponentials(i)
            if i + 1 < UNITS:
                scores(i + 1)
                maxima(i + 1)
            if i < UNITS:
                divide(i)
            if 1 <= i <= UNITS:
                turn(i - 1)
            if more and q == 0:
                project(u + 1, "k")
            if more and q == 1:
                context_scores(u + 1, 0)
            if q == 2 and 1 <= u <= NP0:
                turn_context(u - 1, 0)
            if 1 <= u <= NP0:
                for k in {0: (), 1: (0, 1), 2: (2,), 3: (3,)}[q]:
                    values(u - 1, k)
            if 2 <= u and q == 0:
                values(u - 2, QT)
            if u == NP0 + 1:
                break
        for q in range(QT):
            for u in range(NP0):
                t = pe(lambda e, v, q=q, u=u: e.matmul(psum[:, 0, q * P:(q + 1) * P], att0T[:, u, q * P:(q + 1) * P],
                                                       woT[:, u, :], start=u == 0, stop=u == NP0 - 1),
                       [free[7], free[0]], count=u == NP0 - 1)
        dve(lambda e, v: e.tensor_tensor(xb(v), xb(v), bank(0).rearrange("p (q d) -> p q d", q=QT), ALU.add), [t])
        pr.end()
        pr.meet(phase=True)
        load("wl", wl.rearrange("p l c -> p (l c)"), a["wl"], 2)

        pr.begin("b1", B)
        xb1 = lambda v: x_res[:, bass.ds(v["b1"] * QT, QT), :]

        def mean_square(src, t):
            for q in range(QT):
                t1 = dve(lambda e, v, q=q: e.bn_stats(stats[:, q, :], src[:, q, :]), [t])
            for q in range(QT):
                t2 = dve(lambda e, v, q=q: e.bn_aggr(mv[:, q, :], stats[:, q, :]), [t1])
            t = dve(lambda e, v: e.tensor_tensor(ve[:, :], mv[:, :, 0], mv[:, :, 0], ALU.mult), [t2])
            t = dve(lambda e, v: e.tensor_tensor(ve[:, :], ve[:, :], mv[:, :, 1], ALU.add), [t])
            t = dve(lambda e, v: e.tensor_scalar(ve[:, :], ve[:, :], 1e-8, None, ALU.add), [t])
            return pool(lambda e, v: e.tensor_tensor(rstd[:, :], ve[:, :], neg_half[:, :], ALU.pow), [t])

        def quantise(src, work, dst, w_bc, width, wcol, t):
            for q in range(QT):
                t1 = act(lambda e, v, q=q: e.activation(work[:, q, :], src[:, q, :], ACT.Copy, scale=rstd[:, q:q + 1]), [t])
            t = dve(lambda e, v: e.tensor_tensor(work, work, w_bc.unsqueeze(1).to_broadcast([P, QT, width]), ALU.mult), [t1])
            t = dve(lambda e, v: e.tensor_reduce(small[:, 0, :], work, AX.X, ALU.max, apply_absolute_value=True), [t])
            t = dve(lambda e, v: e.tensor_scalar(small[:, 0, :], small[:, 0, :], 1e-5, None, ALU.max), [t])
            t = dve(lambda e, v: e.reciprocal(small[:, 2, :], small[:, 0, :]), [t])
            t = dve(lambda e, v: e.tensor_scalar(small[:, 2, :], small[:, 2, :], 127.0, None, ALU.mult), [t])
            t1 = dve(lambda e, v: e.tensor_scalar(small[:, 1, :], small[:, 0, :], 1.0 / 127.0, wscale[:, wcol:wcol + 1],
                                                  ALU.mult, ALU.mult), [t])
            for q in range(QT):
                t = dve(lambda e, v, q=q: e.tensor_scalar(work[:, q, :], work[:, q, :], small[:, 2, q:q + 1], MAGIC,
                                                          ALU.mult, ALU.add), [t1])
            t = dve(lambda e, v: e.tensor_scalar(work, work, -MAGIC, 127.0, ALU.add, ALU.min), [t])
            return dve(lambda e, v: e.tensor_scalar(dst, work, -128.0, None, ALU.max), [t])

        t = norm(xb1, y, QT, P, 1e-5)
        t = mean_square(y, t)
        t = quantise(y[:, :, :], z[:, :, :], zq[:, :, :], n1w_bc[:, :], D, 0, t)
        for q in range(QT):
            t1 = pe(lambda e, v, q=q: e.transpose(bank16(0)[:, q * P:(q + 1) * P], zq[:, q, :], ident16[:, :]), [t],
                    count=q == QT - 1)
        t = act(lambda e, v: e.activation(zqT, bank16(0)[:, 0:S], ACT.Copy), [t1])
        for q in range(QT):
            t1 = pe(lambda e, v, q=q: e.matmul(bank(1 + q), zqT[:, q * P:(q + 1) * P], wq1[:, :], start=True, stop=True), [t])
            t2 = act(lambda e, v, q=q: e.activation(hh[:, q, :], bank(1 + q), ACT.Relu, scale=small[:, 1, q:q + 1]), [t1])
        t = act(lambda e, v: e.activation(hh, hh, ACT.Square), [t2])
        t = dve(lambda e, v: e.tensor_scalar(hh, hh, act_sb[:, 0:1], act_sb[:, 1:2], ALU.mult, ALU.add), [t])
        t = mean_square(hh, t)
        t = quantise(hh, hr, hq, n2w_bc[:, :], DFF, 1, t)
        for c in range(FC):
            for q in range(QT):
                t1 = pe(lambda e, v, q=q, c=c: e.transpose(bank16(6 + c // 2)[:, (c % 2) * S + q * P:(c % 2) * S + (q + 1) * P],
                                                           hq[:, q, c * P:(c + 1) * P], ident16[:, :]), [t],
                        count=q == QT - 1)
            if c % 2:
                t2 = act(lambda e, v, c=c: e.activation(hqT[:, c - 1:c + 1, :].rearrange("p c t -> p (c t)"),
                                                        bank16(6 + c // 2), ACT.Copy), [t1])
        for q in range(QT):
            for c in range(FC):
                t = pe(lambda e, v, q=q, c=c: e.matmul(psum[:, 0, q * P:(q + 1) * P], hqT[:, c, q * P:(q + 1) * P],
                                                       wq2[:, c, :], start=c == 0, stop=c == FC - 1), [t2], count=c == FC - 1)
        t = dve(lambda e, v: e.tensor_tensor(z[:, :, :], bank(0).rearrange("p (q d) -> p q d", q=QT),
                                             small[:, 1, :].unsqueeze(2).to_broadcast([P, QT, D]), ALU.mult), [t])
        t = dve(lambda e, v: e.tensor_tensor(xb1(v), xb1(v), z[:, :, :], ALU.add), [t])
        t_y = norm(xb1, y, QT, P, 1e-5, [t])
        dve(lambda e, v: e.tensor_copy(x_st[:, bass.ds(v["b1"] * QT, QT), :], y[:, :, :]),
            [t_y])
        pr.end()

        pr.meet()
        for e in Program.ENGINES:
            loaded(e, "wl")
        for w in (so, co):
            t = pool(lambda e, v, w=w: e.memset(w.gq_raw, 0.0))
            pool(lambda e, v, w=w: e.memset(w.gq.rearrange("p q h r -> p (q h) r")[:, :, MROW:MROW + 1], 1.0), [t])
            t = pool(lambda e, v, w=w: e.memset(w.gk_raw, 0.0))
            for j in range(2):
                lo = 2 * STACK * j + MROW + 1
                pool(lambda e, v, w=w, lo=lo: e.memset(w.gk.rearrange("p q u c -> p (q u) c")[:, :, lo:lo + 3], 1.0), [t])
            pool(lambda e, v, w=w: e.memset(w.v_raw, 1.0))
        pr.meet()

        bfree = {}
        last = {}
        count = {"max": 0, "exp": 0, "misc": 0}
        where_core = [0]

        def new_pass():
            bfree.clear()
            last.clear()
            where_core[0] = -1

        def bank_max():
            count["max"] += 1
            return count["max"] % 2

        def bank_exp():
            count["exp"] += 1
            return 2 + count["exp"] % 3

        def bank_misc():
            count["misc"] += 1
            return (5, 7)[count["misc"] % 2]

        def xs(e, v, back):
            return x_st[:, bass.ds(at(e, v, back, "batch") * QT, QT), :]

        def wcols(e, v, back, lo, n):
            return wl[:, bass.ds(at(e, v, back, "layer"), 1), lo:lo + n].rearrange("p o c -> p (o c)")

        def reads(*keys):
            got = []
            for k in keys:
                t = last.get(k)
                got += t if isinstance(t, list) else [t]
            return got

        def g_norm(w, which, back, after):
            y1 = w.rot[0].rearrange("p (q c) -> p q c", q=QT)
            for q in range(QT):
                t = dve(lambda e, v, q=q: e.bn_stats(w.stats[:, q, :], xs(e, v, back)[:, q, :]), after)
            for q in range(QT):
                t1 = dve(lambda e, v, q=q: e.bn_aggr(w.mv[:, q, :], w.stats[:, q, :]), [t])
            yield
            t2 = dve(lambda e, v: e.tensor_scalar(w.ve, w.mv[:, :, 1], 1e-5, None, ALU.add), [t1])
            t3 = pool(lambda e, v: e.tensor_tensor(w.rstd, w.ve, neg_half[:, :], ALU.pow), [t2])
            yield
            yield
            for q in range(QT):
                t4 = dve(lambda e, v, q=q: e.tensor_scalar(y1[:, q, :], xs(e, v, back)[:, q, :], w.mv[:, q, 0:1],
                                                           w.rstd[:, q:q + 1], ALU.subtract, ALU.mult),
                         [t3] + reads("hT", ("raw", id(w))))
            last["x read"] = t4
            yield
            yield
            b = bank_misc()
            for q in range(QT):
                t = pe(lambda e, v, q=q: e.transpose(psum[:, b, q * P:(q + 1) * P], y1[:, q, :], ident[:, :]),
                       [t4, bfree.get(b)], count=q == QT - 1)
            g = lambda e, v, half: gb[:, bass.ds((which * 2 + half) * NL * B + at(e, v, back, "step"), 1)]
            bfree[b] = act(lambda e, v: e.activation(w.xnT, bank(b), ACT.Identity, scale=g(e, v, 0), bias=g(e, v, 1)),
                           [t] + reads(("xnT", id(w))))
            last["xn", id(w)] = bfree[b]
            yield
            yield

        def g_rotate(w, k, rows):
            nq = w.kt_n if k else QT
            heads = lambda t: t[0:rows, :].rearrange("p (q h d) -> p q h d", q=nq, d=HD1)
            src, dst, tm = heads(w.qk[k]), heads(w.rot[k]), heads(w.tmp[k])
            tab = lambda lo, n: rope[0:rows, 0:nq, lo:lo + n].unsqueeze(2).to_broadcast([rows, nq, H1, n])
            half = HD1 // 2
            ready = [last["qk", id(w), k]]
            pool(lambda e, v: e.tensor_tensor(dst, src, tab(0, HD1), ALU.mult), ready)
            yield
            pool(lambda e, v: e.tensor_tensor(tm[:, :, :, 0:half], src[:, :, :, half:HD1], tab(HD1, half), ALU.mult))
            t = pool(lambda e, v: e.tensor_tensor(tm[:, :, :, half:HD1], src[:, :, :, 0:half], tab(HD1 + half, half), ALU.mult))
            yield
            last["rot", id(w), k] = pool(lambda e, v: e.tensor_tensor(w.rot[k][0:rows, :], w.rot[k][0:rows, :], w.tmp[k][0:rows, :], ALU.add), [t])
            yield

        def g_split(w, k, rows, pairs, after=()):
            slots = SLOT_K if k else SLOT_Q
            nq = w.kt_n if k else QT
            lo, n = pairs
            every = n == H1 // 2
            if k == 0:
                g = w.gq[0:rows].rearrange("p q (u j) r -> p q u j r", j=2)
            else:
                g = w.gk[0:rows].rearrange("p q u (j r) -> p q u j r", r=STACK)[:, :, :, 0:3:2, :]
            def slot(s):
                t = g[:, :, lo:lo + n, :, s * HD1:(s + 1) * HD1]
                return t.rearrange("p q u j d -> p (q u) j d") if every else t.rearrange("p q u j d -> p q (u j) d")
            def flat(t):
                t = t[0:rows, :].rearrange("p (q u j d) -> p q u j d", q=nq, j=2, d=HD1)[:, :, lo:lo + n]
                return t.rearrange("p q u j d -> p (q u) j d") if every else t.rearrange("p q u j d -> p q (u j) d")
            src, rem = flat(w.rot[k]), flat(w.tmp[k])
            where = [[s for s in range(len(slots)) if slots[s] == part] for part in range(3)]
            ends = []
            t1 = pool(lambda e, v: e.tensor_copy(slot(where[0][0]), src), [last["rot", id(w), k]] + list(after))
            yield
            t2 = pool(lambda e, v: e.tensor_tensor(rem, src, slot(where[0][0]), ALU.subtract), [t1])
            for s in where[0][1:]:
                ends.append(act(lambda e, v, s=s: e.activation(slot(s), slot(where[0][0]), ACT.Copy), [t1]))
            yield
            t3 = pool(lambda e, v: e.tensor_copy(slot(where[1][0]), rem), [t2])
            yield
            ends.append(pool(lambda e, v: e.tensor_tensor(slot(where[2][0]), rem, slot(where[1][0]), ALU.subtract), [t3]))
            for s in where[1][1:]:
                ends.append(act(lambda e, v, s=s: e.activation(slot(s), slot(where[1][0]), ACT.Copy), [t3]))
            last["split", id(w), k] = ends
            last["raw", id(w)] = ends[:]
            yield
            yield

        def stack_up(w, k, i, after, evac):
            if k == 0:
                block = lambda q, u: w.gq[:, q, 2 * u:2 * u + 2, :].rearrange("p h r -> p (h r)")
                dst = w.q_st
            else:
                block = lambda q, h: w.gk[:, q, h // 2, (h % 2) * STACK:(h % 2) * STACK + P]
                dst = w.k_st
            b = bank_misc()
            for n in range(2):
                for q in range(QT):
                    t = pe(lambda e, v, n=n, q=q: e.transpose(
                        bank16(b)[:, n * S + q * P:n * S + (q + 1) * P], block(q, i + n), ident16[:, :]),
                        after + [bfree.get(b)], count=n == 1 and q == QT - 1)
            to = dst[:, i:i + 2, :].rearrange("p u t -> p (u t)")
            if evac == "act":
                bfree[b] = act(lambda e, v: e.activation(to, bank16(b), ACT.Copy), [t] + after)
            else:
                bfree[b] = dve(lambda e, v: e.tensor_copy(to, bank16(b)), [t] + after)
            last["stack", id(w), k, i // 2] = bfree[b]
            last["stacked", id(w), k] = t
            return bfree[b]

        def g_mask(w, rows, src):
            ends = []
            for j in range(2):
                ends.append(dve(lambda e, v, j=j: e.tensor_copy(w.gk[0:rows, :, :, 2 * STACK * j + MROW],
                                                                src(e, v).unsqueeze(2).to_broadcast([rows, w.kt_n, H1 // 2])),
                                reads(("stacked", id(w), 1))))
            last["mask", id(w)] = ends
            yield

        def clear_shift(w, lo, n):
            last["cleared", id(w), lo] = pool(
                lambda e, v: e.memset(w.gq[:, :, lo:lo + n, MROW + 1:MROW + 4], 0.0),
                reads(("shift", id(w)), ("shift up", id(w))))

        def g_self_a(back):
            w = so
            yield from g_norm(w, 0, back, [])
            for i in range(2):
                b = bank_misc()
                for q in range(2 * i, 2 * i + 2):
                    t = pe(lambda e, v, q=q, b=b: e.matmul(psum[:, b, (q % 2) * 256:(q % 2) * 256 + 256], w.xnT[:, q * P:(q + 1) * P],
                                                           wcols(e, v, back, W_QKV, 256), start=True, stop=True),
                           [last["xn", id(w)], bfree.get(b)])
                for k in range(2):
                    bfree[b] = act(lambda e, v, i=i, k=k, b=b: e.activation(
                        w.qk[k].rearrange("p (q c) -> p q c", q=QT)[:, 2 * i:2 * i + 2, :],
                        bank(b).rearrange("p (q k c) -> p q k c", q=2, k=2)[:, :, k, :], ACT.Copy), [t] + reads("hT"))
                    last["qk", id(w), k] = bfree[b]
                yield
            yield from g_rotate(w, 1, P)
            yield from g_rotate(w, 0, P)

        def core_at(g):
            while where_core[0] < g:
                yield

        def g_self_b(back):
            w = so
            yield from g_mask(w, P, lambda e, v: mask_row[:, bass.ds(at(e, v, back, "batch") * QT, QT)])
            yield from g_split(w, 1, P, (0, H1 // 2), reads(("stacked", id(w), 1)))
            k_ready = reads(("split", id(w), 1), ("mask", id(w)))
            yield from core_at(1)
            clear_shift(w, 0, H1 // 2)
            yield from g_split(w, 0, P, (0, H1 // 4), reads(("shift up", id(w))))
            for i in (0, 2):
                stack_up(w, 0, i, reads(("split", id(w), 0), ("cleared", id(w), 0), "q read"), "dve")
                yield
            for i in (0, 2):
                stack_up(w, 1, i, k_ready + reads(("k read", 0)), "act")
                yield
            yield from core_at(2)
            for i in (4, 6):
                stack_up(w, 1, i, k_ready + reads(("k read", 1)), "act")
                yield
            yield from core_at(3)
            clear_shift(w, H1 // 2, H1 // 2)
            yield from g_split(w, 0, P, (H1 // 4, H1 // 4), reads(("shift up", id(w))))
            for i in (8, 10):
                stack_up(w, 1, i, k_ready + reads(("k read", 2)), "act")
                yield
            for i in (4, 6):
                stack_up(w, 0, i, reads(("split", id(w), 0), ("cleared", id(w), H1 // 2), "q read"), "dve")
                yield

        def values_of(w, back):
            b = bank_misc()
            for q in range(QT):
                t = pe(lambda e, v, q=q: e.matmul(psum[:, b, q * P:(q + 1) * P], w.xnT[:, q * P:(q + 1) * P],
                                                  wcols(e, v, back, W_QKV + 256, D), start=True, stop=True), [bfree.get(b)])
            last["xnT", id(w)] = t
            for q in range(QT):
                bfree[b] = act(lambda e, v, q=q: e.activation(
                    w.v[:, q, 0:H1 * (HD1 + 1)].rearrange("p (h d) -> p h d", d=HD1 + 1)[:, :, 0:HD1],
                    psum[:, b, q * P:(q + 1) * P].rearrange("p (h d) -> p h d", d=HD1), ACT.Copy), [t])
            last["v", id(w)] = bfree[b]

        def g_start():
            values_of(so, 0)
            yield
            yield
            for i in (12, 14):
                stack_up(so, 1, i, [], "act")
                yield

        def g_cross_keys(back):
            w = co
            t_cb = pool(lambda e, v: e.tensor_copy(ctx_b[:, 0:C], ctxT[:, bass.ds(at(e, v, back, "batch"), 1), :].rearrange("p o c -> p (o c)")))
            clear_shift(w, 0, H1)
            yield
            b = bank_misc()
            t = pe(lambda e, v: e.matmul(psum[0:C, b, 0:256], ctx_b[:, 0:C], wcols(e, v, back, W_CKV, 256), start=True, stop=True),
                   [t_cb, bfree.get(b)])
            last["qk", id(w), 1] = act(lambda e, v: e.activation(w.qk[1][0:C, :], psum[0:C, b, 0:P], ACT.Copy), [t])
            bfree[b] = act(lambda e, v: e.activation(
                w.v[0:C, 0, 0:H1 * (HD1 + 1)].rearrange("p (h d) -> p h d", d=HD1 + 1)[:, :, 0:HD1],
                psum[0:C, b, P:2 * P].rearrange("p (h d) -> p h d", d=HD1), ACT.Copy), [t])
            last["v", id(w)] = bfree[b]
            yield
            yield from g_rotate(w, 1, C)
            yield from g_mask(w, C, lambda e, v: maskc_row[0:C, bass.ds(at(e, v, back, "batch"), 1)])
            yield from g_split(w, 1, C, (0, H1 // 2))
            for n in range(2):
                bn = bank_misc()
                for i in range(8):
                    h = 8 * n + i
                    t = pe(lambda e, v, h=h, i=i, bn=bn: e.transpose(bank16(bn)[:, i * P:i * P + C],
                                                                     w.gk[0:C, 0, h // 2, (h % 2) * STACK:(h % 2) * STACK + P],
                                                                     ident16[0:C, 0:C]),
                           reads(("split", id(w), 1), ("mask", id(w))) + [bfree.get(bn)], count=i == 7)
                bfree[bn] = act(lambda e, v, n=n, bn=bn: e.activation(
                    w.k_st[:, 8 * n:8 * n + 8, 0:C], bank16(bn).rearrange("p (u c) -> p u c", u=8)[:, :, 0:C], ACT.Copy), [t])
                last["k stacks", n] = bfree[bn]
                yield

        def g_cross_queries(back):
            w = co
            yield from g_norm(w, 1, back, reads("x"))
            b = bank_misc()
            for q in range(QT):
                t = pe(lambda e, v, q=q: e.matmul(psum[:, b, q * P:(q + 1) * P], w.xnT[:, q * P:(q + 1) * P],
                                                  wcols(e, v, back, W_CQ, D), start=True, stop=True), [last["xn", id(w)], bfree.get(b)])
            last["qk", id(w), 0] = bfree[b] = act(lambda e, v: e.activation(w.qk[0], bank(b), ACT.Copy), [t])
            yield
            yield from g_rotate(w, 0, P)
            yield from g_split(w, 0, P, (0, H1 // 2))
            for i in (0, 2, 4, 6):
                stack_up(w, 0, i, reads(("split", id(w), 0), ("cleared", id(w), 0)), "dve")
                yield

        def g_project(w, wcol, back):
            b = bank_misc()
            for q in range(QT):
                t = pe(lambda e, v, q=q: e.transpose(psum[:, b, q * P:(q + 1) * P], w.att[:, q, :], ident[:, :]),
                       reads(("att ready", id(w))) + [bfree.get(b)], count=q == QT - 1)
            last["att", id(w)] = t
            bfree[b] = t = act(lambda e, v: e.activation(attT, bank(b), ACT.Copy), [t] + reads("attT"))
            yield
            yield
            b1 = bank_misc()
            for q in range(QT):
                t1 = pe(lambda e, v, q=q: e.matmul(psum[:, b1, q * P:(q + 1) * P], attT[:, q * P:(q + 1) * P],
                                                   wcols(e, v, back, wcol, D), start=True, stop=True), [t, bfree.get(b1)])
            last["attT"] = t1
            bfree[b1] = dve(lambda e, v: e.tensor_tensor(xs(e, v, back), xs(e, v, back), bank(b1).rearrange("p (q d) -> p q d", q=QT),
                                                         ALU.add), [t1] + reads("x read"))
            last["x"] = bfree[b1]
            yield
            yield

        def g_ffn(back):
            w = so
            t_f1 = pool(lambda e, v: e.tensor_copy(f1s, wcols(e, v, back, W_F1, DFF)))
            yield from g_norm(w, 2, back, [])
            for c in range(FC):
                b = bank_misc()
                t = pe(lambda e, v, c=c, b=b: e.matmul(bank(b), f1s[:, c * P:(c + 1) * P], w.xnT, start=True, stop=True),
                       [last["xn", id(w)], t_f1, bfree.get(b)])
                last["xnT", id(w)] = t
                bfree[b] = t2 = dve(lambda e, v, c=c, b=b: e.tensor_scalar(
                    hT[:, c, :], bank(b), f1b[:, bass.ds(at(e, v, back, "layer") * FC + c, 1)], None, ALU.add), [t])
                yield
            t2 = act(lambda e, v: e.activation(hT, hT, ACT.Gelu), [t2])
            yield
            yield
            yield
            b2 = bank_misc()
            for q in range(QT):
                for c in range(FC):
                    pe(lambda e, v, q=q, c=c: e.matmul(psum[:, b2, q * P:(q + 1) * P], hT[:, c, q * P:(q + 1) * P],
                                                       wcols(e, v, back, W_F2 + c * D, D), start=c == 0, stop=False),
                       [t2, bfree.get(b2)], count=False)
                t = pe(lambda e, v, q=q: e.matmul(psum[:, b2, q * P:(q + 1) * P], ones_sq[0:1, :],
                                                  f2b[0:1, bass.ds(at(e, v, back, "layer") * D, D)], start=False, stop=True))
            last["hT"] = t
            bfree[b2] = dve(lambda e, v: e.tensor_tensor(
                xs(e, v, back), xs(e, v, back), bank(b2).rearrange("p (q d) -> p q d", q=QT), ALU.add), [t] + reads("x read"))
            yield

        def max_step(g, i):
            w = so
            j, q = divmod(i, QT)
            h = GROUP * g + j
            b = bank_max()
            t = pe(lambda e, v: e.matmul(bank(b), w.q_st[:, h // 2, q * P:(q + 1) * P], w.k_st[:, h, 0:S], start=True, stop=True),
                   reads(("stack", id(w), 0, h // 4), ("stack", id(w), 1, h // 2)) + [bfree.get(b)])
            bfree[b] = dve(lambda e, v: e.tensor_reduce(w.nm[:, g, q, j:j + 1], bank(b), AX.X, ALU.max, negate=True), [t])
            last["q read"] = t
            return bfree[b]

        def shift(w, lo, n, t, on):
            heads = w.gq[:, :, lo:lo + n, :].rearrange("p q (g j) r -> p g q j r", j=GROUP)
            g0, g1 = lo // GROUP, (lo + n) // GROUP
            same = g1 - g0 == 1
            col = lambda c: heads[:, 0, :, :, MROW + 1 + c] if same else heads[:, :, :, :, MROW + 1 + c]
            nm = w.nm[:, g0, :, :] if same else w.nm
            nmr = w.nmr[:, g0, :, :] if same else w.nmr
            t = on(lambda e, v: e.tensor_copy(col(0), nm), [t])
            t = on(lambda e, v: e.tensor_tensor(nmr, nm, col(0), ALU.subtract), [t])
            t = on(lambda e, v: e.tensor_copy(col(1), nmr), [t])
            last["shift", id(w)] = on(lambda e, v: e.tensor_tensor(col(2), nmr, col(1), ALU.subtract), [t])

        def shift_up(g):
            w = so
            b = bank_misc()
            for n in range(2):
                for q in range(QT):
                    t1 = pe(lambda e, v, n=n, q=q: e.transpose(
                        bank16(b)[:, n * S + q * P:n * S + (q + 1) * P],
                        w.gq[:, q, 4 * g + 2 * n:4 * g + 2 * n + 2, :].rearrange("p h r -> p (h r)"), ident16[:, :]),
                        reads(("shift", id(w))) + [bfree.get(b)], count=n == 1 and q == QT - 1)
            last["shift up", id(w)] = t1
            s = g % 2
            last["q_m ready", s] = bfree[b] = dve(lambda e, v: e.tensor_copy(
                q_m[:, s, :, :].rearrange("p u t -> p (u t)"), bank16(b)), [t1] + reads(("q_m", s)))

        def exp_step(w, h, k, buf, queries, after):
            rows = P if w.kt_n > 1 else C
            j = h % GROUP
            b = bank_exp()
            t = pe(lambda e, v: e.matmul(psum[0:rows, b, :], w.k_st[:, h, k * P:k * P + rows], queries, start=True, stop=True),
                   after + [bfree.get(b)])
            last["pT ready", id(w), buf] = bfree[b] = act(
                lambda e, v: e.activation(w.pT[0:rows, buf, j, :], psum[0:rows, b, :], ACT.Exp, scale=HD1 ** -0.5),
                [t] + reads(("pT", id(w), buf)))
            return t

        def weighted(w, g, k, buf, b):
            rows = P if w.kt_n > 1 else C
            for j in range(GROUP):
                lo = (GROUP * g + j) * (HD1 + 1)
                t1 = pe(lambda e, v, j=j, lo=lo: e.matmul(psum[32 * j:32 * j + 32, b, :], w.v[0:rows, k, lo:lo + 32],
                                                          w.pT[0:rows, buf, j, :], start=k == 0, stop=k == w.kt_n - 1),
                        reads(("pT ready", id(w), buf), ("v", id(w))) + [bfree.get(b)], count=j == GROUP - 1)
            last["pT", id(w), buf] = t1
            last["sum", id(w)] = t1

        def finish_a(w, b):
            bfree[b] = last["o", id(w)] = act(lambda e, v: e.activation(w.o, bank(b), ACT.Copy),
                                              reads(("sum", id(w)), ("o free", id(w))))

        def finish_b(w, g):
            b = bank_misc()
            for q in range(QT):
                t1 = pe(lambda e, v, q=q: e.transpose(psum[:, b, q * P:(q + 1) * P], w.o[:, q * P:(q + 1) * P], ident[:, :]),
                        reads(("o", id(w))) + [bfree.get(b)], count=q == QT - 1)
            last["o free", id(w)] = t1
            o = bank(b).rearrange("p (q j d) -> p q j d", q=QT, j=GROUP)
            t2 = dve(lambda e, v: e.reciprocal(w.rd[:, g, :, :], o[:, :, :, HD1]), [t1])
            n = GROUP * HD1
            last["att ready", id(w)] = bfree[b] = dve(lambda e, v: e.tensor_tensor(
                w.att[:, :, g * n:(g + 1) * n].rearrange("p q (j d) -> p q j d", d=HD1), o[:, :, :, 0:HD1],
                w.rd[:, g, :, :].unsqueeze(3).to_broadcast([P, QT, GROUP, HD1]), ALU.mult), [t2] + reads(("att", id(w))))

        MAX_STEPS = 14

        def g_core(has_next):
            w = so
            pend = None
            for g in range(NG):
                where_core[0] = g
                nxt = (g + 1) % NG
                more = g + 1 < NG or has_next
                i = 0
                for k in range(w.kt_n):
                    for j in range(GROUP):
                        n = GROUP * k + j
                        t = exp_step(w, GROUP * g + j, k, k % 2, q_m[:, g % 2, j // 2, :],
                                     reads(("q_m ready", g % 2), ("stack", id(w), 1, (GROUP * g + j) // 2)))
                        last["k read", g] = last["q_m", g % 2] = t
                        while more and i < min(GROUP * QT, GROUP * QT * (n + 1) // MAX_STEPS):
                            t_m = max_step(nxt, i)
                            i += 1
                        if j == 1 and pend is not None:
                            weighted(w, *pend, 6)
                            if pend[1] == w.kt_n - 1:
                                finish_a(w, 6)
                            pend = None
                        if j == 0 and k == 1 and g > 0:
                            finish_b(w, g - 1)
                        if more and n == MAX_STEPS:
                            shift(w, GROUP * nxt, GROUP, t_m, dve)
                        if more and n == MAX_STEPS + 1:
                            shift_up(nxt)
                        yield
                    pend = (g, k, k % 2)
            weighted(w, *pend, 6)
            finish_a(w, 6)
            yield

        def g_cross_core():
            w = co
            for h in range(H1):
                b = bank_max()
                for q in range(QT):
                    t = pe(lambda e, v, q=q, h=h, b=b: e.matmul(
                        psum[:, b, q * P:q * P + C], w.q_st[:, h // 2, q * P:(q + 1) * P], w.k_st[:, h, 0:C], start=True, stop=True),
                        reads(("stack", id(w), 0, h // 4), ("k stacks", h // 8)) + [bfree.get(b)], count=q == QT - 1)
                t_m = bfree[b] = dve(lambda e, v, h=h, b=b: e.tensor_reduce(
                    w.nm[:, h // GROUP, :, h % GROUP:h % GROUP + 1], bank(b).rearrange("p (q k) -> p q k", q=QT)[:, :, 0:C],
                    AX.X, ALU.max, negate=True), [t])
                if h % 2:
                    yield
            for g in range(NG):
                shift(w, GROUP * g, GROUP, t_m, dve)
            yield
            yield
            for i in (0, 2, 4, 6):
                stack_up(w, 0, i, reads(("shift", id(w))) + [t], "dve")
                yield
            for g in range(NG):
                for j in range(GROUP):
                    h = GROUP * g + j
                    exp_step(w, h, 0, 0, w.q_st[:, h // 2, :], reads(("stack", id(w), 0, h // 4)))
                    if j % 2:
                        yield
                if g:
                    finish_b(w, g - 1)
                b = bank_misc()
                weighted(w, g, 0, 0, b)
                finish_a(w, b)
                yield
            yield
            finish_b(w, NG - 1)
            yield

        def g_then(*makes):
            for make in makes:
                yield from make()

        def step(has_prev, has_ffn, has_next, is_step=True):
            new_pass()
            one, two, three = [], [], []
            if is_step:
                two.append(g_start)
            if has_prev:
                def end_self():
                    finish_b(so, NG - 1)
                    yield
                    yield
                one += [end_self, lambda: g_project(so, W_SO, 1), lambda: g_cross_queries(1), g_cross_core, lambda: g_project(co, W_CO, 1)]
                three.append(lambda: g_cross_keys(1))
            if has_ffn:
                two.append(lambda: g_ffn(2))
            if has_next:
                two += [lambda: g_self_a(-1), lambda: g_self_b(-1)]
            run_beside(g_core(has_next) if is_step else iter(()), g_then(*one), g_then(*two), g_then(*three))

        def at_step(n):
            for e in Program.ENGINES:
                pr.stack[e][-1].append(("set", "n", n))

        steps = NL * B
        at_step(-1)
        new_pass()
        where_core[0] = NG
        run_beside(iter(()), g_then(lambda: g_self_a(-1), lambda: g_self_b(-1)))
        for i in range(GROUP * QT):
            t_m = max_step(0, i)
        shift(so, 0, GROUP, t_m, dve)
        shift_up(0)
        pr.meet()
        for n in range(2):
            at_step(n)
            step(n > 0, False, True)
            pr.meet()
        pr.begin("n", steps - 3, 2)
        step(True, True, True)
        pr.end()
        at_step(steps - 1)
        step(True, True, False)
        pr.meet()
        at_step(steps)
        step(True, True, False, is_step=False)
        pr.meet()
        at_step(steps + 1)
        step(False, True, False, is_step=False)
        pr.meet(phase=True)

        load("wm", A1[:, 0:1552], a["wm"], 3)
        for e in ("tensor", "vector"):
            loaded(e, "wm")
        pr.begin("m", B)
        xm = lambda v: x_res[:, bass.ds(v["m"] * QT, QT), :]
        t = dve(lambda e, v: e.tensor_tensor(xm(v), xm(v), x_st[:, bass.ds(v["m"] * QT, QT), :], ALU.add))
        t = norm(xm, y, QT, P, 1e-5, [t])
        t = transposes(7, y, QT, [t])
        t = act(lambda e, v: e.activation(xnT[:, 0:S], bank(7), ACT.Copy), [t])
        for q in range(QT):
            t1 = pe(lambda e, v, q=q: e.matmul(psum[:, 0, q * E:(q + 1) * E], xnT[:, q * P:(q + 1) * P], gateT, start=True, stop=True), [t])
        lgv = psum[:, 0, 0:QT * E].rearrange("p (q e) -> p q e", q=QT)
        t = dve(lambda e, v: e.tensor_copy(lg, lgv), [t1])
        t = dve(lambda e, v: e.tensor_reduce(top[:, 0, :], lg, AX.X, ALU.max), [t])
        t_rw = act(lambda e, v: e.activation(top[:, 1, :], top[:, 0, :], ACT.Sigmoid), [t])
        t = dve(lambda e, v: e.tensor_tensor(oh, lg, top[:, 0, :].unsqueeze(2).to_broadcast([P, QT, E]), ALU.is_equal), [t])
        t = dve(lambda e, v: e.tensor_tensor(oh, oh, rank.unsqueeze(1).to_broadcast([P, QT, E]), ALU.mult), [t])
        t = dve(lambda e, v: e.tensor_reduce(top[:, 2, :], oh, AX.X, ALU.max), [t])
        t_oh = dve(lambda e, v: e.tensor_tensor(oh, oh, top[:, 2, :].unsqueeze(2).to_broadcast([P, QT, E]), ALU.is_equal), [t])
        t2 = None
        gates, ups = [], []
        for q in range(QT):
            t1 = pe(lambda e, v, q=q: e.matmul(bank(1 + q % 2), xnT[:, q * P:(q + 1) * P], wgT, start=True, stop=True),
                    [ups[q - 2]] if q >= 2 else [])
            gates.append(act(lambda e, v, q=q: e.activation(eg[:, q, :], bank(1 + q % 2), ACT.Copy, scale=top[:, 1, q:q + 1]), [t1, t_rw]))
            t1 = pe(lambda e, v, q=q: e.matmul(bank(3 + q % 2), xnT[:, q * P:(q + 1) * P], wuT, start=True, stop=True),
                    [ups[q - 2]] if q >= 2 else [])
            ups.append(act(lambda e, v, q=q: e.activation(eu[:, q, :], bank(3 + q % 2), ACT.Copy, scale=top[:, 1, q:q + 1]), [t1]))
        t = act(lambda e, v: e.activation(es, eg, ACT.Sigmoid), [ups[-1]])
        t1 = dve(lambda e, v: e.tensor_tensor(eu, eu, eg, ALU.mult), [ups[-1]])
        t1 = dve(lambda e, v: e.tensor_tensor(eu, eu, es, ALU.mult), [t, t1])
        for q in range(QT):
            t = dve(lambda e, v, q=q: e.tensor_tensor(es[:, q, :].rearrange("p (e i) -> p e i", e=E), eu[:, q, :].rearrange("p (e i) -> p e i", e=E),
                                                      oh[:, q, :].unsqueeze(2).to_broadcast([P, E, I]), ALU.mult), [t1, t_oh])
        for c in range(FC):
            for q in range(QT):
                t1 = pe(lambda e, v, q=q, c=c: e.transpose(psum[:, 3 + c, q * P:(q + 1) * P], es[:, q, c * P:(c + 1) * P], ident[:, :]),
                        [t], count=q == QT - 1)
            t2 = act(lambda e, v, c=c: e.activation(ehT[:, c, :], bank(3 + c), ACT.Copy), [t1])
        for q in range(QT):
            for c in range(FC):
                t = pe(lambda e, v, q=q, c=c: e.matmul(psum[:, 0, q * P:(q + 1) * P], ehT[:, c, q * P:(q + 1) * P], wdT[:, c, :],
                                                       start=c == 0, stop=c == FC - 1), [t2, t_oh], count=c == FC - 1)
        dve(lambda e, v: e.tensor_tensor(xm(v), xm(v), bank(0).rearrange("p (q d) -> p q d", q=QT), ALU.add), [t])
        pr.end()
        pr.meet(phase=True)

        block = ctx.enter_context(nc.Block())

        @block.sync
        def _(eng):
            for s, dst, src, after in dma_list:
                if after:
                    eng.wait_ge(phase, after)
                eng.dma_start(dst, src).then_inc(s, 16)
            eng.wait_ge(phase, 4)
            eng.dma_start(out.rearrange("b (q p) d -> p (b q) d", p=P), x_res[:, :, :]).then_inc(s_out, 16)
            eng.wait_ge(s_out, 16)

        @block.tensor
        def _(eng):
            pr.emit("tensor", eng, (done, arrived, go, phase))

        @block.vector
        def _(eng):
            pr.emit("vector", eng, (done, arrived, go, phase))

        @block.scalar
        def _(eng):
            pr.emit("scalar", eng, (done, arrived, go, phase))

        @block.gpsimd
        def _(eng):
            pr.emit("gpsimd", eng, (done, arrived, go, phase))


def kernel(**inputs):
    import concourse.bacc as _bacc
    from concourse.bass_utils import run_bass_kernel_spmd as _run

    g = {k: np.asarray(v) for k, v in inputs.items()}
    c = np.ascontiguousarray

    def cols(*parts):
        return c(np.concatenate([p.reshape(P, -1) for p in parts], axis=1))

    def chunks(w):
        return w.reshape(-1, P, w.shape[-1]).transpose(1, 0, 2).reshape(P, -1)

    def words(m):
        wide = np.zeros(m.shape + (4,), m.dtype)
        wide[..., 0] = m
        return wide.view(np.int32)[..., 0].copy()

    L = "L1_xcond_"
    layer = [cols(g[L + "qkv_w"][l].T, g[L + "so_w"][l].T, g[L + "cq_w"][l].T, g[L + "ck_w"][l].T, g[L + "cv_w"][l].T,
                  g[L + "co_w"][l].T, g[L + "f1_w"][l].T, chunks(g[L + "f2_w"][l].T)) for l in range(NL)]
    norms_w = np.stack([g[L + f"n{n}_w"] for n in (1, 2, 3)], axis=1).reshape(NL * 6, D, D)
    norms_b = np.stack([g[L + f"n{n}_b"] for n in (1, 2, 3)], axis=1).reshape(NL * 6, D)
    wkv = g["L0_xcond_Wkv"]
    arrays = {
        "x": c(g["x"]),
        "ctx": c(g["ctx_1024"]),
        "ctxT": c(g["ctx_1024"].transpose(2, 0, 1)),
        "condT": c(g["cond_1024"].T),
        "ident": np.eye(P, dtype=np.float32),
        "rope": rope_tables(),
        "mask": words(g["mask_BxS_bf0"].reshape(B * QT, P).T),
        "maskc": words(g["mask_BxS2_bf0"].T),
        "vec": c(np.stack([g["L0_xcond_ln1_w"], g["L0_xcond_ln1_b"], g["L0_xcond_ln2_w"], g["L0_xcond_ln2_b"]], axis=1)),
        "n1w": c(g["L0_ffn_norm1_w"]),
        "n2w": c(g["L0_ffn_norm2_w"]),
        "actsb": c(np.concatenate([g["L0_ffn_act_scale"], g["L0_ffn_act_bias"]])),
        "nb": c(norms_b.T),
        "f1b": c(g[L + "f1_b"].reshape(NL * FC, P).T),
        "f2b": c(g[L + "f2_b"].reshape(1, NL * D)),
        "nT": cols(norms_w.transpose(2, 0, 1)),
        "w1T": c(g["L0_ffn_w1"].T),
        "w2T": c(chunks(g["L0_ffn_w2"].T)),
        "w0": cols(g["L0_xcond_Wq"].T, wkv[:INNER].T, wkv[INNER:].T, chunks(g["L0_xcond_Wo"].T)),
        "wl": cols(*layer),
        "wm": cols(g["L1_ffn_w_gate"].reshape(E * I, D).T, g["L1_ffn_w_up"].reshape(E * I, D).T,
                   chunks(g["L1_ffn_w_down"].transpose(0, 2, 1).reshape(E * I, D)), g["L1_ffn_gate_w"].T,
                   np.tile(np.arange(E, 0, -1, dtype=np.float32), (P, 1))),
    }
    nc = _bacc.Bacc("TRN2", target_bir_lowering=False, num_devices=1)
    aps, feed = {}, {}
    for name, v in arrays.items():
        aps[name] = nc.dram_tensor("in_" + name, v.shape, mybir.dt.from_np(v.dtype), kind="ExternalInput").ap()
        feed["in_" + name] = v
    out = nc.dram_tensor("out_0", (B, S, D), fp32, kind="ExternalOutput").ap()
    build(nc, aps, out)
    r = _run(nc, [feed], core_ids=[0])
    return r.results[0]["out_0"]
```
